# Optimizing a Trainium2 kernel written in Bass

```python
import numpy as np
import jax
import jax.numpy as jnp

def _softmax(x, axis=-1):
    return jax.nn.softmax(x, axis=axis)

def _gelu(x):
    return jax.nn.gelu(x, approximate=True)

def _silu(x):
    return jax.nn.silu(x)

def _sigmoid(x):
    return jax.nn.sigmoid(x)

def _layernorm(x, axis=-1, eps=1e-05):
    m = jnp.mean(x, axis=axis, keepdims=True)
    v = jnp.var(x, axis=axis, keepdims=True)
    return (x - m) / jnp.sqrt(v + eps)

def _scatter_add(tgt, idx, src, axis=0):
    return tgt.at[idx].add(src)

def _segment_sum(src, seg, n):
    return jax.ops.segment_sum(src, seg, n)
kernel_name = 'mk_xattn_ffn_d2_seqx_r8_8733a9'

def setup_inputs(seed: int=0):
    np.random.seed(seed)
    _w = jnp.asarray

    def _rec_inputs():
        import jax
        import jax.numpy as jnp
        _rk = jax.random.key(seed)
        x = -0.000125 + 0.9999 * jax.random.normal(jax.random.fold_in(_rk, 1), (8, 128, 128), jnp.float32)
        _lenS = 128 - jax.random.randint(jax.random.fold_in(_rk, 7), (8,), 0, max(1, 128 // 4) + 1, jnp.int32)
        _lenS2 = 128 - jax.random.randint(jax.random.fold_in(_rk, 8), (8,), 0, max(1, 128 // 4) + 1, jnp.int32)
        _ctx_1024P = jax.random.normal(jax.random.fold_in(_rk, 11), (8, 16, 128), jnp.float32)
        _ctx_1024c = jax.random.dirichlet(jax.random.fold_in(_rk, 511), 0.3 * jnp.ones((16,), jnp.float32), (8, 128))
        _ctx_1024t = jnp.einsum('bsk,bkd->bsd', _ctx_1024c, _ctx_1024P)
        _ctx_1024t = _ctx_1024t * jax.lax.rsqrt(jnp.mean(jnp.square(_ctx_1024t)) + 1e-12) * 0.953939
        ctx_1024 = -1.52775e-05 + 0.999936 * (_ctx_1024t + 0.3 * jax.random.normal(jax.random.fold_in(_rk, 611), (8, 128, 128), jnp.float32))
        return (x, ctx_1024)
    x, ctx_1024 = _rec_inputs()

    def _L0_xattn_setup():
        import jax, jax.numpy as jnp
        import numpy as np
        N_HEADS = 4
        IN_FEATURES = 128

        def _channel_attention(qm, km, vm, scale):
            b, n, c = qm.shape
            d = c // N_HEADS
            qh = qm.reshape(b, n, N_HEADS, d).transpose(0, 2, 3, 1)
            kh = km.reshape(b, n, N_HEADS, d).transpose(0, 2, 3, 1)
            vh = vm.reshape(b, n, N_HEADS, d).transpose(0, 2, 3, 1)
            scores = jnp.einsum('bhdn,bhen->bhde', qh, kh) * scale
            attn = jax.nn.softmax(scores, axis=-1)
            out = jnp.einsum('bhde,bhen->bhdn', attn, vh)
            return out.transpose(0, 3, 1, 2).reshape(b, n, c)
        key = jax.random.key(seed)
        ks = jax.random.split(key, 20)
        B, HW, C = (2, 2048, 128)
        inp = {'q': jax.random.normal(ks[0], (B, HW, C), dtype=jnp.float32), 'k': jax.random.normal(ks[1], (B, HW, C), dtype=jnp.float32), 'v': jax.random.normal(ks[2], (B, HW, C), dtype=jnp.float32)}
        names = ['wqg', 'bqg', 'wkg', 'bkg', 'wvg', 'bvg', 'wql', 'bql', 'wkl', 'bkl', 'wvl', 'bvl', 'wp', 'bp']
        for i, n in enumerate(names):
            inp[n] = jax.random.normal(ks[3 + i], (C,), dtype=jnp.float32)
        return inp
    _L0_xattn_all = _L0_xattn_setup()
    _L0_xattn_in = {k: v for k, v in _L0_xattn_all.items() if k in ('wqg', 'bqg', 'wkg', 'bkg', 'wvg', 'bvg', 'wql', 'bql', 'wkl', 'bkl', 'wvl', 'bvl', 'wp', 'bp')}
    del _L0_xattn_all

    def _L0_ffn_setup():
        import jax, jax.numpy as jnp
        import numpy as np
        HIDDEN = 128
        HEAD_DIM = 64
        N_EXPERTS = 16
        MIN_EXPERTS = 2
        B, T = (4, 256)

        def _normalize(x, axis):
            n = jnp.sqrt(jnp.sum(x * x, axis=axis, keepdims=True))
            return x / jnp.maximum(n, 1e-12)

        def _ste(x):
            hard = jax.lax.stop_gradient((x > 0).astype(x.dtype))
            return hard + x - jax.lax.stop_gradient(x)

        def _gating(hidden_states, sim_matrix, gates):
            b, t, c = hidden_states.shape
            flat = hidden_states.reshape(b * t, c)
            logits = _normalize(flat, -1) @ _normalize(sim_matrix, 0) - jax.nn.sigmoid(gates)
            gated = jax.nn.relu(logits)
            mask = _ste(gated)
            inactive = jnp.sum(mask, axis=1) == 0
            _, fb_idx = jax.lax.top_k(logits, MIN_EXPERTS)
            fb = jnp.zeros_like(mask).at[jnp.arange(b * t)[:, None], fb_idx].set(1.0)
            fb_applied = inactive[:, None] & (fb > 0)
            mask = jnp.where(fb_applied, 1.0, mask)
            masked_logits = jnp.where(mask > 0, gated, -jnp.inf)
            return jax.nn.softmax(masked_logits, axis=-1).reshape(b, t, -1)
        key = jax.random.key(seed)
        ks = jax.random.split(key, 6)
        xav_qkv = float(np.sqrt(6.0 / (HIDDEN + HEAD_DIM)))
        return {'hidden_states': jax.random.normal(ks[0], (B, T, HIDDEN), dtype=jnp.float32), 'sim_matrix': jax.random.normal(ks[1], (HIDDEN, N_EXPERTS), dtype=jnp.float32), 'gates': jnp.zeros((N_EXPERTS,), dtype=jnp.float32), 'q_proj': jax.random.uniform(ks[2], (N_EXPERTS, HIDDEN, HEAD_DIM), jnp.float32, -xav_qkv, xav_qkv), 'k_proj': jax.random.uniform(ks[3], (N_EXPERTS, HIDDEN, HEAD_DIM), jnp.float32, -xav_qkv, xav_qkv), 'v_proj': jax.random.uniform(ks[4], (N_EXPERTS, HIDDEN, HEAD_DIM), jnp.float32, -xav_qkv, xav_qkv), 'o_proj': jax.random.uniform(ks[5], (N_EXPERTS, HEAD_DIM, HIDDEN), jnp.float32, -xav_qkv, xav_qkv)}
    _L0_ffn_all = _L0_ffn_setup()
    _L0_ffn_in = {k: v for k, v in _L0_ffn_all.items() if k in ('sim_matrix', 'gates', 'q_proj', 'k_proj', 'v_proj', 'o_proj')}
    del _L0_ffn_all

    def _L1_xattn_setup():
        import jax, jax.numpy as jnp
        import numpy as np
        D_MODEL = 128
        N_HEAD = 16
        HEAD_DIM = D_MODEL // N_HEAD
        key = jax.random.key(seed)
        ks = jax.random.split(key, 9)
        B, T = (2, 256)
        s = 0.02
        return {'k': jax.random.normal(ks[0], (B, T, D_MODEL), jnp.float32), 'q': jax.random.normal(ks[1], (B, T, D_MODEL), jnp.float32), 'v': jax.random.normal(ks[2], (B, T, D_MODEL), jnp.float32), 'Wk': jax.random.normal(ks[3], (D_MODEL, D_MODEL), jnp.float32) * s, 'bk': jnp.zeros((D_MODEL,), jnp.float32), 'Wq': jax.random.normal(ks[4], (D_MODEL, D_MODEL), jnp.float32) * s, 'bq': jnp.zeros((D_MODEL,), jnp.float32), 'Wc': jax.random.normal(ks[5], (D_MODEL, D_MODEL), jnp.float32) * s, 'bc': jnp.zeros((D_MODEL,), jnp.float32)}
    _L1_xattn_all = _L1_xattn_setup()
    _L1_xattn_in = {k: v for k, v in _L1_xattn_all.items() if k in ('Wk', 'bk', 'Wq', 'bq', 'Wc', 'bc')}
    del _L1_xattn_all

    def _L1_ffn_setup():
        import jax, jax.numpy as jnp
        import numpy as np
        B, T, C = (4, 256, 128)
        E = 8
        K = 2
        H = 176
        HS = 176 * 2
        key = jax.random.key(seed)
        k = jax.random.split(key, 8)
        s = 0.02
        return {'x': jax.random.normal(k[0], (B, T, C), jnp.float32), 'Wg': jax.random.normal(k[1], (C, E), jnp.float32) * s, 'W1': jax.random.normal(k[2], (E, C, H), jnp.float32) * s, 'W2': jax.random.normal(k[3], (E, C, H), jnp.float32) * s, 'W3': jax.random.normal(k[4], (E, H, C), jnp.float32) * s, 'Ws1': jax.random.normal(k[5], (C, HS), jnp.float32) * s, 'Ws2': jax.random.normal(k[6], (C, HS), jnp.float32) * s, 'Ws3': jax.random.normal(k[7], (HS, C), jnp.float32) * s}
    _L1_ffn_all = _L1_ffn_setup()
    _L1_ffn_in = {k: v for k, v in _L1_ffn_all.items() if k in ('Wg', 'W1', 'W2', 'W3', 'Ws1', 'Ws2', 'Ws3')}
    del _L1_ffn_all
    return {'x': x, 'ctx_1024': ctx_1024, 'L0_xattn_wqg': _L0_xattn_in['wqg'], 'L0_xattn_bqg': _L0_xattn_in['bqg'], 'L0_xattn_wkg': _L0_xattn_in['wkg'], 'L0_xattn_bkg': _L0_xattn_in['bkg'], 'L0_xattn_wvg': _L0_xattn_in['wvg'], 'L0_xattn_bvg': _L0_xattn_in['bvg'], 'L0_xattn_wql': _L0_xattn_in['wql'], 'L0_xattn_bql': _L0_xattn_in['bql'], 'L0_xattn_wkl': _L0_xattn_in['wkl'], 'L0_xattn_bkl': _L0_xattn_in['bkl'], 'L0_xattn_wvl': _L0_xattn_in['wvl'], 'L0_xattn_bvl': _L0_xattn_in['bvl'], 'L0_xattn_wp': _L0_xattn_in['wp'], 'L0_xattn_bp': _L0_xattn_in['bp'], 'L0_ffn_sim_matrix': _L0_ffn_in['sim_matrix'], 'L0_ffn_gates': _L0_ffn_in['gates'], 'L0_ffn_q_proj': _L0_ffn_in['q_proj'], 'L0_ffn_k_proj': _L0_ffn_in['k_proj'], 'L0_ffn_v_proj': _L0_ffn_in['v_proj'], 'L0_ffn_o_proj': _L0_ffn_in['o_proj'], 'L1_xattn_Wk': _L1_xattn_in['Wk'], 'L1_xattn_bk': _L1_xattn_in['bk'], 'L1_xattn_Wq': _L1_xattn_in['Wq'], 'L1_xattn_bq': _L1_xattn_in['bq'], 'L1_xattn_Wc': _L1_xattn_in['Wc'], 'L1_xattn_bc': _L1_xattn_in['bc'], 'L1_ffn_Wg': _L1_ffn_in['Wg'], 'L1_ffn_W1': _L1_ffn_in['W1'], 'L1_ffn_W2': _L1_ffn_in['W2'], 'L1_ffn_W3': _L1_ffn_in['W3'], 'L1_ffn_Ws1': _L1_ffn_in['Ws1'], 'L1_ffn_Ws2': _L1_ffn_in['Ws2'], 'L1_ffn_Ws3': _L1_ffn_in['Ws3']}

def reference(x, ctx_1024, L0_xattn_wqg, L0_xattn_bqg, L0_xattn_wkg, L0_xattn_bkg, L0_xattn_wvg, L0_xattn_bvg, L0_xattn_wql, L0_xattn_bql, L0_xattn_wkl, L0_xattn_bkl, L0_xattn_wvl, L0_xattn_bvl, L0_xattn_wp, L0_xattn_bp, L0_ffn_sim_matrix, L0_ffn_gates, L0_ffn_q_proj, L0_ffn_k_proj, L0_ffn_v_proj, L0_ffn_o_proj, L1_xattn_Wk, L1_xattn_bk, L1_xattn_Wq, L1_xattn_bq, L1_xattn_Wc, L1_xattn_bc, L1_ffn_Wg, L1_ffn_W1, L1_ffn_W2, L1_ffn_W3, L1_ffn_Ws1, L1_ffn_Ws2, L1_ffn_Ws3):
    import jax
    import jax.numpy as jnp

    def _L0_xattn_ref(q, k, v, wqg, bqg, wkg, bkg, wvg, bvg, wql, bql, wkl, bkl, wvl, bvl, wp, bp):
        import jax, jax.numpy as jnp
        import numpy as np
        N_HEADS = 4
        IN_FEATURES = 128

        def _channel_attention(qm, km, vm, scale):
            b, n, c = qm.shape
            d = c // N_HEADS
            qh = qm.reshape(b, n, N_HEADS, d).transpose(0, 2, 3, 1)
            kh = km.reshape(b, n, N_HEADS, d).transpose(0, 2, 3, 1)
            vh = vm.reshape(b, n, N_HEADS, d).transpose(0, 2, 3, 1)
            scores = jnp.einsum('bhdn,bhen->bhde', qh, kh) * scale
            attn = jax.nn.softmax(scores, axis=-1)
            out = jnp.einsum('bhde,bhen->bhdn', attn, vh)
            return out.transpose(0, 3, 1, 2).reshape(b, n, c)
        scale = IN_FEATURES ** (-0.5)
        att_global = _channel_attention(q * wqg + bqg, k * wkg + bkg, v * wvg + bvg, scale)
        att_local = _channel_attention(q * wql + bql, k * wkl + bkl, v * wvl + bvl, scale)
        att = att_global + att_local
        return 2.0 * att * wp + bp

    def _L0_ffn_ref(hidden_states, sim_matrix, gates, q_proj, k_proj, v_proj, o_proj):
        import jax, jax.numpy as jnp
        import numpy as np
        HIDDEN = 128
        HEAD_DIM = 64
        N_EXPERTS = 16
        MIN_EXPERTS = 2
        B, T = (4, 256)

        def _normalize(x, axis):
            n = jnp.sqrt(jnp.sum(x * x, axis=axis, keepdims=True))
            return x / jnp.maximum(n, 1e-12)

        def _ste(x):
            hard = jax.lax.stop_gradient((x > 0).astype(x.dtype))
            return hard + x - jax.lax.stop_gradient(x)

        def _gating(hidden_states, sim_matrix, gates):
            b, t, c = hidden_states.shape
            flat = hidden_states.reshape(b * t, c)
            logits = _normalize(flat, -1) @ _normalize(sim_matrix, 0) - jax.nn.sigmoid(gates)
            gated = jax.nn.relu(logits)
            mask = _ste(gated)
            inactive = jnp.sum(mask, axis=1) == 0
            _, fb_idx = jax.lax.top_k(logits, MIN_EXPERTS)
            fb = jnp.zeros_like(mask).at[jnp.arange(b * t)[:, None], fb_idx].set(1.0)
            fb_applied = inactive[:, None] & (fb > 0)
            mask = jnp.where(fb_applied, 1.0, mask)
            masked_logits = jnp.where(mask > 0, gated, -jnp.inf)
            return jax.nn.softmax(masked_logits, axis=-1).reshape(b, t, -1)
        b, t, c = hidden_states.shape
        rw = _gating(hidden_states, sim_matrix, gates)
        q = jnp.einsum('bte,bted->btd', rw, jnp.einsum('btc,ecd->bted', hidden_states, q_proj))
        k = jnp.einsum('bte,bted->btd', rw, jnp.einsum('btc,ecd->bted', hidden_states, k_proj))
        v = jnp.einsum('bte,bted->btd', rw, jnp.einsum('btc,ecd->bted', hidden_states, v_proj))
        scale = 1.0 / jnp.sqrt(jnp.asarray(HEAD_DIM, dtype=q.dtype))
        scores = jnp.einsum('bqd,bkd->bqk', q, k) * scale
        causal = jnp.tril(jnp.ones((t, t), dtype=bool))
        scores = jnp.where(causal, scores, -jnp.inf)
        attn = jnp.einsum('bqk,bkd->bqd', jax.nn.softmax(scores, axis=-1), v)
        mixed = attn[:, :, None, :] * rw[..., None]
        return jnp.einsum('bted,edc->btc', mixed, o_proj)

    def _L1_xattn_ref(k, q, v, Wk, bk, Wq, bq, Wc, bc):
        import jax, jax.numpy as jnp
        import numpy as np
        D_MODEL = 128
        N_HEAD = 16
        HEAD_DIM = D_MODEL // N_HEAD
        B, T_v, C = v.shape
        T_q = q.shape[1]
        H, hd = (N_HEAD, C // N_HEAD)
        kp = k @ Wk.T + bk
        qp = q @ Wq.T + bq
        kh = kp.reshape(B, T_v, H, hd).transpose(0, 2, 1, 3)
        qh = qp.reshape(B, T_q, H, hd).transpose(0, 2, 1, 3)
        vh = v.reshape(B, T_v, H, hd).transpose(0, 2, 1, 3)
        scale = 1.0 / jnp.sqrt(jnp.asarray(hd, kh.dtype))
        att = jnp.einsum('bhqd,bhkd->bhqk', qh, kh) * scale
        att = jax.nn.softmax(att, axis=-1)
        y = jnp.einsum('bhqk,bhkd->bhqd', att, vh)
        y = y.transpose(0, 2, 1, 3).reshape(B, T_q, C)
        return y @ Wc.T + bc

    def _L1_ffn_ref(x, Wg, W1, W2, W3, Ws1, Ws2, Ws3):
        import jax, jax.numpy as jnp
        import numpy as np
        B, T, C = (4, 256, 128)
        E = 8
        K = 2
        H = 176
        HS = 176 * 2
        b, t, c = x.shape
        xf = x.reshape(-1, c)
        n = xf.shape[0]
        router = xf @ Wg
        top_logits, idx = jax.lax.top_k(router, K)
        probs = jax.nn.softmax(top_logits.astype(jnp.float32), axis=-1).astype(x.dtype)
        w = jnp.zeros((n, E), x.dtype).at[jnp.arange(n)[:, None], idx].add(probs)
        h = jax.nn.silu(jnp.einsum('tc,ech->eth', xf, W1)) * jnp.einsum('tc,ech->eth', xf, W2)
        y = jnp.einsum('eth,ehc,te->tc', h, W3, w)
        y = y.reshape(b, t, c)
        hs = jax.nn.silu(xf @ Ws1) * (xf @ Ws2)
        y = y + (hs @ Ws3).reshape(b, t, c)
        return y
    x = x + _L0_xattn_ref(_layernorm(x, axis=-1), ctx_1024, ctx_1024, L0_xattn_wqg, L0_xattn_bqg, L0_xattn_wkg, L0_xattn_bkg, L0_xattn_wvg, L0_xattn_bvg, L0_xattn_wql, L0_xattn_bql, L0_xattn_wkl, L0_xattn_bkl, L0_xattn_wvl, L0_xattn_bvl, L0_xattn_wp, L0_xattn_bp)
    x = x + _L0_ffn_ref(_layernorm(x, axis=-1), L0_ffn_sim_matrix, L0_ffn_gates, L0_ffn_q_proj, L0_ffn_k_proj, L0_ffn_v_proj, L0_ffn_o_proj)
    x = x + _L1_xattn_ref(ctx_1024, _layernorm(x, axis=-1), ctx_1024, L1_xattn_Wk, L1_xattn_bk, L1_xattn_Wq, L1_xattn_bq, L1_xattn_Wc, L1_xattn_bc)
    x = x + _L1_ffn_ref(_layernorm(x, axis=-1), L1_ffn_Wg, L1_ffn_W1, L1_ffn_W2, L1_ffn_W3, L1_ffn_Ws1, L1_ffn_Ws2, L1_ffn_Ws3)
    return x

_drawn_inputs = setup_inputs


def setup_inputs(seed=0):
    import zlib

    import numpy as np

    out = dict(_drawn_inputs(seed))
    spreads = {'L0_ffn_gates': (0.0, 0.1),
     'L1_xattn_bk': (0.0, 0.8),
     'L1_xattn_bq': (0.0, 0.8),
     'L1_xattn_bc': (0.0, 0.384)}
    factors = {'L0_ffn_q_proj': 4.364,
     'L0_ffn_k_proj': 3.498,
     'L1_xattn_Wk': 8.0,
     'L1_xattn_Wq': 8.0,
     'L1_ffn_Wg': 8.0,
     'L1_ffn_W1': 8.0,
     'L1_ffn_W2': 8.0,
     'L1_ffn_W3': 8.0,
     'L1_ffn_Ws1': 8.0,
     'L1_ffn_Ws2': 8.0,
     'L1_ffn_Ws3': 8.0}
    for name, (base, spread) in spreads.items():
        noise = np.random.default_rng([zlib.crc32(name.encode()), seed]).standard_normal(out[name].shape)
        drawn = base * np.exp(spread * noise) if base else spread * noise
        out[name] = jnp.asarray(drawn.astype(out[name].dtype))
    for name, factor in factors.items():
        out[name] = (out[name] * factor).astype(out[name].dtype)
    return out
```

```python
from contextlib import ExitStack

import concourse.bass as bass
from concourse import mybir

F32 = mybir.dt.float32
F32R = mybir.dt.float32r
BF16 = mybir.dt.bfloat16
I32 = mybir.dt.int32
ALU = mybir.AluOpType
ACT = mybir.ActivationFunctionType
AX = mybir.AxisListType

NB = 8
T = 128
C = 128
H0, D0 = 4, 32
E0, HD = 16, 64
H1, D1 = 16, 8
E1, HID = 8, 176
HS = 2 * HID
HALF = NB // 2
EPS = 1e-5
NEG = -1e30
RUP = E1 * HID + HS
NCH = -(-RUP // 128)
NROUTED = E1 * HID // 128
S0_SCALE = C ** -0.5
A_SCALE = HD ** -0.5
S1_SCALE = D1 ** -0.5

Q3 = 4 * NB
F4 = Q3 + 4 * NB + 4
LAST = F4 + 2 * NCH + 3

WQG, BQG, WQL, BQL, WVG, BVG, WVL, BVL, WP = range(9)
R_BP, R_BC, R_BK, R_BQ = range(4)


def bc(ap, axis, n):
    a = ap.unsqueeze(axis)
    shape = list(a.shape)
    shape[axis] = n
    return a.to_broadcast(shape)


def diag(tile, start):
    a = tile.rearrange("p h c -> p (h c)")
    return bass.AP(a.tensor, a.offset + start, [list(a.ap[0]), [128 + D1, 8], [1, D1]])


def build(nc, x_d, ctx_d, ctxT_d, cols_d, rows_d, kv_d, sim_d, wattn_d, wqkv_d, wo_d, wa_d, wb_d, wdn_d, wg_d, out_d):
    with ExitStack() as ctx:
        def sb(name, shape, dt=F32):
            return ctx.enter_context(nc.sbuf_tensor(name, shape, dt))

        def sem(name):
            return ctx.enter_context(nc.semaphore(name))

        xr = sb("xr", [T, NB, C])
        cx = sb("cx", [T, NB, C])
        cxT = sb("cxT", [C, NB * T])
        cols = sb("cols", [C, 9])
        rows = sb("rows", [128, 4, C])
        gates = sb("gates", [128, E0])
        kv = sb("kv", [C, 4, D0])
        sim = sb("sim", [C, E0])
        wattn = sb("wattn", [C, 3, C])
        wqkv = sb("wqkv", [C, E0, 3 * HD])
        wo = sb("wo", [2 * HD, E0 // 2, C])
        wa = sb("wa", [C, RUP])
        wb = sb("wb", [C, RUP])
        wdn = sb("wdn", [128, NCH, C])
        wg = sb("wg", [C, E1])

        ident = sb("ident", [128, 128])
        identb = sb("identb", [128, 128], BF16)
        ones = sb("ones", [128, 128])
        causal = sb("causal", [T, T])
        orderi = sb("orderi", [128, E0], I32)
        order = sb("order", [128, E0])
        wp2 = sb("wp2", [C, 1])
        part16 = sb("part16", [128, E0])
        part8 = sb("part8", [128, E1])
        hmask = sb("hmask", [128, 4])
        sel = sb("sel", [128, E0, 128], BF16)
        sel2 = sb("sel2", [128, E0 // 2, 2, HD], BF16)
        selw = sb("selw", [128, E1, HID], BF16)

        st = sb("st", [128, 4, NB, 6])
        mv = sb("mv", [128, 4, NB, 2])
        ve = sb("ve", [128, 4, NB])
        rstd = sb("rstd", [128, 4, NB])
        hn = sb("hn", [128, NB])
        rhn = sb("rhn", [128, NB])
        xna = sb("xna", [T, NB, C])
        xnb = sb("xnb", [T, NB, C])
        xn2T = sb("xn2T", [C, NB, T])
        xn4T = xn2T[:, :, :].rearrange("p b t -> p (b t)")

        kw = sb("kw", [C, 2, NB, D0])
        kb = sb("kb", [C, 2, D0])
        sc = sb("sc", [C, 2, HALF, D0])
        sc2 = sb("sc2", [C, 2, HALF, D0])
        cm = sb("cm", [C, 2 * HALF])
        cs = sb("cs", [C, 2 * HALF])

        sim2 = sb("sim2", [C, E0])
        simn = sb("simn", [C, E0])
        sgate = sb("sgate", [128, E0])
        lg = sb("lg", [T, HALF, E0])
        ga = sb("ga", [T, HALF, E0])
        f1 = sb("f1", [T, HALF, E0])
        f2 = sb("f2", [T, HALF, E0])
        gv = sb("gv", [T, 6, HALF])
        gin = sb("gin", [T, HALF, E0])
        gex = sb("gex", [T, HALF, E0])
        rw = sb("rw", [T, HALF, E0])
        parts = sb("parts", [T, NB, 128], BF16)
        rwT = sb("rwT", [128, NB, T], BF16)
        wparts = sb("wparts", [T, NB, 128], BF16)
        wT = sb("wT", [128, NB * T], BF16)

        hm = sb("hm", [C, 2, E0, T])
        qk = sb("qk", [T, 2, 2 * HD])
        v2 = sb("v2", [T, 2, 2, HD])
        qkT = sb("qkT", [HD, 2, 2, T])
        s2 = sb("s2", [T, 2, T])
        mx2 = sb("mx2", [T, NB])
        nmx2 = sb("nmx2", [T, NB])
        den2 = sb("den2", [T, NB])
        rden2 = sb("rden2", [T, NB])
        pn = sb("pn", [T, 2, T])
        pT2 = sb("pT2", [T, 2, T])
        aT = sb("aT", [2 * HD, 2, T])
        m16 = sb("m16", [128, E0])
        mixT = sb("mixT", [2 * HD, E0 // 2, T])

        kf = sb("kf", [T, C])
        qf = sb("qf", [T, C])
        ksp = sb("ksp", [T, 4, 4, 32])
        qsp = sb("qsp", [T, 4, 4, 32])
        ks = sb("ks", [128, NB, 4, T], F32R)
        qs = sb("qs", [128, NB, 4, T], F32R)
        xn3T = sb("xn3T", [C, T])
        km = sb("km", [128, 2, 4, 4, T], F32R)
        vm = sb("vm", [T, 2, H1, 128])
        ex = sb("ex", [T, 4, 4 * T])
        exT = sb("exT", [T, 4, 4 * T])
        mx3 = sb("mx3", [T, 8, 4])
        ry = sb("ry", [64, 2, T])
        yT = sb("yT", [C, 2, T])
        vT = exT[:, :, :].rearrange("p a n -> p (a n)").rearrange("p (v n) -> p v n", v=2)
        bd = ex[:, :, :].rearrange("p a n -> p (a n)").rearrange("p (f v b n) -> p f v b n", f=2, v=2, b=HALF)
        ff = hm[:, :, :, :].rearrange("p a e t -> p (a e t)").rearrange("p (k n) -> p k n", n=4 * T)
        gated, prod, hid = ff[:, 0:2, :], ff[:, 2:4, :], ff[:, 4:7, :]

        PB = [ctx.enter_context(nc.psum_tensor(f"bank{i}", [128, 512], F32)) for i in range(8)]

        ld_x = [sem(f"ld_x{i}") for i in range(2)]
        ld_ctx = [sem(f"ld_ctx{i}") for i in range(2)]
        ld_vec = sem("ld_vec")
        ld_ctxT = sem("ld_ctxT")
        ld_attn = sem("ld_attn")
        ld_qkv = sem("ld_qkv")
        ld_o = sem("ld_o")
        ld_up = sem("ld_up")
        ld_dn = sem("ld_dn")
        c_id = sem("c_id"); c_ones = sem("c_ones"); c_pool = sem("c_pool"); pool_step = sem("pool_step")
        c_part = sem("c_part"); c_sel = sem("c_sel")
        zeroed = sem("zeroed")
        dve_step = sem("dve_step")
        ve_ready = sem("ve_ready"); rstd_ready = sem("rstd_ready")
        hn_ready = sem("hn_ready"); rhn_ready = sem("rhn_ready")
        xbp_ready = sem("xbp_ready")
        k1_used = sem("k1_used"); s_used = sem("s_used"); x1_ready = sem("x1_ready"); lg_used = sem("lg_used")
        x2_ready = sem("x2_ready"); kp_used = sem("kp_used"); x3_ready = sem("x3_ready"); xbc_ready = sem("xbc_ready")
        nmx_ready = sem("nmx_ready"); mixw_ready = sem("mixw_ready");
        k1_ready = sem("k1_ready"); sim2_ready = sem("sim2_ready"); simsum_ready = sem("simsum_ready")
        ssq_ready = sem("ssq_ready"); simr_ready = sem("simr_ready"); simn_ready = sem("simn_ready")
        egate_ready = sem("egate_ready"); vT_ready = sem("vT_ready")
        xn1_ready = sem("xn1_ready"); s_ready = sem("s_ready"); sc_ready = sem("sc_ready"); sce_ready = sem("sce_ready")
        bd_ready = sem("bd_ready"); att_ready = sem("att_ready")
        xn2_ready = sem("xn2_ready"); xn2T_ps = sem("xn2T_ps"); xn2T_ready = sem("xn2T_ready")
        lg_ps = sem("lg_ps"); gin_ready = sem("gin_ready"); gex_ready = sem("gex_ready")
        parts_ready = sem("parts_ready"); rwT_ps = sem("rwT_ps"); rwT_ready = sem("rwT_ready")
        rb_ready = sem("rb_ready"); hm_ready = sem("hm_ready"); qkv_done = sem("qkv_done")
        qk_ready = sem("qk_ready"); qkT_ps = sem("qkT_ps"); qkT_ready = sem("qkT_ready")
        s2_ps = sem("s2_ps"); s2_ready = sem("s2_ready"); p2_ready = sem("p2_ready"); pn_ready = sem("pn_ready")
        pT2_ps = sem("pT2_ps"); pT2_ready = sem("pT2_ready"); aT_ps = sem("aT_ps"); aT_ready = sem("aT_ready")
        mix_ready = sem("mix_ready"); o_ready = sem("o_ready")
        kp_ready = sem("kp_ready"); ksp_ready = sem("ksp_ready"); ksT_ps = sem("ksT_ps"); ks_ready = sem("ks_ready")
        xn3_ready = sem("xn3_ready"); xn3T_ps = sem("xn3T_ps"); xn3T_ready = sem("xn3T_ready")
        qp_ready = sem("qp_ready"); qsp_ready = sem("qsp_ready"); qsT_ps = sem("qsT_ps"); qs_ready = sem("qs_ready")
        km_ready = sem("km_ready"); vm_ready = sem("vm_ready")
        s3_ready = sem("s3_ready"); ex_in = sem("ex_in"); ex_ready = sem("ex_ready")
        exT_ps = sem("exT_ps"); exT_ready = sem("exT_ready"); pv_done = sem("pv_done")
        yT_ready = sem("yT_ready"); c_ready = sem("c_ready")
        xn4_ready = sem("xn4_ready"); xn4T_ps = sem("xn4T_ps"); xn4T_ready = sem("xn4T_ready")
        rt_ps = sem("rt_ps"); rin_ready = sem("rin_ready"); rex_ready = sem("rex_ready")
        wparts_ready = sem("wparts_ready"); wT_ps = sem("wT_ps"); wT_ready = sem("wT_ready")
        up_ready = sem("up_ready"); gated_ready = sem("gated_ready"); prod_ready = sem("prod_ready")
        hid_ready = sem("hid_ready"); down_done = sem("down_done");
        out_ready = sem("out_ready"); stored = sem("stored")

        def bs(hf):
            return slice(HALF * hf, HALF * hf + HALF)

        def head_rows(h):
            return slice(D0 * h, D0 * h + D0)

        def chunk_rows(ch):
            return min(128, RUP - 128 * ch)

        def n_routed(k):
            return NROUTED * (k // NCH) + min(k % NCH + 1, NROUTED)

        def routed_chunk(r):
            return (r - 1) // NROUTED * NCH + (r - 1) % NROUTED

        def b_read(eng, k):
            if k % NCH < NROUTED:
                eng.wait_ge(prod_ready, n_routed(k))
            else:
                eng.wait_ge(hid_ready, k + 1)

        block = ctx.enter_context(nc.Block())

        @block.sync
        def _(sp):
            sp.dma_start(xr[:, bs(0), :], x_d[:, bs(0), :]).then_inc(ld_x[0], 16)
            sp.dma_start(cx[:, bs(0), :], ctx_d[:, bs(0), :]).then_inc(ld_ctx[0], 16)
            sp.dma_start(xr[:, bs(1), :], x_d[:, bs(1), :]).then_inc(ld_x[1], 16)
            sp.dma_start(cx[:, bs(1), :], ctx_d[:, bs(1), :]).then_inc(ld_ctx[1], 16)
            sp.dma_start(cxT[:, :], ctxT_d).then_inc(ld_ctxT, 16)
            sp.dma_start(wqkv[:, :, :], wqkv_d).then_inc(ld_qkv, 16)
            sp.dma_start(wattn[:, :, :], wattn_d).then_inc(ld_attn, 16)
            sp.dma_start(wo[:, :, :], wo_d).then_inc(ld_o, 16)
            sp.dma_start(wa[:, :], wa_d).then_inc(ld_up, 16)
            sp.dma_start(wb[:, :], wb_d).then_inc(ld_up, 16)
            sp.dma_start(wg[:, :], wg_d).then_inc(ld_up, 16)
            full = RUP // 128
            sp.dma_start(wdn[:, 0:full, :], wdn_d[0:full * 128, :].rearrange("(k p) c -> p k c", p=128)).then_inc(ld_dn, 16)
            sp.dma_start(wdn[0:RUP - full * 128, full, :], wdn_d[full * 128:RUP, :]).then_inc(ld_dn, 16)
            for hf in range(2):
                sp.wait_ge(out_ready, hf + 1)
                sp.dma_start(out_d[:, bs(hf), :], xr[:, bs(hf), :]).then_inc(stored, 16)
            sp.wait_ge(stored, 32)

        @block.gpsimd
        def _(pool):
            steps = [0]

            def link(ins):
                steps[0] += 1
                ins.then_inc(pool_step, 1)
                pool.wait_ge(pool_step, steps[0])

            link(nc.gpsimd.memset(ident[:, :], 0.0))
            nc.gpsimd.affine_select(out=ident[:, :], in_=ident[:, :], compare_op=ALU.not_equal, fill=1.0, base=0,
                                    pattern=[[-1, 128]], channel_multiplier=1).then_inc(c_id, 1)
            nc.gpsimd.memset(m16[:, :], -0.5).then_inc(c_pool, 1)
            nc.gpsimd.iota(orderi[:, :], [[-1, E0]], base=E0, channel_multiplier=0).then_inc(c_pool, 1)

            def power(dst, src, signal):
                nc.gpsimd.tensor_tensor(dst, src, m16[:, 0:src.shape[1]], ALU.pow).then_inc(signal, 1)

            def rstd_of(n, k, b0, b1):
                pool.wait_ge(ve_ready, n)
                power(rstd[:, k, b0:b1], ve[:, k, b0:b1], rstd_ready)

            pool.wait_ge(c_pool, 2)
            rstd_of(1, 0, 0, HALF)
            rstd_of(2, 0, HALF, NB)
            nc.gpsimd.memset(ex[:, :, :], 0.0).then_inc(zeroed, 1)
            pool.wait_ge(ssq_ready, 1)
            power(sim2[:, :], sim2[:, :], simr_ready)
            pool.wait_ge(ld_vec, 16 * 8)
            for hf in range(2):
                pool.wait_ge(xn1_ready, hf + 1)
                nc.gpsimd.tensor_tensor(xr[:, bs(hf), :], xr[:, bs(hf), :], bc(rows[:, R_BP, :], 1, HALF), ALU.add).then_inc(xbp_ready, 1)
            nc.gpsimd.memset(parts[:, :, :], 0.0).then_inc(zeroed, 1)
            for hf in range(2):
                rstd_of(3 + hf, 1, HALF * hf, HALF * hf + HALF)
                pool.wait_ge(hn_ready, hf + 1)
                power(rhn[:, bs(hf)], hn[:, bs(hf)], rhn_ready)
            link(nc.gpsimd.memset(causal[:, :], 0.0))
            nc.gpsimd.affine_select(out=causal[:, :], in_=causal[:, :], compare_op=ALU.is_ge, fill=NEG, base=0,
                                    pattern=[[-1, T]], channel_multiplier=1).then_inc(c_pool, 1)
            nc.gpsimd.memset(wparts[:, :, :], 0.0).then_inc(zeroed, 1)
            link(nc.gpsimd.memset(vm[:, :, :, :], 0.0))
            for p in range(2):
                for g in range(2):
                    ins = nc.gpsimd.memset(diag(vm[:, p, 8 * g:8 * g + 8, :], 64), 1.0)
            link(ins)

            def fill_vm(b):
                if b >= 2:
                    pool.wait_ge(pv_done, 4 * (b - 1))
                for g in range(2):
                    ins = nc.gpsimd.tensor_copy(diag(vm[:, b % 2, 8 * g:8 * g + 8, :], 0),
                                                cx[:, b, 64 * g:64 * g + 64].rearrange("p (h i) -> p h i", i=D1))
                ins.then_inc(vm_ready, 1)

            def mask_k(b):
                pool.wait_ge(ks_ready, b + 1)
                if b >= 2:
                    pool.wait_ge(s3_ready, 4 * (b - 1))
                for g in range(4):
                    ins = nc.gpsimd.tensor_tensor(km[:, b % 2, g, :, :], bc(ks[:, b, g, :].bitcast(F32), 1, 4),
                                                  bc(hmask[:, :], 2, T), ALU.mult)
                ins.then_inc(km_ready, 1)

            def add_bc(b):
                pool.wait_ge(xn3_ready, b + 1)
                nc.gpsimd.tensor_tensor(xr[:, b, :], xr[:, b, :], rows[:, R_BC, :], ALU.add).then_inc(xbc_ready, 1)

            pool.wait_ge(ld_ctx[0], 16)
            pool.wait_ge(ld_ctx[1], 16)
            pool.wait_ge(c_part, 1)
            for b in range(NB):
                rstd_of(5 + b, 2, b, b + 1)
                add_bc(b)
                if b in (2, 4):
                    fill_vm(b // 2 - 1)
                    mask_k(b // 2 - 1)
            mask_k(2)
            for b in range(NB):
                if b + 3 < NB:
                    mask_k(b + 3)
                if b + 2 < NB:
                    fill_vm(b + 2)
                rstd_of(5 + NB + b, 3, b, b + 1)

        @block.scalar
        def _(act):
            act.dma_start(cols[:, :], cols_d).then_inc(ld_vec, 16)
            act.dma_start(rows[:, :, :].rearrange("p a c -> p (a c)"), rows_d[0:4 * C].partition_broadcast(128)).then_inc(ld_vec, 16)
            act.dma_start(gates[:, :], rows_d[4 * C:4 * C + E0].partition_broadcast(128)).then_inc(ld_vec, 16)
            act.dma_start(sim[:, :], sim_d).then_inc(ld_vec, 16)
            for h in range(H0):
                act.dma_start(kv[head_rows(h), :, :].rearrange("p v e -> p (v e)"), kv_d[h, :].partition_broadcast(D0)).then_inc(ld_vec, 16)
            act.wait_ge(ld_vec, 16 * 8)
            nc.scalar.activation(sgate[:, :], gates[:, :], ACT.Exp, scale=-1.0).then_inc(egate_ready, 1)
            act.wait_ge(ld_ctxT, 16)
            for v, (w, b) in enumerate(((WVG, BVG), (WVL, BVL))):
                nc.scalar.activation(vT[:, v, :], cxT[:, :], ACT.Identity, bias=cols[:, b:b + 1],
                                     scale=cols[:, w:w + 1]).then_inc(vT_ready, 1)
            act.wait_ge(c_part, 1)
            nc.scalar.activation(sel[:, :, :], bc(part16[:, :], 2, 128), ACT.Copy)
            nc.scalar.activation(sel2[:, :, :, :].rearrange("p r j d -> p (r j) d"), bc(part16[:, :], 2, HD), ACT.Copy)
            nc.scalar.activation(selw[:, :, :], bc(part8[:, :], 2, HID), ACT.Copy)
            nc.scalar.activation(identb[:, :], ident[:, :], ACT.Copy).then_inc(c_sel, 1)
            for hf in range(2):
                act.wait_ge(sc_ready, hf + 1)
                nc.scalar.activation(sc2[:, :, :, :], sc[:, :, :, :], ACT.Exp, scale=S0_SCALE).then_inc(sce_ready, 1)
                act.wait_ge(xn2T_ps, hf + 1)
                nc.scalar.activation(xn2T[:, bs(hf), :].rearrange("p b t -> p (b t)"), PB[6 + hf][:, :], ACT.Copy).then_inc(xn2T_ready, 1)
                act.wait_ge(gin_ready, hf + 1)
                nc.scalar.activation(gex[:, :, :], gin[:, :, :], ACT.Exp).then_inc(gex_ready, 1)
                act.wait_ge(rwT_ps, hf + 1)
                nc.scalar.activation(rwT[:, bs(hf), :].rearrange("p b t -> p (b t)"), PB[2 + hf][:, 0:256].bitcast(BF16), ACT.Copy).then_inc(rwT_ready, 1)

            def take_qkv(b):
                act.wait_ge(qkv_done, 4 * b + 4)
                if b >= 2:
                    act.wait_ge(aT_ps, b - 1)
                bank = PB[0 if b % 2 == 0 else 2]
                nc.scalar.activation(qk[:, b % 2, :], bank[:, 0:2 * HD], ACT.Copy)
                nc.scalar.activation(v2[:, b % 2, :, :], bc(bank[:, 2 * HD:3 * HD], 1, 2), ACT.Copy).then_inc(qk_ready, 1)

            def take_qkT(b):
                act.wait_ge(qkT_ps, b + 1)
                if b >= 2:
                    act.wait_ge(s2_ps, b - 1)
                nc.scalar.activation(qkT[:, b % 2, :, :].rearrange("p a t -> p (a t)"), PB[1][0:HD, 0:2 * T], ACT.Copy).then_inc(qkT_ready, 1)

            def exp2(b):
                act.wait_ge(s2_ready, b + 1)
                act.wait_ge(nmx_ready, b + 1)
                if b >= 2:
                    act.wait_ge(pT2_ps, b - 1)
                nc.scalar.activation(pn[:, b % 2, :], s2[:, b % 2, :], ACT.Exp, bias=nmx2[:, b:b + 1], scale=A_SCALE,
                                     accum_out=den2[:, b:b + 1]).then_inc(p2_ready, 1)

            def take_pT(b):
                act.wait_ge(pT2_ps, b + 1)
                if b >= 2:
                    act.wait_ge(aT_ps, b - 1)
                nc.scalar.activation(pT2[:, b % 2, :], PB[3][:, 0:T], ACT.Copy).then_inc(pT2_ready, 1)

            def take_aT(b):
                act.wait_ge(aT_ps, b + 1)
                if b >= 2:
                    act.wait_ge(mix_ready, 2 * (b - 1))
                nc.scalar.activation(aT[:, b % 2, :], PB[3][:, 0:T], ACT.Copy).then_inc(aT_ready, 1)

            def take_ks(b):
                act.wait_ge(ksT_ps, b + 1)
                nc.scalar.activation(ks[:, b, :, :].rearrange("p g t -> p (g t)"), PB[5][:, :], ACT.Copy).then_inc(ks_ready, 1)

            def take_xn3T(b):
                act.wait_ge(xn3T_ps, b + 1)
                if b >= 1:
                    act.wait_ge(qp_ready, b)
                nc.scalar.activation(xn3T[:, :], PB[7][:, 0:T], ACT.Copy).then_inc(xn3T_ready, 1)

            def take_qs(b):
                act.wait_ge(qsT_ps, b + 1)
                nc.scalar.activation(qs[:, b, :, :].rearrange("p g t -> p (g t)"), PB[7][:, :], ACT.Copy).then_inc(qs_ready, 1)

            def exp3(u):
                act.wait_ge(ex_in, u + 1)
                nc.scalar.activation(ex[:, u % 4, :], ex[:, u % 4, :], ACT.Exp, scale=S1_SCALE).then_inc(ex_ready, 1)

            def take_exT(v):
                act.wait_ge(exT_ps, v + 1)
                if v >= 4:
                    act.wait_ge(pv_done, v - 3)
                nc.scalar.activation(exT[:, v % 4, :], PB[1 if v % 2 == 0 else 3][:, :], ACT.Copy).then_inc(exT_ready, 1)

            def take_xn4T(hf):
                act.wait_ge(xn4T_ps, hf + 1)
                nc.scalar.activation(xn4T[:, 512 * hf:512 * hf + 512], PB[5][:, :], ACT.Copy).then_inc(xn4T_ready, 1)

            def router_exp(hf):
                act.wait_ge(rin_ready, hf + 1)
                nc.scalar.activation(gex[:, :, 0:E1], gin[:, :, 0:E1], ACT.Exp).then_inc(rex_ready, 1)

            def take_wT(hf):
                act.wait_ge(wT_ps, hf + 1)
                nc.scalar.activation(wT[:, 512 * hf:512 * hf + 512], PB[5][:, 0:256].bitcast(BF16), ACT.Copy).then_inc(wT_ready, 1)

            def silu(k):
                act.wait_ge(up_ready, k + 1)
                if k >= 2:
                    b_read(act, k - 2)
                n = chunk_rows(k % NCH)
                nc.scalar.activation(gated[0:n, k % 2, :], PB[0 if k % 2 == 0 else 2][0:n, :], ACT.Silu).then_inc(gated_ready, 1)

            for s in range(LAST):
                if s % 4 == 0 and 4 <= s <= 4 * NB:
                    take_qkv(s // 4 - 1)
                    take_qkT(s // 4 - 1)
                for b in range(NB):
                    if s == 4 * b + 2:
                        take_ks(b)
                    if s == 4 * b + 5:
                        exp2(b)
                    if s == 4 * b + 7:
                        take_pT(b)
                    if s == 4 * b + 8:
                        take_aT(b)
                    if s == 4 * b + 13:
                        take_xn3T(b)
                    if s == 4 * b + 15:
                        take_qs(b)
                if 0 <= s - Q3 < 4 * NB:
                    exp3(s - Q3)
                if 0 <= s - Q3 - 3 < 4 * NB:
                    take_exT(s - Q3 - 3)
                for hf in range(2):
                    e = Q3 + 4 * (HALF * hf + HALF - 1) + 12
                    if s == e:
                        take_xn4T(hf)
                    if s == e + 2:
                        router_exp(hf)
                    if s == e + 3:
                        take_wT(hf)
                if 0 <= s - F4 < 2 * NCH:
                    silu(s - F4)

        @block.vector
        def _(dve):
            steps = [0]

            def link(ins):
                steps[0] += 1
                ins.then_inc(dve_step, 1)
                dve.wait_ge(dve_step, steps[0])

            V = nc.vector

            def stats(k, b0, b1):
                for b in range(b0, b1):
                    ins = V.bn_stats(st[:, k, b, :], xr[:, b, :])
                link(ins)
                for b in range(b0, b1):
                    ins = V.bn_aggr(mv[:, k, b, :], st[:, k, b, :])
                link(ins)
                V.tensor_scalar(ve[:, k, b0:b1], mv[:, k, b0:b1, 1], EPS, None, ALU.add).then_inc(ve_ready, 1)

            def normalise(dst, k, b0, b1, n, signal):
                dve.wait_ge(rstd_ready, n)
                for b in range(b0, b1):
                    ins = V.tensor_scalar(dst[:, b, :], xr[:, b, :], mv[:, k, b, 0:1], rstd[:, k, b:b + 1],
                                          ALU.subtract, ALU.mult)
                ins.then_inc(signal, 1)

            def first_of_max(f, l, vi, ti, e, w):
                link(V.tensor_reduce(gv[:, vi, :], l, AX.X, ALU.max))
                link(V.tensor_tensor(ga[:, :, 0:e], l, bc(gv[:, vi, :], 2, e), ALU.is_equal))
                link(V.tensor_tensor(ga[:, :, 0:e], ga[:, :, 0:e], bc(w, 1, HALF), ALU.mult))
                link(V.tensor_reduce(gv[:, ti, :], ga[:, :, 0:e], AX.X, ALU.max))
                link(V.tensor_tensor(f, ga[:, :, 0:e], bc(gv[:, ti, :], 2, e), ALU.is_equal))

            def two_best(e):
                l, a, b = lg[:, :, 0:e], f1[:, :, 0:e], f2[:, :, 0:e]
                w = order[:, E0 - e:E0]
                first_of_max(a, l, 0, 1, e, w)
                link(V.scalar_tensor_tensor(out=gin[:, :, 0:e], in0=a, scalar=-1e30, in1=l, op0=ALU.mult, op1=ALU.add))
                first_of_max(b, gin[:, :, 0:e], 2, 3, e, w)
                link(V.tensor_tensor(f1[:, :, 0:e], a, b, ALU.add))

            def weigh(e, mask, into, b0):
                p = rw[:, :, 0:e]
                link(V.tensor_tensor(p, gex[:, :, 0:e], mask, ALU.mult))
                link(V.tensor_reduce(gv[:, 4, :], p, AX.X, ALU.add))
                link(V.reciprocal(gv[:, 5, :], gv[:, 4, :]))
                link(V.tensor_tensor(p, p, bc(gv[:, 5, :], 2, e), ALU.mult))
                for j in range(3):
                    part = into[:, b0:b0 + HALF, j * e:j * e + e]
                    ins = V.tensor_copy(part, p)
                    if j < 2:
                        link(ins)
                        link(V.tensor_tensor(p, p, part, ALU.subtract))
                return ins

            link(V.memset(ones[:, :], 1.0))
            c_ones_done = V.memset(wp2[:, :], 0.0)
            c_ones_done.then_inc(c_ones, 1)
            dve.wait_ge(ld_x[0], 16)
            stats(0, 0, HALF)
            dve.wait_ge(ld_x[1], 16)
            stats(0, HALF, NB)
            dve.wait_ge(c_id, 1)
            V.tensor_reduce(part16[:, :], ident[:, 0:3 * E0].rearrange("p (m e) -> p e m", m=3), AX.X, ALU.add)
            V.tensor_reduce(part8[:, :], ident[:, 0:3 * E1].rearrange("p (m e) -> p e m", m=3), AX.X, ALU.add)
            V.tensor_reduce(hmask[:, :], ident[:, :].rearrange("p (g j i) -> p j g i", g=4, j=4), AX.XY, ALU.add).then_inc(c_part, 1)
            normalise(xna, 0, 0, HALF, 1, xn1_ready)
            normalise(xna, 0, HALF, NB, 2, xn1_ready)
            dve.wait_ge(c_pool, 2)
            V.tensor_copy(order[:, :], orderi[:, :])
            dve.wait_ge(ld_vec, 16 * 8)
            dve.wait_ge(c_ones, 1)
            V.tensor_scalar(wp2[:, :], cols[:, WP:WP + 1], 2.0, None, ALU.mult)
            V.tensor_scalar(kb[:, 0, :], kv[:, 1, :], float(T), None, ALU.mult)
            V.tensor_scalar(kb[:, 1, :], kv[:, 3, :], float(T), None, ALU.mult)
            V.tensor_tensor(sim2[:, :], sim[:, :], sim[:, :], ALU.mult).then_inc(sim2_ready, 1)
            dve.wait_ge(k1_ready, 1)
            dve.wait_ge(sim2_ready, 1)
            for v in range(2):
                ins = V.tensor_tensor(kw[:, v, :, :], PB[2][:, 0:NB * D0].rearrange("p (b e) -> p b e", e=D0),
                                      bc(kv[:, 2 * v, :], 1, NB), ALU.mult)
            ins.then_inc(k1_used, 1)
            dve.wait_ge(k1_used, 1)
            for v in range(2):
                ins = V.tensor_tensor(kw[:, v, :, :], kw[:, v, :, :], bc(kb[:, v, :], 1, NB), ALU.add)
            link(ins)
            for v, q in enumerate((BQG, BQL)):
                V.tensor_scalar(kw[:, v, :, :], kw[:, v, :, :], cols[:, q:q + 1], None, ALU.mult)
            dve.wait_ge(simsum_ready, 1)
            V.tensor_scalar(sim2[:, :], PB[3][:, 0:E0], 1e-24, None, ALU.max).then_inc(ssq_ready, 1)
            dve.wait_ge(egate_ready, 1)
            link(V.tensor_scalar(sgate[:, :], sgate[:, :], 1.0, None, ALU.add))
            link(V.reciprocal(sgate[:, :], sgate[:, :]))

            def channel_scores(hf):
                dve.wait_ge(s_ready, hf + 1)
                bank = PB[hf]
                qk_sum = bank[:, 0:HALF * D0].rearrange("p (b e) -> p b e", e=D0)
                q_sum = bank[:, HALF * D0:HALF * D0 + HALF]
                for v in range(2):
                    V.tensor_tensor(sc[:, v, :, :], qk_sum, bc(kv[:, 2 * v, :], 1, HALF), ALU.mult)
                for v in range(2):
                    ins = V.tensor_tensor(sc2[:, v, :, :], bc(q_sum, 2, D0), bc(kv[:, 2 * v + 1, :], 1, HALF), ALU.mult)
                ins.then_inc(s_used, 1)
                dve.wait_ge(s_used, hf + 1)
                link(V.tensor_tensor(sc[:, :, :, :], sc[:, :, :, :], sc2[:, :, :, :], ALU.add))
                for v, q in enumerate((WQG, WQL)):
                    ins = V.scalar_tensor_tensor(out=sc[:, v, :, :], in0=sc[:, v, :, :], scalar=cols[:, q:q + 1],
                                                 in1=kw[:, v, bs(hf), :], op0=ALU.mult, op1=ALU.add)
                link(ins)
                flat = sc[:, :, :, :].rearrange("p v b e -> p (v b) e")
                link(V.tensor_reduce(cm[:, :], flat, AX.X, ALU.max))
                V.tensor_tensor(flat, flat, bc(cm[:, :], 2, D0), ALU.subtract).then_inc(sc_ready, 1)

            def channel_weights(hf):
                dve.wait_ge(sce_ready, hf + 1)
                e = sc2[:, :, :, :].rearrange("p v b e -> p (v b) e")
                w = sc[:, :, :, :].rearrange("p v b e -> p (v b) e")
                link(V.tensor_reduce(cs[:, :], e, AX.X, ALU.add))
                link(V.reciprocal(cs[:, :], cs[:, :]))
                link(V.scalar_tensor_tensor(out=w, in0=e, scalar=wp2[:, 0:1], in1=bc(cs[:, :], 2, D0), op0=ALU.mult, op1=ALU.mult))
                for h in range(H0):
                    r = head_rows(h)
                    ins = V.transpose(bd[r, hf, :, :, r].rearrange("p v b e -> p (v b) e"), w[r, :, :])
                ins.then_inc(bd_ready, 1)

            def after_channel_attention(hf):
                dve.wait_ge(att_ready, hf + 1)
                dve.wait_ge(xbp_ready, hf + 1)
                x = xr[:, bs(hf), :].rearrange("p b c -> p (b c)")
                V.tensor_tensor(x, x, PB[4 + hf][:, :], ALU.add).then_inc(x1_ready, 1)
                dve.wait_ge(x1_ready, hf + 1)
                stats(1, HALF * hf, HALF * hf + HALF)

            def second_norm(hf):
                b0 = HALF * hf
                normalise(xnb, 1, b0, b0 + HALF, 3 + hf, xn2_ready)
                h = hn[:, bs(hf)]
                link(V.tensor_tensor(h, rstd[:, 1, bs(hf)], rstd[:, 1, bs(hf)], ALU.mult))
                link(V.scalar_tensor_tensor(out=h, in0=h, scalar=float(C), in1=mv[:, 1, bs(hf), 1], op0=ALU.mult, op1=ALU.mult))
                V.tensor_scalar(h, h, 1e-24, None, ALU.max).then_inc(hn_ready, 1)

            def gate(hf):
                dve.wait_ge(lg_ps, hf + 1)
                dve.wait_ge(rhn_ready, hf + 1)
                V.tensor_tensor(lg[:, :, :], PB[hf][:, 0:HALF * E0].rearrange("p (b e) -> p b e", e=E0),
                                bc(rhn[:, bs(hf)], 2, E0), ALU.mult).then_inc(lg_used, 1)
                dve.wait_ge(lg_used, hf + 1)
                link(V.tensor_tensor(lg[:, :, :], lg[:, :, :], bc(sgate[:, :], 1, HALF), ALU.subtract))
                two_best(E0)
                link(V.tensor_scalar(gv[:, 1, :], gv[:, 0, :], 0.0, None, ALU.is_le))
                link(V.tensor_tensor(f1[:, :, :], f1[:, :, :], bc(gv[:, 1, :], 2, E0), ALU.mult))
                link(V.scalar_tensor_tensor(out=f2[:, :, :], in0=lg[:, :, :], scalar=0.0, in1=f1[:, :, :], op0=ALU.is_gt, op1=ALU.max))
                link(V.tensor_scalar(gv[:, 0, :], gv[:, 0, :], 0.0, None, ALU.max))
                V.scalar_tensor_tensor(out=gin[:, :, :], in0=lg[:, :, :], scalar=0.0, in1=bc(gv[:, 0, :], 2, E0),
                                       op0=ALU.max, op1=ALU.subtract).then_inc(gin_ready, 1)
                dve.wait_ge(gex_ready, hf + 1)
                weigh(E0, f2[:, :, :], parts, HALF * hf).then_inc(parts_ready, 1)

            dve.wait_ge(zeroed, 1)
            for hf in range(2):
                channel_scores(hf)
                channel_weights(hf)
                after_channel_attention(hf)
                second_norm(hf)
                if hf == 0:
                    dve.wait_ge(simr_ready, 1)
                    V.tensor_tensor(simn[:, :], sim[:, :], sim2[:, :], ALU.mult).then_inc(simn_ready, 1)
                    dve.wait_ge(zeroed, 2)
                gate(hf)

            def scale_hidden(i):
                b, q = i // 4, i % 4
                dve.wait_ge(rb_ready, i + 1)
                if i >= 8:
                    dve.wait_ge(qkv_done, i - 7)
                V.tensor_tensor(hm[:, b % 2, 4 * q:4 * q + 4, :], bc(xn2T[:, b, :], 1, 4),
                                PB[4 if i % 2 == 0 else 6][:, :].rearrange("p (e t) -> p e t", e=4), ALU.mult).then_inc(hm_ready, 1)

            def split(src, dst, hi, lo):
                s4 = bc(src[:, :].rearrange("p (g c) -> p g c", g=4), 2, 2)
                link(V.tensor_copy(dst[:, :, hi, :].bitcast(F32R), s4))
                return V.tensor_tensor(dst[:, :, lo, :], s4, dst[:, :, hi, :], ALU.subtract)

            def split_k(b):
                dve.wait_ge(kp_ready, b + 1)
                V.tensor_tensor(kf[:, :], PB[5][:, 0:C], rows[:, R_BK, :], ALU.add).then_inc(kp_used, 1)
                dve.wait_ge(kp_used, b + 1)
                if b >= 1:
                    dve.wait_ge(ksT_ps, b)
                split(kf, ksp, slice(0, 4, 2), slice(1, 4, 2)).then_inc(ksp_ready, 1)

            def split_q(b):
                dve.wait_ge(qp_ready, b + 1)
                if b >= 1:
                    dve.wait_ge(qsT_ps, b)
                link(V.tensor_tensor(qf[:, :], PB[7][:, 0:C], rows[:, R_BQ, :], ALU.add))
                split(qf, qsp, slice(0, 2), slice(2, 4)).then_inc(qsp_ready, 1)

            def softmax2_max(b):
                dve.wait_ge(s2_ps, b + 1)
                V.tensor_tensor_reduce(s2[:, b % 2, :], PB[1][:, 0:T], causal[:, :], 1.0, NEG, ALU.add, ALU.max,
                                       mx2[:, b:b + 1]).then_inc(s2_ready, 1)
                dve.wait_ge(s2_ready, b + 1)
                V.tensor_scalar(nmx2[:, b:b + 1], mx2[:, b:b + 1], -A_SCALE, None, ALU.mult).then_inc(nmx_ready, 1)

            def softmax2_norm(b):
                dve.wait_ge(p2_ready, b + 1)
                link(V.reciprocal(rden2[:, b:b + 1], den2[:, b:b + 1]))
                V.tensor_scalar(pn[:, b % 2, :], pn[:, b % 2, :], rden2[:, b:b + 1], None, ALU.mult).then_inc(pn_ready, 1)

            def mix(b, i):
                dve.wait_ge(mixw_ready, 2 * b + i + 1)
                dve.wait_ge(aT_ready, b + 1)
                if b >= 1:
                    dve.wait_ge(o_ready, b)
                V.tensor_tensor(mixT[:, 4 * i:4 * i + 4, :], bc(aT[:, b % 2, :], 1, 4),
                                PB[5][:, :].rearrange("p (r t) -> p r t", r=4), ALU.mult).then_inc(mix_ready, 1)

            def after_mixture(b):
                dve.wait_ge(o_ready, b + 1)
                V.tensor_tensor(xr[:, b, :], xr[:, b, :], PB[5][:, 0:C], ALU.add).then_inc(x2_ready, 1)
                dve.wait_ge(x2_ready, b + 1)
                stats(2, b, b + 1)

            def softmax3(u):
                b, g = u // 4, u % 4
                bank = PB[0 if u % 2 == 0 else 2][:, :].rearrange("p (j k) -> p j k", j=4)
                dve.wait_ge(s3_ready, u + 1)
                link(V.tensor_reduce(mx3[:, u % 8, :], bank, AX.X, ALU.max))
                if u >= 4:
                    dve.wait_ge(exT_ps, u - 3)
                V.tensor_tensor(ex[:, u % 4, :].rearrange("p (j k) -> p j k", j=4), bank, bc(mx3[:, u % 8, :], 2, T),
                                ALU.subtract).then_inc(ex_in, 1)

            def divide(b):
                dve.wait_ge(pv_done, 4 * b + 4)
                bank = PB[4][:, 0:2 * T]
                link(V.reciprocal(ry[:, :, :].rearrange("p g t -> p (g t)"), bank[64:128, :]))
                if b >= 2:
                    dve.wait_ge(c_ready, b - 1)
                for g in range(2):
                    ins = V.tensor_tensor(yT[64 * g:64 * g + 64, b % 2, :], ry[:, g, :], bank[0:64, T * g:T * g + T], ALU.mult)
                ins.then_inc(yT_ready, 1)

            def after_attention(b):
                dve.wait_ge(c_ready, b + 1)
                dve.wait_ge(xbc_ready, b + 1)
                V.tensor_tensor(xr[:, b, :], xr[:, b, :], PB[6][:, 0:C], ALU.add).then_inc(x3_ready, 1)
                dve.wait_ge(x3_ready, b + 1)
                stats(3, b, b + 1)

            def route(hf):
                dve.wait_ge(rt_ps, hf + 1)
                link(V.tensor_copy(lg[:, :, 0:E1], PB[5][:, 0:HALF * E1].rearrange("p (b e) -> p b e", e=E1)))
                two_best(E1)
                V.tensor_tensor(gin[:, :, 0:E1], lg[:, :, 0:E1], bc(gv[:, 0, :], 2, E1), ALU.subtract).then_inc(rin_ready, 1)

            def route_weights(hf):
                dve.wait_ge(zeroed, 3)
                dve.wait_ge(rex_ready, hf + 1)
                weigh(E1, f1[:, :, 0:E1], wparts, HALF * hf).then_inc(wparts_ready, 1)

            def hidden(k):
                ch = k % NCH
                n = chunk_rows(ch)
                bank = PB[7 if k % 2 == 0 else 1][0:n, :]
                dve.wait_ge(gated_ready, k + 1)
                if k >= 3:
                    dve.wait_ge(down_done, k - 2)
                if ch >= NROUTED:
                    V.tensor_tensor(hid[0:n, k % 3, :], gated[0:n, k % 2, :], bank, ALU.mult).then_inc(hid_ready, 1)
                    return
                if k >= 2:
                    dve.wait_ge(hid_ready, k - 1)
                V.tensor_tensor(prod[:, k % 2, :], gated[:, k % 2, :], bank, ALU.mult).then_inc(prod_ready, 1)
                dve.wait_ge(prod_ready, n_routed(k))
                V.tensor_tensor(hid[:, k % 3, :], prod[:, k % 2, :], PB[3 if n_routed(k) % 2 == 1 else 4][:, :], ALU.mult).then_inc(hid_ready, 1)

            def result(hf):
                dve.wait_ge(down_done, NCH * (hf + 1))
                x = xr[:, bs(hf), :].rearrange("p b c -> p (b c)")
                V.tensor_tensor(x, x, PB[6][:, :], ALU.add).then_inc(out_ready, 1)

            scale_hidden(0)
            scale_hidden(1)
            dve.wait_ge(c_pool, 3)
            for s in range(LAST):
                if s + 2 < 4 * NB:
                    scale_hidden(s + 2)
                for b in range(NB):
                    if s == 4 * b:
                        split_k(b)
                    if s == 4 * b + 5:
                        softmax2_max(b)
                    if s == 4 * b + 6:
                        softmax2_norm(b)
                    if s == 4 * b + 9:
                        mix(b, 0)
                    if s == 4 * b + 10:
                        mix(b, 1)
                    if s == 4 * b + 11:
                        after_mixture(b)
                    if s == 4 * b + 12:
                        normalise(xna, 2, b, b + 1, 5 + b, xn3_ready)
                    if s == 4 * b + 14:
                        split_q(b)
                if 0 <= s - Q3 < 4 * NB:
                    softmax3(s - Q3)
                for b in range(NB):
                    if s == Q3 + 4 * b + 8:
                        divide(b)
                    if s == Q3 + 4 * b + 9:
                        after_attention(b)
                    if s == Q3 + 4 * b + 11:
                        normalise(xnb, 3, b, b + 1, 5 + NB + b, xn4_ready)
                for hf in range(2):
                    e = Q3 + 4 * (HALF * hf + HALF - 1) + 12
                    if s == e + 1:
                        route(hf)
                    if s == e + 2:
                        route_weights(hf)
                if 0 <= s - F4 < 2 * NCH:
                    hidden(s - F4)
                if s - F4 in (NCH + 2, 2 * NCH + 2):
                    result(0 if s - F4 == NCH + 2 else 1)

        @block.tensor
        def _(pe):
            mm = nc.tensor.matmul
            tr = nc.tensor.transpose
            pe.wait_ge(c_ones, 1)
            pe.wait_ge(ld_ctx[0], 16)
            pe.wait_ge(ld_ctx[1], 16)
            for b in range(NB):
                for h in range(H0):
                    r = head_rows(h)
                    last = mm(PB[2][r, D0 * b:D0 * b + D0], ones[:, 0:D0], cx[:, b, r], start=True, stop=True)
            last.then_inc(k1_ready, 1)
            pe.wait_ge(sim2_ready, 1)
            mm(PB[3][:, 0:E0], ones[:, :], sim2[:, :], start=True, stop=True).then_inc(simsum_ready, 1)
            for hf in range(2):
                pe.wait_ge(xn1_ready, hf + 1)
                for b in range(HALF * hf, HALF * hf + HALF):
                    i = b % HALF
                    for h in range(H0):
                        r = head_rows(h)
                        mm(PB[hf][r, D0 * i:D0 * i + D0], xna[:, b, r], cx[:, b, r], start=True, stop=True)
                        last = mm(PB[hf][r, HALF * D0 + i:HALF * D0 + i + 1], xna[:, b, r], ones[:, 0:1], start=True, stop=True)
                last.then_inc(s_ready, 1)
            pe.wait_ge(vT_ready, 2)
            for hf in range(2):
                pe.wait_ge(bd_ready, hf + 1)
                for i in range(HALF):
                    b = HALF * hf + i
                    for v in range(2):
                        last = mm(PB[4 + hf][:, C * i:C * i + C], vT[:, v, T * b:T * b + T], bd[:, hf, v, i, :],
                                  start=(v == 0), stop=(v == 1))
                last.then_inc(att_ready, 1)
                pe.wait_ge(xn2_ready, hf + 1)
                for i in range(HALF):
                    last = tr(PB[6 + hf][:, T * i:T * i + T], xnb[:, HALF * hf + i, :], ident[:, :])
                last.then_inc(xn2T_ps, 1)
                pe.wait_ge(xn2T_ready, hf + 1)
                pe.wait_ge(simn_ready, 1)
                pe.wait_ge(s_used, hf + 1)
                for i in range(HALF):
                    last = mm(PB[hf][:, E0 * i:E0 * i + E0], xn2T[:, HALF * hf + i, :], simn[:, :], start=True, stop=True)
                last.then_inc(lg_ps, 1)
                pe.wait_ge(c_sel, 1)
                pe.wait_ge(parts_ready, hf + 1)
                pe.wait_ge(k1_used, 1) if hf == 0 else pe.wait_ge(ssq_ready, 1)
                for i in range(HALF):
                    last = tr(PB[2 + hf][:, 0:256].bitcast(BF16)[:, T * i:T * i + T], parts[:, HALF * hf + i, :], identb[:, :])
                last.then_inc(rwT_ps, 1)

            def spread(i):
                b, q = i // 4, i % 4
                pe.wait_ge(rwT_ready, b // HALF + 1)
                if i == 0:
                    pe.wait_ge(x1_ready, 1)
                if i == 1:
                    pe.wait_ge(xn2T_ready, 1)
                if i >= 2:
                    pe.wait_ge(hm_ready, i - 1)
                for e in range(4):
                    last = mm(PB[4 if i % 2 == 0 else 6][:, T * e:T * e + T], sel[:, 4 * q + e, :], rwT[:, b, :],
                              start=True, stop=True)
                last.then_inc(rb_ready, 1)

            def project(i):
                b, q = i // 4, i % 4
                bank = PB[0 if b % 2 == 0 else 2]
                pe.wait_ge(hm_ready, i + 1)
                if i == 0:
                    pe.wait_ge(ld_qkv, 16)
                    pe.wait_ge(lg_used, 1)
                if i == 4:
                    pe.wait_ge(rwT_ready, 1)
                if q == 0 and b >= 2:
                    pe.wait_ge(qk_ready, b - 1)
                for e in range(4 * q, 4 * q + 4):
                    last = mm(bank[:, 0:3 * HD], hm[:, b % 2, e, :], wqkv[:, e, :], start=(e == 0), stop=(e == E0 - 1))
                last.then_inc(qkv_done, 1)

            def turn_qk(b):
                if b >= 1:
                    pe.wait_ge(s2_ready, b)
                else:
                    pe.wait_ge(lg_used, 2)
                pe.wait_ge(qk_ready, b + 1)
                tr(PB[1][0:HD, 0:T], qk[:, b % 2, 0:HD], ident[:, :])
                tr(PB[1][0:HD, T:2 * T], qk[:, b % 2, HD:2 * HD], ident[:, :]).then_inc(qkT_ps, 1)

            def scores2(b):
                pe.wait_ge(qkT_ready, b + 1)
                mm(PB[1][:, 0:T], qkT[:, b % 2, 0, :], qkT[:, b % 2, 1, :], start=True, stop=True).then_inc(s2_ps, 1)

            def turn_p(b):
                pe.wait_ge(aT_ready, b) if b >= 1 else pe.wait_ge(rwT_ready, 2)
                pe.wait_ge(pn_ready, b + 1)
                tr(PB[3][:, 0:T], pn[:, b % 2, :], ident[:, :]).then_inc(pT2_ps, 1)

            def attend2(b):
                pe.wait_ge(pT2_ready, b + 1)
                mm(PB[3][:, 0:T], v2[:, b % 2, :, :].rearrange("p j d -> p (j d)"), pT2[:, b % 2, :], start=True, stop=True).then_inc(aT_ps, 1)

            def project_k(b):
                if b == 0:
                    pe.wait_ge(ld_attn, 16)
                    pe.wait_ge(x1_ready, 2)
                else:
                    pe.wait_ge(ks_ready, b)
                if b >= 3:
                    pe.wait_ge(x2_ready, b - 2)
                mm(PB[5][:, 0:C], cxT[:, T * b:T * b + T], wattn[:, 0, :], start=True, stop=True).then_inc(kp_ready, 1)

            def turn_k(b):
                pe.wait_ge(ksp_ready, b + 1)
                if b >= 2:
                    pe.wait_ge(mix_ready, 2 * (b - 2) + 1)
                for g in range(4):
                    last = tr(PB[5][:, T * g:T * g + T], ksp[:, g, :, :].rearrange("p a c -> p (a c)"), ident[:, :])
                last.then_inc(ksT_ps, 1)

            def spread_pairs(b, i):
                if b + 2 < NB:
                    pe.wait_ge(kp_used, b + 3) if i == 0 else pe.wait_ge(ks_ready, b + 3)
                if i == 0 and b >= 1:
                    pe.wait_ge(x2_ready, b)
                if i == 1:
                    pe.wait_ge(mix_ready, 2 * b + 1)
                for r in range(4):
                    last = mm(PB[5][:, T * r:T * r + T], sel2[:, 4 * i + r, :, :].rearrange("p j d -> p (j d)"), rwT[:, b, :],
                              start=True, stop=True)
                last.then_inc(mixw_ready, 1)

            def project_o(b):
                if b == 0:
                    pe.wait_ge(ld_o, 16)
                pe.wait_ge(mix_ready, 2 * b + 2)
                for r in range(E0 // 2):
                    last = mm(PB[5][:, 0:C], mixT[:, r, :], wo[:, r, :], start=(r == 0), stop=(r == E0 // 2 - 1))
                last.then_inc(o_ready, 1)

            def turn_x3(b):
                pe.wait_ge(qs_ready, b) if b >= 1 else pe.wait_ge(xn2T_ready, 2)
                pe.wait_ge(xn3_ready, b + 1)
                tr(PB[7][:, 0:T], xna[:, b, :], ident[:, :]).then_inc(xn3T_ps, 1)

            def project_q(b):
                pe.wait_ge(xn3T_ready, b + 1)
                mm(PB[7][:, 0:C], xn3T[:, :], wattn[:, 1, :], start=True, stop=True).then_inc(qp_ready, 1)

            def turn_q(b):
                pe.wait_ge(qsp_ready, b + 1)
                for g in range(4):
                    last = tr(PB[7][:, T * g:T * g + T], qsp[:, g, :, :].rearrange("p a c -> p (a c)"), ident[:, :])
                last.then_inc(qsT_ps, 1)

            def scores3(u):
                b, g = u // 4, u % 4
                if u < 2:
                    pe.wait_ge(qk_ready, NB - 1 + u)
                else:
                    pe.wait_ge(ex_in, u - 1)
                pe.wait_ge(km_ready, b + 1)
                pe.wait_ge(qs_ready, b + 1)
                mm(PB[0 if u % 2 == 0 else 2][:, :], qs[:, b, g, :], km[:, b % 2, g, :, :].rearrange("p j k -> p (j k)"),
                   start=True, stop=True).then_inc(s3_ready, 1)

            def turn_ex(v):
                if v == 0:
                    pe.wait_ge(s2_ready, NB)
                elif v == 1:
                    pe.wait_ge(aT_ready, NB)
                else:
                    pe.wait_ge(exT_ready, v - 1)
                pe.wait_ge(ex_ready, v + 1)
                for j in range(4):
                    last = tr(PB[1 if v % 2 == 0 else 3][:, T * j:T * j + T], ex[:, v % 4, T * j:T * j + T], ident[:, :])
                last.then_inc(exT_ps, 1)

            def attend3(w):
                b, g = w // 4, w % 4
                pe.wait_ge(exT_ready, w + 1)
                if g == 0:
                    pe.wait_ge(vm_ready, b + 1)
                    pe.wait_ge(yT_ready, b) if b >= 1 else pe.wait_ge(hm_ready, 4 * NB)
                for j in range(4):
                    h = 4 * g + j
                    last = mm(PB[4][:, T * (g // 2):T * (g // 2) + T], vm[:, b % 2, h, :], exT[:, w % 4, T * j:T * j + T],
                              start=(h % 8 == 0), stop=(h % 8 == 7))
                last.then_inc(pv_done, 1)

            def project_c(b):
                pe.wait_ge(x3_ready, b) if b >= 1 else pe.wait_ge(hm_ready, 4 * NB)
                pe.wait_ge(yT_ready, b + 1)
                mm(PB[6][:, 0:C], yT[:, b % 2, :], wattn[:, 2, :], start=True, stop=True).then_inc(c_ready, 1)

            def turn_x4(hf):
                pe.wait_ge(wT_ready, 1) if hf else pe.wait_ge(x2_ready, NB)
                pe.wait_ge(xn4_ready, HALF * hf + HALF)
                for i in range(HALF):
                    last = tr(PB[5][:, T * i:T * i + T], xnb[:, HALF * hf + i, :], ident[:, :])
                last.then_inc(xn4T_ps, 1)

            def router(hf):
                pe.wait_ge(xn4T_ready, hf + 1)
                if hf == 0:
                    pe.wait_ge(ld_up, 48)
                for i in range(HALF):
                    b = HALF * hf + i
                    last = mm(PB[5][:, E1 * i:E1 * i + E1], xn4T[:, T * b:T * b + T], wg[:, :], start=True, stop=True)
                last.then_inc(rt_ps, 1)

            def turn_w(hf):
                pe.wait_ge(wparts_ready, hf + 1)
                for i in range(HALF):
                    last = tr(PB[5][:, 0:256].bitcast(BF16)[:, T * i:T * i + T], wparts[:, HALF * hf + i, :], identb[:, :])
                last.then_inc(wT_ps, 1)

            def up(k):
                hf, ch = k // NCH, k % NCH
                n = chunk_rows(ch)
                c0 = 128 * ch
                x = xn4T[:, 512 * hf:512 * hf + 512]
                if k < 2:
                    pe.wait_ge(ex_in, 4 * NB - 1 + k)
                    pe.wait_ge(exT_ready, 4 * NB)
                    pe.wait_ge(qs_ready, NB)
                else:
                    pe.wait_ge(gated_ready, k - 1)
                    b_read(pe, k - 2)
                pe.wait_ge(xn4T_ready, hf + 1)
                mm(PB[0 if k % 2 == 0 else 2][0:n, :], wa[:, c0:c0 + n], x, start=True, stop=True)
                last = mm(PB[7 if k % 2 == 0 else 1][0:n, :], wb[:, c0:c0 + n], x, start=True, stop=True)
                if ch < NROUTED:
                    r = n_routed(k)
                    if r == 2:
                        pe.wait_ge(yT_ready, NB)
                    if r >= 3:
                        pe.wait_ge(hid_ready, routed_chunk(r - 2) + 1)
                    pe.wait_ge(wT_ready, hf + 1)
                    last = mm(PB[3 if r % 2 == 1 else 4][:, :], selw[:, :, :].rearrange("p e j -> p (e j)")[:, c0:c0 + 128],
                              wT[:, 512 * hf:512 * hf + 512], start=True, stop=True)
                last.then_inc(up_ready, 1)

            def down(k):
                hf, ch = k // NCH, k % NCH
                n = chunk_rows(ch)
                pe.wait_ge(hid_ready, k + 1)
                if ch == 0:
                    pe.wait_ge(out_ready, 1) if hf else pe.wait_ge(x3_ready, NB)
                    pe.wait_ge(ld_dn, 32)
                for i in range(HALF):
                    last = mm(PB[6][:, C * i:C * i + C], hid[0:n, k % 3, T * i:T * i + T], wdn[0:n, ch, :],
                              start=(ch == 0 and i == 0), stop=(ch == NCH - 1), skip_group_check=True)
                last.then_inc(down_done, 1)

            spread(0)
            spread(1)
            for s in range(LAST):
                if s + 2 < 4 * NB:
                    spread(s + 2)
                if s < 4 * NB:
                    project(s)
                for b in range(NB):
                    if s == 4 * b:
                        project_k(b)
                    if s == 4 * b + 2:
                        turn_k(b)
                    if s == 4 * b + 4:
                        turn_qk(b)
                    if s == 4 * b + 5:
                        scores2(b)
                    if s == 4 * b + 7:
                        turn_p(b)
                    if s == 4 * b + 8:
                        attend2(b)
                    if s == 4 * b + 13:
                        turn_x3(b)
                    if s == 4 * b + 14:
                        project_q(b)
                    if s == 4 * b + 15:
                        turn_q(b)
                for b in range(NB):
                    if s == 4 * b + 9:
                        spread_pairs(b, 0)
                    if s == 4 * b + 10:
                        spread_pairs(b, 1)
                    if s == 4 * b + 11:
                        project_o(b)
                if 0 <= s - Q3 < 4 * NB:
                    scores3(s - Q3)
                if 0 <= s - Q3 - 3 < 4 * NB:
                    turn_ex(s - Q3 - 3)
                if 0 <= s - Q3 - 4 < 4 * NB:
                    attend3(s - Q3 - 4)
                for b in range(NB):
                    if s == Q3 + 4 * b + 9:
                        project_c(b)
                for hf in range(2):
                    e = Q3 + 4 * (HALF * hf + HALF - 1) + 12
                    if s == e:
                        turn_x4(hf)
                    if s == e + 1:
                        router(hf)
                    if s == e + 3:
                        turn_w(hf)
                if 0 <= s - F4 < 2 * NCH:
                    up(s - F4)
                if 0 <= s - F4 - 2 < 2 * NCH:
                    down(s - F4 - 2)


def kernel(**inputs):
    import numpy as np
    import concourse.bacc as bacc
    from concourse.bass_utils import run_bass_kernel_spmd

    a = {k: np.asarray(v) for k, v in inputs.items()}
    xa, fa, xb, fb = "L0_xattn_", "L0_ffn_", "L1_xattn_", "L1_ffn_"
    ctx = a["ctx_1024"]
    kvecs = np.stack([a[xa + n] for n in ("wkg", "bkg", "wkl", "bkl")])
    laid = {
        "x": a["x"].transpose(1, 0, 2),
        "ctx": ctx.transpose(1, 0, 2),
        "ctxT": ctx.reshape(NB * T, C).T,
        "cols": np.stack([a[xa + n] for n in ("wqg", "bqg", "wql", "bql", "wvg", "bvg", "wvl", "bvl", "wp")], axis=1),
        "rows": np.concatenate([a[xa + "bp"], a[xb + "bc"], a[xb + "bk"], a[xb + "bq"], a[fa + "gates"]]),
        "kv": kvecs.reshape(4, H0, D0).transpose(1, 0, 2).reshape(H0, 4 * D0),
        "sim": a[fa + "sim_matrix"],
        "wattn": np.stack([a[xb + n].T for n in ("Wk", "Wq", "Wc")], axis=1),
        "wqkv": np.concatenate([a[fa + n] for n in ("q_proj", "k_proj", "v_proj")], axis=2).transpose(1, 0, 2),
        "wo": a[fa + "o_proj"].reshape(E0 // 2, 2 * HD, C).transpose(1, 0, 2),
        "wa": np.concatenate([a[fb + "W1"].transpose(1, 0, 2).reshape(C, E1 * HID), a[fb + "Ws1"]], axis=1),
        "wb": np.concatenate([a[fb + "W2"].transpose(1, 0, 2).reshape(C, E1 * HID), a[fb + "Ws2"]], axis=1),
        "wdn": np.concatenate([a[fb + "W3"].reshape(E1 * HID, C), a[fb + "Ws3"]], axis=0),
        "wg": a[fb + "Wg"],
    }
    nc = bacc.Bacc("TRN2", target_bir_lowering=False, num_devices=1)
    arrays, args = {}, []
    for name, v in laid.items():
        v = np.ascontiguousarray(v)
        arrays[f"{name}_dram"] = v
        args.append(nc.dram_tensor(f"{name}_dram", v.shape, mybir.dt.from_np(v.dtype), kind="ExternalInput").ap())
    out = nc.dram_tensor("out_dram", (T, NB, C), F32, kind="ExternalOutput").ap()
    build(nc, *args, out)
    r = run_bass_kernel_spmd(nc, [arrays], core_ids=[0])
    return np.ascontiguousarray(r.results[0]["out_dram"].transpose(1, 0, 2))
```

```python
from contextlib import ExitStack

import concourse.bass as bass
from concourse import mybir

F32 = mybir.dt.float32
F32R = mybir.dt.float32r
BF16 = mybir.dt.bfloat16
I32 = mybir.dt.int32
ALU = mybir.AluOpType
ACT = mybir.ActivationFunctionType
AX = mybir.AxisListType

NB = 8
T = 128
C = 128
H0, D0 = 4, 32
E0, HD = 16, 64
H1, D1 = 16, 8
E1, HID = 8, 176
HS = 2 * HID
HALF = NB // 2
EPS = 1e-5
NEG = -1e30
RUP = E1 * HID + HS
NCH = -(-RUP // 128)
NROUTED = E1 * HID // 128
S0_SCALE = C ** -0.5
A_SCALE = HD ** -0.5
S1_SCALE = D1 ** -0.5

Q3 = 4 * NB + 2
F4 = Q3 + 4 * NB + 4
LAST = F4 + 2 * NCH + 3

WQG, BQG, WQL, BQL, WVG, BVG, WVL, BVL, WP = range(9)
R_BP, R_BC, R_BK, R_BQ = range(4)


def bc(ap, axis, n):
    a = ap.unsqueeze(axis)
    shape = list(a.shape)
    shape[axis] = n
    return a.to_broadcast(shape)


def diag(tile, start):
    a = tile.rearrange("p h c -> p (h c)")
    return bass.AP(a.tensor, a.offset + start, [list(a.ap[0]), [128 + D1, 8], [1, D1]])


def build(nc, x_d, ctx_d, ctxT_d, cols_d, rows_d, kv_d, wattn_d, wqkv_d, wo_d, wa_d, wb_d, wdn_d, wg_d, out_d):
    with ExitStack() as ctx:
        def sb(name, shape, dt=F32):
            return ctx.enter_context(nc.sbuf_tensor(name, shape, dt))

        def sem(name):
            return ctx.enter_context(nc.semaphore(name))

        xr = sb("xr", [T, NB, C])
        cx = sb("cx", [T, NB, C])
        cxT = sb("cxT", [C, NB * T])
        colsim = sb("colsim", [C, 9 + E0])
        cols, sim = colsim[:, 0:9], colsim[:, 9:9 + E0]
        rowv = sb("rowv", [128, 4 * C + E0])
        rows = rowv[:, 0:4 * C].rearrange("p (a c) -> p a c", c=C)
        gates = rowv[:, 4 * C:4 * C + E0]
        kv = sb("kv", [C, 4, D0])
        wattn = sb("wattn", [C, 3, C])
        wqkv = sb("wqkv", [C, E0, 3 * HD])
        wo = sb("wo", [2 * HD, E0 // 2, C])
        wa = sb("wa", [C, RUP])
        wb = sb("wb", [C, RUP])
        wdn = sb("wdn", [128, NCH, C])
        wg = sb("wg", [C, E1])

        ident = sb("ident", [128, 128])
        identb = sb("identb", [128, 128], BF16)
        ones = sb("ones", [128, 128])
        causal = sb("causal", [T, T])
        orderi = sb("orderi", [128, E0], I32)
        order = sb("order", [128, E0])
        wp2 = sb("wp2", [C, 1])
        part16 = sb("part16", [128, E0])
        part8 = sb("part8", [128, E1])
        hmask = sb("hmask", [128, 4])
        sel = sb("sel", [128, E0, 128], BF16)
        sel2 = sb("sel2", [128, E0 // 2, 2, HD], BF16)
        selw = sb("selw", [128, E1, HID], BF16)

        st = sb("st", [128, 4, NB, 6])
        mv = sb("mv", [128, 4, NB, 2])
        ve = sb("ve", [128, 4, NB])
        rstd = sb("rstd", [128, 4, NB])
        hn = sb("hn", [128, NB])
        rhn = sb("rhn", [128, NB])
        xna = sb("xna", [T, NB, C])
        xnb = sb("xnb", [T, NB, C])
        xn2T = sb("xn2T", [C, NB, T])
        xn4T = xn2T[:, :, :].rearrange("p b t -> p (b t)")

        kw = sb("kw", [C, 2, NB, D0])
        kb = sb("kb", [C, 2, D0])
        cm = sb("cm", [C, 2 * NB])
        cs = sb("cs", [C, 2 * NB])

        sim2 = sb("sim2", [C, E0])
        simn = sb("simn", [C, E0])
        sgate = sb("sgate", [128, E0])
        lg = sb("lg", [T, NB, E0])
        ga = sb("ga", [T, NB, E0])
        f1 = sb("f1", [T, NB, E0])
        f2 = sb("f2", [T, NB, E0])
        gv = sb("gv", [T, 6, NB])
        gin = sb("gin", [T, NB, E0])
        gex = sb("gex", [T, NB, E0])
        rw = sb("rw", [T, NB, E0])
        parts = sb("parts", [T, NB, 128], BF16)
        rwT = sb("rwT", [128, NB, T], BF16)
        wparts = sb("wparts", [T, NB, 128], BF16)
        wT = sb("wT", [128, NB * T], BF16)

        hm = sb("hm", [C, 2, E0, T])
        qk = sb("qk", [T, 2, 2 * HD])
        v2 = sb("v2", [T, 2, 2, HD])
        qkT = sb("qkT", [HD, 2, 2, T])
        s2 = sb("s2", [T, 2, T])
        mx2 = sb("mx2", [T, NB])
        nmx2 = sb("nmx2", [T, NB])
        den2 = sb("den2", [T, NB])
        rden2 = sb("rden2", [T, NB])
        pn = sb("pn", [T, 2, T])
        pT2 = sb("pT2", [T, 2, T])
        aT = sb("aT", [2 * HD, 2, T])
        m16 = sb("m16", [128, E0])
        mixT = sb("mixT", [2 * HD, E0 // 2, T])

        kf = sb("kf", [T, C])
        qf = sb("qf", [T, C])
        ksp = sb("ksp", [T, 4, 4, 32])
        qsp = sb("qsp", [T, 4, 4, 32])
        ks = sb("ks", [128, NB, 4, T], F32R)
        qs = sb("qs", [128, NB, 4, T], F32R)
        xn3T = sb("xn3T", [C, T])
        km = sb("km", [128, 2, 4, 4, T], F32R)
        vm = sb("vm", [T, 2, H1, 128])
        ex = sb("ex", [T, 4, 4 * T])
        exT = sb("exT", [T, 4, 4 * T])
        mx3 = sb("mx3", [T, 8, 4])
        ry = sb("ry", [64, 2, T])
        yT = sb("yT", [C, 2, T])
        vT = exT[:, :, :].rearrange("p a n -> p (a n)").rearrange("p (v n) -> p v n", v=2)
        bd = ex[:, :, :].rearrange("p a n -> p (a n)").rearrange("p (v b n) -> p v b n", v=2, b=NB)
        early = hm[:, 1, :, :].rearrange("p e t -> p (e t)")
        sc = early[:, 0:512].rearrange("p (v b e) -> p v b e", v=2, b=NB)
        sc2 = early[:, 512:1024].rearrange("p (v b e) -> p v b e", v=2, b=NB)
        ff = hm[:, :, :, :].rearrange("p a e t -> p (a e t)").rearrange("p (k n) -> p k n", n=4 * T)
        gated, prod, hid = ff[:, 0:2, :], ff[:, 2:4, :], ff[:, 4:7, :]

        PB = [ctx.enter_context(nc.psum_tensor(f"bank{i}", [128, 512], F32)) for i in range(8)]

        ld_x = [sem(f"ld_x{i}") for i in range(2)]
        ld_ctx = [sem(f"ld_ctx{i}") for i in range(2)]
        ld_vec = sem("ld_vec")
        ld_ctxT = sem("ld_ctxT")
        ld_attn = sem("ld_attn")
        ld_qkv = sem("ld_qkv")
        ld_o = sem("ld_o")
        ld_up = sem("ld_up")
        ld_dn = sem("ld_dn")
        c_id = sem("c_id"); c_ones = sem("c_ones"); c_pool = sem("c_pool"); pool_step = sem("pool_step")
        c_part = sem("c_part"); c_sel = sem("c_sel")
        zeroed = sem("zeroed")
        dve_step = sem("dve_step")
        ve_ready = sem("ve_ready"); rstd_ready = sem("rstd_ready")
        hn_ready = sem("hn_ready"); rhn_ready = sem("rhn_ready")
        xbp_ready = sem("xbp_ready")
        k1_used = sem("k1_used"); s_used = sem("s_used"); x1_ready = sem("x1_ready"); lg_used = sem("lg_used")
        x2_ready = sem("x2_ready"); kp_used = sem("kp_used"); x3_ready = sem("x3_ready"); xbc_ready = sem("xbc_ready")
        nmx_ready = sem("nmx_ready"); mixw_ready = sem("mixw_ready");
        k1_ready = sem("k1_ready"); sim2_ready = sem("sim2_ready"); simsum_ready = sem("simsum_ready")
        ssq_ready = sem("ssq_ready"); simr_ready = sem("simr_ready"); simn_ready = sem("simn_ready")
        egate_ready = sem("egate_ready"); vT_ready = sem("vT_ready")
        xn1_ready = sem("xn1_ready"); s_ready = sem("s_ready"); sc_ready = sem("sc_ready"); sce_ready = sem("sce_ready")
        bd_ready = sem("bd_ready"); att_ready = sem("att_ready")
        xn2_ready = sem("xn2_ready"); xn2T_ps = sem("xn2T_ps"); xn2T_ready = sem("xn2T_ready")
        lg_ps = sem("lg_ps"); gin_ready = sem("gin_ready"); gex_ready = sem("gex_ready")
        parts_ready = sem("parts_ready"); rwT_ps = sem("rwT_ps"); rwT_ready = sem("rwT_ready")
        rb_ready = sem("rb_ready"); hm_ready = sem("hm_ready"); qkv_done = sem("qkv_done")
        qk_ready = sem("qk_ready"); qkT_ps = sem("qkT_ps"); qkT_ready = sem("qkT_ready")
        s2_ps = sem("s2_ps"); s2_ready = sem("s2_ready"); p2_ready = sem("p2_ready"); pn_ready = sem("pn_ready")
        pT2_ps = sem("pT2_ps"); pT2_ready = sem("pT2_ready"); aT_ps = sem("aT_ps"); aT_ready = sem("aT_ready")
        mix_ready = sem("mix_ready"); o_ready = sem("o_ready")
        kp_ready = sem("kp_ready"); ksp_ready = sem("ksp_ready"); ksT_ps = sem("ksT_ps"); ks_ready = sem("ks_ready")
        xn3_ready = sem("xn3_ready"); xn3T_ps = sem("xn3T_ps"); xn3T_ready = sem("xn3T_ready")
        qp_ready = sem("qp_ready"); qsp_ready = sem("qsp_ready"); qsT_ps = sem("qsT_ps"); qs_ready = sem("qs_ready")
        km_ready = sem("km_ready"); vm_ready = sem("vm_ready")
        s3_ready = sem("s3_ready"); ex_in = sem("ex_in"); ex_ready = sem("ex_ready")
        exT_ps = sem("exT_ps"); exT_ready = sem("exT_ready"); pv_done = sem("pv_done")
        yT_ready = sem("yT_ready"); c_ready = sem("c_ready")
        xn4_ready = sem("xn4_ready"); xn4T_ps = sem("xn4T_ps"); xn4T_ready = sem("xn4T_ready")
        rt_ps = sem("rt_ps"); rin_ready = sem("rin_ready"); rex_ready = sem("rex_ready")
        wparts_ready = sem("wparts_ready"); wT_ps = sem("wT_ps"); wT_ready = sem("wT_ready")
        up_ready = sem("up_ready"); gated_ready = sem("gated_ready"); prod_ready = sem("prod_ready")
        hid_ready = sem("hid_ready"); down_done = sem("down_done");
        out_ready = sem("out_ready"); stored = sem("stored")

        def bs(hf):
            return slice(HALF * hf, HALF * hf + HALF)

        def head_rows(h):
            return slice(D0 * h, D0 * h + D0)

        def chunk_rows(ch):
            return min(128, RUP - 128 * ch)

        def n_routed(k):
            return NROUTED * (k // NCH) + min(k % NCH + 1, NROUTED)

        def routed_chunk(r):
            return (r - 1) // NROUTED * NCH + (r - 1) % NROUTED

        def tail(hf):
            return Q3 + 4 * (HALF * hf + HALF - 1) + 13

        def b_read(eng, k):
            if k % NCH < NROUTED:
                eng.wait_ge(prod_ready, n_routed(k))
            else:
                eng.wait_ge(hid_ready, k + 1)

        block = ctx.enter_context(nc.Block())

        @block.sync
        def _(sp):
            sp.dma_start(xr[:, bs(0), :], x_d[:, bs(0), :]).then_inc(ld_x[0], 16)
            sp.dma_start(colsim[:, :], cols_d).then_inc(ld_vec, 16)
            sp.dma_start(rowv[:, :], rows_d.partition_broadcast(128)).then_inc(ld_vec, 16)
            sp.dma_start(cx[:, bs(0), :], ctx_d[:, bs(0), :]).then_inc(ld_ctx[0], 16)
            sp.dma_start(xr[:, bs(1), :], x_d[:, bs(1), :]).then_inc(ld_x[1], 16)
            sp.dma_start(cx[:, bs(1), :], ctx_d[:, bs(1), :]).then_inc(ld_ctx[1], 16)
            sp.dma_start(cxT[:, :], ctxT_d).then_inc(ld_ctxT, 16)
            sp.dma_start(wqkv[:, :, :], wqkv_d).then_inc(ld_qkv, 16)
            sp.dma_start(wattn[:, :, :], wattn_d).then_inc(ld_attn, 16)
            sp.dma_start(wo[:, :, :], wo_d).then_inc(ld_o, 16)
            sp.dma_start(wa[:, :], wa_d).then_inc(ld_up, 16)
            sp.dma_start(wb[:, :], wb_d).then_inc(ld_up, 16)
            sp.dma_start(wg[:, :], wg_d).then_inc(ld_up, 16)
            full = RUP // 128
            sp.dma_start(wdn[:, 0:full, :], wdn_d[0:full * 128, :].rearrange("(k p) c -> p k c", p=128)).then_inc(ld_dn, 16)
            sp.dma_start(wdn[0:RUP - full * 128, full, :], wdn_d[full * 128:RUP, :]).then_inc(ld_dn, 16)
            for hf in range(2):
                sp.wait_ge(out_ready, hf + 1)
                sp.dma_start(out_d[:, bs(hf), :], xr[:, bs(hf), :]).then_inc(stored, 16)
            sp.wait_ge(stored, 32)

        @block.gpsimd
        def _(pool):
            steps = [0]

            def link(ins):
                steps[0] += 1
                ins.then_inc(pool_step, 1)
                pool.wait_ge(pool_step, steps[0])

            link(nc.gpsimd.memset(ident[:, :], 0.0))
            nc.gpsimd.affine_select(out=ident[:, :], in_=ident[:, :], compare_op=ALU.not_equal, fill=1.0, base=0,
                                    pattern=[[-1, 128]], channel_multiplier=1).then_inc(c_id, 1)
            nc.gpsimd.memset(m16[:, :], -0.5).then_inc(c_pool, 1)
            nc.gpsimd.iota(orderi[:, :], [[-1, E0]], base=E0, channel_multiplier=0).then_inc(c_pool, 1)

            def power(dst, src, signal):
                nc.gpsimd.tensor_tensor(dst, src, m16[:, 0:src.shape[1]], ALU.pow).then_inc(signal, 1)

            def rstd_of(n, k, b0, b1):
                pool.wait_ge(ve_ready, n)
                power(rstd[:, k, b0:b1], ve[:, k, b0:b1], rstd_ready)

            pool.wait_ge(c_pool, 2)
            rstd_of(1, 0, 0, HALF)
            rstd_of(2, 0, HALF, NB)
            nc.gpsimd.memset(ex[:, :, :], 0.0).then_inc(zeroed, 1)
            pool.wait_ge(ssq_ready, 1)
            power(sim2[:, :], sim2[:, :], simr_ready)
            pool.wait_ge(ld_vec, 16 * 6)
            for hf in range(2):
                pool.wait_ge(xn1_ready, hf + 1)
                nc.gpsimd.tensor_tensor(xr[:, bs(hf), :], xr[:, bs(hf), :], bc(rows[:, R_BP, :], 1, HALF), ALU.add).then_inc(xbp_ready, 1)
            nc.gpsimd.memset(parts[:, :, :], 0.0).then_inc(zeroed, 1)
            for hf in range(2):
                rstd_of(3 + hf, 1, HALF * hf, HALF * hf + HALF)
            pool.wait_ge(hn_ready, 1)
            power(rhn[:, :], hn[:, :], rhn_ready)
            link(nc.gpsimd.memset(causal[:, :], 0.0))
            nc.gpsimd.affine_select(out=causal[:, :], in_=causal[:, :], compare_op=ALU.is_ge, fill=NEG, base=0,
                                    pattern=[[-1, T]], channel_multiplier=1).then_inc(c_pool, 1)
            nc.gpsimd.memset(wparts[:, :, :], 0.0).then_inc(zeroed, 1)
            link(nc.gpsimd.memset(vm[:, :, :, :], 0.0))
            for p in range(2):
                for g in range(2):
                    ins = nc.gpsimd.memset(diag(vm[:, p, 8 * g:8 * g + 8, :], 64), 1.0)
            link(ins)

            def fill_vm(b):
                if b >= 2:
                    pool.wait_ge(pv_done, 4 * (b - 1))
                for g in range(2):
                    ins = nc.gpsimd.tensor_copy(diag(vm[:, b % 2, 8 * g:8 * g + 8, :], 0),
                                                cx[:, b, 64 * g:64 * g + 64].rearrange("p (h i) -> p h i", i=D1))
                ins.then_inc(vm_ready, 1)

            def mask_k(b):
                pool.wait_ge(ks_ready, b + 1)
                if b >= 2:
                    pool.wait_ge(s3_ready, 4 * (b - 1))
                for g in range(4):
                    ins = nc.gpsimd.tensor_tensor(km[:, b % 2, g, :, :], bc(ks[:, b, g, :].bitcast(F32), 1, 4),
                                                  bc(hmask[:, :], 2, T), ALU.mult)
                ins.then_inc(km_ready, 1)

            def add_bc(b):
                pool.wait_ge(xn3_ready, b + 1)
                nc.gpsimd.tensor_tensor(xr[:, b, :], xr[:, b, :], rows[:, R_BC, :], ALU.add).then_inc(xbc_ready, 1)

            pool.wait_ge(ld_ctx[0], 16)
            pool.wait_ge(ld_ctx[1], 16)
            pool.wait_ge(c_part, 1)
            for b in range(NB):
                rstd_of(5 + b, 2, b, b + 1)
                add_bc(b)
                if b in (2, 4):
                    fill_vm(b // 2 - 1)
                    mask_k(b // 2 - 1)
                if b == 6:
                    mask_k(2)
            for b in range(NB):
                if b + 3 < NB:
                    mask_k(b + 3)
                if b + 2 < NB:
                    fill_vm(b + 2)
                rstd_of(5 + NB + b, 3, b, b + 1)

        @block.scalar
        def _(act):
            for h in range(H0):
                act.dma_start(kv[head_rows(h), :, :].rearrange("p v e -> p (v e)"), kv_d[h, :].partition_broadcast(D0)).then_inc(ld_vec, 16)
            act.wait_ge(ld_vec, 16 * 6)
            nc.scalar.activation(sgate[:, :], gates[:, :], ACT.Exp, scale=-1.0).then_inc(egate_ready, 1)
            act.wait_ge(ld_ctxT, 16)
            for v, (w, b) in enumerate(((WVG, BVG), (WVL, BVL))):
                nc.scalar.activation(vT[:, v, :], cxT[:, :], ACT.Identity, bias=cols[:, b:b + 1],
                                     scale=cols[:, w:w + 1]).then_inc(vT_ready, 1)
            act.wait_ge(sc_ready, 1)
            nc.scalar.activation(sc2, sc, ACT.Exp, scale=S0_SCALE).then_inc(sce_ready, 1)
            act.wait_ge(c_part, 1)
            nc.scalar.activation(identb[:, :], ident[:, :], ACT.Copy)
            nc.scalar.activation(sel[:, :, :], bc(part16[:, :], 2, 128), ACT.Copy).then_inc(c_sel, 1)
            for hf in range(2):
                act.wait_ge(xn2T_ps, hf + 1)
                nc.scalar.activation(xn2T[:, bs(hf), :].rearrange("p b t -> p (b t)"), PB[6 + hf][:, :], ACT.Copy).then_inc(xn2T_ready, 1)
            act.wait_ge(gin_ready, 1)
            nc.scalar.activation(gex[:, :, :], gin[:, :, :], ACT.Exp).then_inc(gex_ready, 1)
            for hf in range(2):
                act.wait_ge(rwT_ps, hf + 1)
                nc.scalar.activation(rwT[:, bs(hf), :].rearrange("p b t -> p (b t)"), PB[2 + hf][:, 0:256].bitcast(BF16), ACT.Copy).then_inc(rwT_ready, 1)
            nc.scalar.activation(sel2[:, :, :, :].rearrange("p r j d -> p (r j) d"), bc(part16[:, :], 2, HD), ACT.Copy)
            nc.scalar.activation(selw[:, :, :], bc(part8[:, :], 2, HID), ACT.Copy).then_inc(c_sel, 1)

            def take_qkv(b):
                act.wait_ge(qkv_done, 4 * b + 4)
                if b >= 2:
                    act.wait_ge(aT_ps, b - 1)
                bank = PB[0 if b % 2 == 0 else 2]
                nc.scalar.activation(qk[:, b % 2, :], bank[:, 0:2 * HD], ACT.Copy)
                nc.scalar.activation(v2[:, b % 2, :, :], bc(bank[:, 2 * HD:3 * HD], 1, 2), ACT.Copy).then_inc(qk_ready, 1)

            def take_qkT(b):
                act.wait_ge(qkT_ps, b + 1)
                if b >= 2:
                    act.wait_ge(s2_ps, b - 1)
                nc.scalar.activation(qkT[:, b % 2, :, :].rearrange("p a t -> p (a t)"), PB[1][0:HD, 0:2 * T], ACT.Copy).then_inc(qkT_ready, 1)

            def exp2(b):
                act.wait_ge(s2_ready, b + 1)
                act.wait_ge(nmx_ready, b + 1)
                if b >= 2:
                    act.wait_ge(pT2_ps, b - 1)
                nc.scalar.activation(pn[:, b % 2, :], s2[:, b % 2, :], ACT.Exp, bias=nmx2[:, b:b + 1], scale=A_SCALE,
                                     accum_out=den2[:, b:b + 1]).then_inc(p2_ready, 1)

            def take_pT(b):
                act.wait_ge(pT2_ps, b + 1)
                if b >= 2:
                    act.wait_ge(aT_ps, b - 1)
                nc.scalar.activation(pT2[:, b % 2, :], PB[3][:, 0:T], ACT.Copy).then_inc(pT2_ready, 1)

            def take_aT(b):
                act.wait_ge(aT_ps, b + 1)
                if b >= 2:
                    act.wait_ge(mix_ready, 2 * (b - 1))
                nc.scalar.activation(aT[:, b % 2, :], PB[3][:, 0:T], ACT.Copy).then_inc(aT_ready, 1)

            def take_ks(b):
                act.wait_ge(ksT_ps, b + 1)
                nc.scalar.activation(ks[:, b, :, :].rearrange("p g t -> p (g t)"), PB[1][:, :], ACT.Copy).then_inc(ks_ready, 1)

            def take_xn3T(b):
                act.wait_ge(xn3T_ps, b + 1)
                if b >= 1:
                    act.wait_ge(qp_ready, b)
                nc.scalar.activation(xn3T[:, :], PB[7][:, 0:T], ACT.Copy).then_inc(xn3T_ready, 1)

            def take_qs(b):
                act.wait_ge(qsT_ps, b + 1)
                nc.scalar.activation(qs[:, b, :, :].rearrange("p g t -> p (g t)"), PB[7][:, :], ACT.Copy).then_inc(qs_ready, 1)

            def exp3(u):
                act.wait_ge(ex_in, u + 1)
                nc.scalar.activation(ex[:, u % 4, :], ex[:, u % 4, :], ACT.Exp, scale=S1_SCALE).then_inc(ex_ready, 1)

            def take_exT(v):
                act.wait_ge(exT_ps, v + 1)
                if v >= 4:
                    act.wait_ge(pv_done, v - 3)
                nc.scalar.activation(exT[:, v % 4, :], PB[1 if v % 2 == 0 else 3][:, :], ACT.Copy).then_inc(exT_ready, 1)

            def take_xn4T(hf):
                act.wait_ge(xn4T_ps, hf + 1)
                nc.scalar.activation(xn4T[:, 512 * hf:512 * hf + 512], PB[5][:, :], ACT.Copy).then_inc(xn4T_ready, 1)

            def router_exp(hf):
                act.wait_ge(rin_ready, hf + 1)
                nc.scalar.activation(gex[:, 0:HALF, 0:E1], gin[:, 0:HALF, 0:E1], ACT.Exp).then_inc(rex_ready, 1)

            def take_wT(hf):
                act.wait_ge(wT_ps, hf + 1)
                nc.scalar.activation(wT[:, 512 * hf:512 * hf + 512], PB[5][:, 0:256].bitcast(BF16), ACT.Copy).then_inc(wT_ready, 1)

            def silu(k):
                act.wait_ge(up_ready, k + 1)
                if k >= 2:
                    b_read(act, k - 2)
                n = chunk_rows(k % NCH)
                nc.scalar.activation(gated[0:n, k % 2, :], PB[0 if k % 2 == 0 else 2][0:n, :], ACT.Silu).then_inc(gated_ready, 1)

            for s in range(LAST):
                for b in range(NB):
                    if s == 4 * b + 4:
                        take_qkv(b)
                    if s == 4 * b + 5:
                        take_qkT(b)
                    if s == 4 * b + 7:
                        exp2(b)
                    if s == 4 * b + 8:
                        take_ks(b)
                    if s == 4 * b + 9:
                        take_pT(b)
                    if s == 4 * b + 10:
                        take_aT(b)
                    if s == 4 * b + 16:
                        take_xn3T(b)
                    if s == 4 * b + 19:
                        take_qs(b)
                if 0 <= s - Q3 - 3 < 4 * NB:
                    take_exT(s - Q3 - 3)
                if 0 <= s - Q3 < 4 * NB:
                    exp3(s - Q3)
                for hf in range(2):
                    if s == tail(hf):
                        take_xn4T(hf)
                    if s == tail(hf) + 2:
                        router_exp(hf)
                    if s == tail(hf) + 4:
                        take_wT(hf)
                if 0 <= s - F4 < 2 * NCH:
                    silu(s - F4)

        @block.vector
        def _(dve):
            steps = [0]

            def link(ins):
                steps[0] += 1
                ins.then_inc(dve_step, 1)
                dve.wait_ge(dve_step, steps[0])

            V = nc.vector

            def stats(k, b0, b1):
                for b in range(b0, b1):
                    ins = V.bn_stats(st[:, k, b, :], xr[:, b, :])
                link(ins)
                for b in range(b0, b1):
                    ins = V.bn_aggr(mv[:, k, b, :], st[:, k, b, :])
                link(ins)
                V.tensor_scalar(ve[:, k, b0:b1], mv[:, k, b0:b1, 1], EPS, None, ALU.add).then_inc(ve_ready, 1)

            def normalise(dst, k, b0, b1, n, signal):
                dve.wait_ge(rstd_ready, n)
                for b in range(b0, b1):
                    ins = V.tensor_scalar(dst[:, b, :], xr[:, b, :], mv[:, k, b, 0:1], rstd[:, k, b:b + 1],
                                          ALU.subtract, ALU.mult)
                ins.then_inc(signal, 1)

            def first_of_max(f, l, vi, ti, e, n, w):
                link(V.tensor_reduce(gv[:, vi, 0:n], l, AX.X, ALU.max))
                link(V.tensor_tensor(ga[:, 0:n, 0:e], l, bc(gv[:, vi, 0:n], 2, e), ALU.is_equal))
                link(V.tensor_tensor(ga[:, 0:n, 0:e], ga[:, 0:n, 0:e], bc(w, 1, n), ALU.mult))
                link(V.tensor_reduce(gv[:, ti, 0:n], ga[:, 0:n, 0:e], AX.X, ALU.max))
                link(V.tensor_tensor(f, ga[:, 0:n, 0:e], bc(gv[:, ti, 0:n], 2, e), ALU.is_equal))

            def two_best(e, n):
                l, a, b = lg[:, 0:n, 0:e], f1[:, 0:n, 0:e], f2[:, 0:n, 0:e]
                w = order[:, E0 - e:E0]
                first_of_max(a, l, 0, 1, e, n, w)
                link(V.scalar_tensor_tensor(out=gin[:, 0:n, 0:e], in0=a, scalar=-1e30, in1=l, op0=ALU.mult, op1=ALU.add))
                first_of_max(b, gin[:, 0:n, 0:e], 2, 3, e, n, w)
                link(V.tensor_tensor(f1[:, 0:n, 0:e], a, b, ALU.add))

            def weigh(e, n, mask, into, b0):
                p = rw[:, 0:n, 0:e]
                link(V.tensor_tensor(p, gex[:, 0:n, 0:e], mask, ALU.mult))
                link(V.tensor_reduce(gv[:, 4, 0:n], p, AX.X, ALU.add))
                link(V.reciprocal(gv[:, 5, 0:n], gv[:, 4, 0:n]))
                link(V.tensor_tensor(p, p, bc(gv[:, 5, 0:n], 2, e), ALU.mult))
                for j in range(3):
                    part = into[:, b0:b0 + n, j * e:j * e + e]
                    ins = V.tensor_copy(part, p)
                    if j < 2:
                        link(ins)
                        link(V.tensor_tensor(p, p, part, ALU.subtract))
                return ins

            link(V.memset(ones[:, :], 1.0))
            c_ones_done = V.memset(wp2[:, :], 0.0)
            c_ones_done.then_inc(c_ones, 1)
            dve.wait_ge(ld_x[0], 16)
            stats(0, 0, HALF)
            dve.wait_ge(ld_x[1], 16)
            stats(0, HALF, NB)
            dve.wait_ge(c_id, 1)
            V.tensor_reduce(part16[:, :], ident[:, 0:3 * E0].rearrange("p (m e) -> p e m", m=3), AX.X, ALU.add)
            V.tensor_reduce(part8[:, :], ident[:, 0:3 * E1].rearrange("p (m e) -> p e m", m=3), AX.X, ALU.add)
            V.tensor_reduce(hmask[:, :], ident[:, :].rearrange("p (g j i) -> p j g i", g=4, j=4), AX.XY, ALU.add).then_inc(c_part, 1)
            normalise(xna, 0, 0, HALF, 1, xn1_ready)
            normalise(xna, 0, HALF, NB, 2, xn1_ready)
            dve.wait_ge(c_pool, 2)
            V.tensor_copy(order[:, :], orderi[:, :])
            dve.wait_ge(ld_vec, 16 * 6)
            dve.wait_ge(c_ones, 1)
            V.tensor_scalar(wp2[:, :], cols[:, WP:WP + 1], 2.0, None, ALU.mult)
            V.tensor_scalar(kb[:, 0, :], kv[:, 1, :], float(T), None, ALU.mult)
            V.tensor_scalar(kb[:, 1, :], kv[:, 3, :], float(T), None, ALU.mult)
            V.tensor_tensor(sim2[:, :], sim, sim, ALU.mult).then_inc(sim2_ready, 1)
            dve.wait_ge(k1_ready, 1)
            dve.wait_ge(sim2_ready, 1)
            for v in range(2):
                ins = V.tensor_tensor(kw[:, v, :, :], PB[2][:, 0:NB * D0].rearrange("p (b e) -> p b e", e=D0),
                                      bc(kv[:, 2 * v, :], 1, NB), ALU.mult)
            ins.then_inc(k1_used, 1)
            dve.wait_ge(k1_used, 1)
            for v in range(2):
                ins = V.tensor_tensor(kw[:, v, :, :], kw[:, v, :, :], bc(kb[:, v, :], 1, NB), ALU.add)
            link(ins)
            for v, q in enumerate((BQG, BQL)):
                V.tensor_scalar(kw[:, v, :, :], kw[:, v, :, :], cols[:, q:q + 1], None, ALU.mult)
            dve.wait_ge(simsum_ready, 1)
            V.tensor_scalar(sim2[:, :], PB[3][:, 0:E0], 1e-24, None, ALU.max).then_inc(ssq_ready, 1)
            dve.wait_ge(egate_ready, 1)
            link(V.tensor_scalar(sgate[:, :], sgate[:, :], 1.0, None, ALU.add))
            V.reciprocal(sgate[:, :], sgate[:, :])

            def unit_sim():
                dve.wait_ge(simr_ready, 1)
                V.tensor_tensor(simn[:, :], sim, sim2[:, :], ALU.mult).then_inc(simn_ready, 1)


            dve.wait_ge(s_ready, 2)
            qk_sum = PB[0][:, 0:NB * D0].rearrange("p (b e) -> p b e", e=D0)
            q_sum = PB[0][:, NB * D0:NB * D0 + NB]
            for v in range(2):
                V.tensor_tensor(sc[:, v, :, :], qk_sum, bc(kv[:, 2 * v, :], 1, NB), ALU.mult)
            for v in range(2):
                ins = V.tensor_tensor(sc2[:, v, :, :], bc(q_sum, 2, D0), bc(kv[:, 2 * v + 1, :], 1, NB), ALU.mult)
            ins.then_inc(s_used, 1)
            dve.wait_ge(s_used, 1)
            link(V.tensor_tensor(sc, sc, sc2, ALU.add))
            for v, q in enumerate((WQG, WQL)):
                ins = V.scalar_tensor_tensor(out=sc[:, v, :, :], in0=sc[:, v, :, :], scalar=cols[:, q:q + 1],
                                             in1=kw[:, v, :, :], op0=ALU.mult, op1=ALU.add)
            link(ins)
            w = sc.rearrange("p v b e -> p (v b) e")
            e = sc2.rearrange("p v b e -> p (v b) e")
            link(V.tensor_reduce(cm[:, :], w, AX.X, ALU.max))
            V.tensor_tensor(w, w, bc(cm[:, :], 2, D0), ALU.subtract).then_inc(sc_ready, 1)
            dve.wait_ge(zeroed, 1)
            dve.wait_ge(sce_ready, 1)
            link(V.tensor_reduce(cs[:, :], e, AX.X, ALU.add))
            link(V.reciprocal(cs[:, :], cs[:, :]))
            link(V.scalar_tensor_tensor(out=w, in0=e, scalar=wp2[:, 0:1], in1=bc(cs[:, :], 2, D0), op0=ALU.mult, op1=ALU.mult))
            for h in range(H0):
                r = head_rows(h)
                ins = V.transpose(bd[r, :, :, r].rearrange("p v b e -> p (v b) e"), w[r, :, :])
            ins.then_inc(bd_ready, 1)

            unit_sim()
            for hf in range(2):
                dve.wait_ge(att_ready, hf + 1)
                dve.wait_ge(xbp_ready, hf + 1)
                x = xr[:, bs(hf), :].rearrange("p b c -> p (b c)")
                V.tensor_tensor(x, x, PB[4 + hf][:, :], ALU.add).then_inc(x1_ready, 1)
                dve.wait_ge(x1_ready, hf + 1)
                stats(1, HALF * hf, HALF * hf + HALF)
            for hf in range(2):
                normalise(xnb, 1, HALF * hf, HALF * hf + HALF, 3 + hf, xn2_ready)
            link(V.tensor_tensor(hn[:, :], rstd[:, 1, :], rstd[:, 1, :], ALU.mult))
            link(V.scalar_tensor_tensor(out=hn[:, :], in0=hn[:, :], scalar=float(C), in1=mv[:, 1, :, 1], op0=ALU.mult, op1=ALU.mult))
            V.tensor_scalar(hn[:, :], hn[:, :], 1e-24, None, ALU.max).then_inc(hn_ready, 1)

            dve.wait_ge(lg_ps, 1)
            dve.wait_ge(rhn_ready, 1)
            V.tensor_tensor(lg[:, :, :], PB[1][:, 0:NB * E0].rearrange("p (b e) -> p b e", e=E0),
                            bc(rhn[:, :], 2, E0), ALU.mult).then_inc(lg_used, 1)
            dve.wait_ge(lg_used, 1)
            link(V.tensor_tensor(lg[:, :, :], lg[:, :, :], bc(sgate[:, :], 1, NB), ALU.subtract))
            two_best(E0, NB)
            link(V.tensor_scalar(gv[:, 1, :], gv[:, 0, :], 0.0, None, ALU.is_le))
            link(V.tensor_tensor(f1[:, :, :], f1[:, :, :], bc(gv[:, 1, :], 2, E0), ALU.mult))
            link(V.scalar_tensor_tensor(out=f2[:, :, :], in0=lg[:, :, :], scalar=0.0, in1=f1[:, :, :], op0=ALU.is_gt, op1=ALU.max))
            link(V.tensor_scalar(gv[:, 0, :], gv[:, 0, :], 0.0, None, ALU.max))
            V.scalar_tensor_tensor(out=gin[:, :, :], in0=lg[:, :, :], scalar=0.0, in1=bc(gv[:, 0, :], 2, E0),
                                   op0=ALU.max, op1=ALU.subtract).then_inc(gin_ready, 1)
            dve.wait_ge(zeroed, 2)
            dve.wait_ge(gex_ready, 1)
            weigh(E0, NB, f2[:, :, :], parts, 0).then_inc(parts_ready, 1)

            def scale_hidden(i):
                b, q = i // 4, i % 4
                dve.wait_ge(rb_ready, i + 1)
                if i >= 8:
                    dve.wait_ge(qkv_done, i - 7)
                V.tensor_tensor(hm[:, b % 2, 4 * q:4 * q + 4, :], bc(xn2T[:, b, :], 1, 4),
                                PB[4 if i % 2 == 0 else 6][:, :].rearrange("p (e t) -> p e t", e=4), ALU.mult).then_inc(hm_ready, 1)

            def split(src, dst, hi, lo):
                s4 = bc(src[:, :].rearrange("p (g c) -> p g c", g=4), 2, 2)
                link(V.tensor_copy(dst[:, :, hi, :].bitcast(F32R), s4))
                return V.tensor_tensor(dst[:, :, lo, :], s4, dst[:, :, hi, :], ALU.subtract)

            def split_k(b):
                dve.wait_ge(kp_ready, b + 1)
                V.tensor_tensor(kf[:, :], PB[3][:, 0:C], rows[:, R_BK, :], ALU.add).then_inc(kp_used, 1)
                dve.wait_ge(kp_used, b + 1)
                if b >= 1:
                    dve.wait_ge(ksT_ps, b)
                split(kf, ksp, slice(0, 4, 2), slice(1, 4, 2)).then_inc(ksp_ready, 1)

            def split_q(b):
                dve.wait_ge(qp_ready, b + 1)
                if b >= 1:
                    dve.wait_ge(qsT_ps, b)
                link(V.tensor_tensor(qf[:, :], PB[7][:, 0:C], rows[:, R_BQ, :], ALU.add))
                split(qf, qsp, slice(0, 2), slice(2, 4)).then_inc(qsp_ready, 1)

            def softmax2_max(b):
                dve.wait_ge(s2_ps, b + 1)
                V.tensor_tensor_reduce(s2[:, b % 2, :], PB[1][:, 0:T], causal[:, :], 1.0, NEG, ALU.add, ALU.max,
                                       mx2[:, b:b + 1]).then_inc(s2_ready, 1)
                dve.wait_ge(s2_ready, b + 1)
                V.tensor_scalar(nmx2[:, b:b + 1], mx2[:, b:b + 1], -A_SCALE, None, ALU.mult).then_inc(nmx_ready, 1)

            def softmax2_norm(b):
                dve.wait_ge(p2_ready, b + 1)
                link(V.reciprocal(rden2[:, b:b + 1], den2[:, b:b + 1]))
                V.tensor_scalar(pn[:, b % 2, :], pn[:, b % 2, :], rden2[:, b:b + 1], None, ALU.mult).then_inc(pn_ready, 1)

            def mix(b, i):
                dve.wait_ge(mixw_ready, 2 * b + i + 1)
                dve.wait_ge(aT_ready, b + 1)
                if b >= 1:
                    dve.wait_ge(o_ready, b)
                V.tensor_tensor(mixT[:, 4 * i:4 * i + 4, :], bc(aT[:, b % 2, :], 1, 4),
                                PB[5][:, :].rearrange("p (r t) -> p r t", r=4), ALU.mult).then_inc(mix_ready, 1)

            def after_mixture(b):
                dve.wait_ge(o_ready, b + 1)
                V.tensor_tensor(xr[:, b, :], xr[:, b, :], PB[5][:, 0:C], ALU.add).then_inc(x2_ready, 1)
                dve.wait_ge(x2_ready, b + 1)
                stats(2, b, b + 1)

            def softmax3(u):
                b, g = u // 4, u % 4
                bank = PB[0 if u % 2 == 0 else 2][:, :].rearrange("p (j k) -> p j k", j=4)
                dve.wait_ge(s3_ready, u + 1)
                link(V.tensor_reduce(mx3[:, u % 8, :], bank, AX.X, ALU.max))
                if u >= 4:
                    dve.wait_ge(exT_ps, u - 3)
                V.tensor_tensor(ex[:, u % 4, :].rearrange("p (j k) -> p j k", j=4), bank, bc(mx3[:, u % 8, :], 2, T),
                                ALU.subtract).then_inc(ex_in, 1)

            def divide(b):
                dve.wait_ge(pv_done, 4 * b + 4)
                bank = PB[4][:, 0:2 * T]
                link(V.reciprocal(ry[:, :, :].rearrange("p g t -> p (g t)"), bank[64:128, :]))
                if b >= 2:
                    dve.wait_ge(c_ready, b - 1)
                for g in range(2):
                    ins = V.tensor_tensor(yT[64 * g:64 * g + 64, b % 2, :], ry[:, g, :], bank[0:64, T * g:T * g + T], ALU.mult)
                ins.then_inc(yT_ready, 1)

            def after_attention(b):
                dve.wait_ge(c_ready, b + 1)
                dve.wait_ge(xbc_ready, b + 1)
                V.tensor_tensor(xr[:, b, :], xr[:, b, :], PB[6][:, 0:C], ALU.add).then_inc(x3_ready, 1)
                dve.wait_ge(x3_ready, b + 1)
                stats(3, b, b + 1)

            def route(hf):
                dve.wait_ge(rt_ps, hf + 1)
                link(V.tensor_copy(lg[:, 0:HALF, 0:E1], PB[5][:, 0:HALF * E1].rearrange("p (b e) -> p b e", e=E1)))
                two_best(E1, HALF)
                V.tensor_tensor(gin[:, 0:HALF, 0:E1], lg[:, 0:HALF, 0:E1], bc(gv[:, 0, 0:HALF], 2, E1), ALU.subtract).then_inc(rin_ready, 1)

            def route_weights(hf):
                dve.wait_ge(zeroed, 3)
                dve.wait_ge(rex_ready, hf + 1)
                weigh(E1, HALF, f1[:, 0:HALF, 0:E1], wparts, HALF * hf).then_inc(wparts_ready, 1)

            def hidden(k):
                ch = k % NCH
                n = chunk_rows(ch)
                bank = PB[7 if k % 2 == 0 else 1][0:n, :]
                dve.wait_ge(gated_ready, k + 1)
                if k >= 3:
                    dve.wait_ge(down_done, k - 2)
                if ch >= NROUTED:
                    V.tensor_tensor(hid[0:n, k % 3, :], gated[0:n, k % 2, :], bank, ALU.mult).then_inc(hid_ready, 1)
                    return
                if k >= 2:
                    dve.wait_ge(hid_ready, k - 1)
                V.tensor_tensor(prod[:, k % 2, :], gated[:, k % 2, :], bank, ALU.mult).then_inc(prod_ready, 1)
                dve.wait_ge(prod_ready, n_routed(k))
                V.tensor_tensor(hid[:, k % 3, :], prod[:, k % 2, :], PB[3 if n_routed(k) % 2 == 1 else 4][:, :], ALU.mult).then_inc(hid_ready, 1)

            def result(hf):
                dve.wait_ge(down_done, NCH * (hf + 1))
                x = xr[:, bs(hf), :].rearrange("p b c -> p (b c)")
                V.tensor_tensor(x, x, PB[6][:, :], ALU.add).then_inc(out_ready, 1)

            scale_hidden(0)
            scale_hidden(1)
            dve.wait_ge(c_pool, 3)
            for s in range(LAST):
                for b in range(NB):
                    if s == 4 * b + 7:
                        softmax2_max(b)
                    if s == 4 * b + 8:
                        softmax2_norm(b)
                    if s == 4 * b + 11:
                        mix(b, 0)
                    if s == 4 * b + 12:
                        mix(b, 1)
                    if s == 4 * b + 14:
                        after_mixture(b)
                    if s == 4 * b + 15:
                        normalise(xna, 2, b, b + 1, 5 + b, xn3_ready)
                    if s == 4 * b + 18:
                        split_q(b)
                    if s == 4 * b + 4:
                        split_k(b)
                if s + 2 < 4 * NB:
                    scale_hidden(s + 2)
                for b in range(NB):
                    if s == Q3 + 4 * b + 8:
                        divide(b)
                    if s == Q3 + 4 * b + 10:
                        after_attention(b)
                    if s == Q3 + 4 * b + 12:
                        normalise(xnb, 3, b, b + 1, 5 + NB + b, xn4_ready)
                if 0 <= s - Q3 < 4 * NB:
                    softmax3(s - Q3)
                for hf in range(2):
                    if s == tail(hf) + 2:
                        route(hf)
                    if s == tail(hf) + 3:
                        route_weights(hf)
                if 0 <= s - F4 < 2 * NCH:
                    hidden(s - F4)
                if s - F4 in (NCH + 2, 2 * NCH + 2):
                    result(0 if s - F4 == NCH + 2 else 1)

        @block.tensor
        def _(pe):
            mm = nc.tensor.matmul
            tr = nc.tensor.transpose
            pe.wait_ge(c_ones, 1)
            for hf in range(2):
                pe.wait_ge(xn1_ready, hf + 1)
                pe.wait_ge(ld_ctx[hf], 16)
                for b in range(HALF * hf, HALF * hf + HALF):
                    for h in range(H0):
                        r = head_rows(h)
                        mm(PB[0][r, D0 * b:D0 * b + D0], xna[:, b, r], cx[:, b, r], start=True, stop=True)
                        last = mm(PB[0][r, NB * D0 + b:NB * D0 + b + 1], xna[:, b, r], ones[:, 0:1], start=True, stop=True)
                last.then_inc(s_ready, 1)
                if hf == 0:
                    pe.wait_ge(ld_ctx[1], 16)
                    for b in range(NB):
                        for h in range(H0):
                            r = head_rows(h)
                            last = mm(PB[2][r, D0 * b:D0 * b + D0], ones[:, 0:D0], cx[:, b, r], start=True, stop=True)
                    last.then_inc(k1_ready, 1)
            pe.wait_ge(sim2_ready, 1)
            mm(PB[3][:, 0:E0], ones[:, :], sim2[:, :], start=True, stop=True).then_inc(simsum_ready, 1)
            pe.wait_ge(vT_ready, 2)
            pe.wait_ge(bd_ready, 1)
            for hf in range(2):
                for i in range(HALF):
                    b = HALF * hf + i
                    for v in range(2):
                        last = mm(PB[4 + hf][:, C * i:C * i + C], vT[:, v, T * b:T * b + T], bd[:, v, b, :],
                                  start=(v == 0), stop=(v == 1))
                last.then_inc(att_ready, 1)
            for hf in range(2):
                pe.wait_ge(xn2_ready, hf + 1)
                for i in range(HALF):
                    last = tr(PB[6 + hf][:, T * i:T * i + T], xnb[:, HALF * hf + i, :], ident[:, :])
                last.then_inc(xn2T_ps, 1)
            pe.wait_ge(simn_ready, 1)
            for hf in range(2):
                pe.wait_ge(xn2T_ready, hf + 1)
                for b in range(HALF * hf, HALF * hf + HALF):
                    last = mm(PB[1][:, E0 * b:E0 * b + E0], xn2T[:, b, :], simn[:, :], start=True, stop=True)
            last.then_inc(lg_ps, 1)
            pe.wait_ge(c_sel, 1)
            pe.wait_ge(parts_ready, 1)
            for hf in range(2):
                for i in range(HALF):
                    last = tr(PB[2 + hf][:, 0:256].bitcast(BF16)[:, T * i:T * i + T], parts[:, HALF * hf + i, :], identb[:, :])
                last.then_inc(rwT_ps, 1)

            def spread(i):
                b, q = i // 4, i % 4
                pe.wait_ge(rwT_ready, b // HALF + 1)
                if i == 0:
                    pe.wait_ge(x1_ready, 1)
                if i == 1:
                    pe.wait_ge(xn2T_ready, 1)
                if i >= 2:
                    pe.wait_ge(hm_ready, i - 1)
                for e in range(4):
                    last = mm(PB[4 if i % 2 == 0 else 6][:, T * e:T * e + T], sel[:, 4 * q + e, :], rwT[:, b, :],
                              start=True, stop=True)
                last.then_inc(rb_ready, 1)

            def project(i):
                b, q = i // 4, i % 4
                bank = PB[0 if b % 2 == 0 else 2]
                pe.wait_ge(hm_ready, i + 1)
                if i == 0:
                    pe.wait_ge(ld_qkv, 16)
                    pe.wait_ge(s_used, 1)
                if i == 4:
                    pe.wait_ge(rwT_ready, 1)
                if q == 0 and b >= 2:
                    pe.wait_ge(qk_ready, b - 1)
                for e in range(4 * q, 4 * q + 4):
                    last = mm(bank[:, 0:3 * HD], hm[:, b % 2, e, :], wqkv[:, e, :], start=(e == 0), stop=(e == E0 - 1))
                last.then_inc(qkv_done, 1)

            def turn_qk(b):
                pe.wait_ge(ks_ready, b) if b >= 1 else pe.wait_ge(lg_used, 1)
                pe.wait_ge(qk_ready, b + 1)
                tr(PB[1][0:HD, 0:T], qk[:, b % 2, 0:HD], ident[:, :])
                tr(PB[1][0:HD, T:2 * T], qk[:, b % 2, HD:2 * HD], ident[:, :]).then_inc(qkT_ps, 1)

            def scores2(b):
                pe.wait_ge(qkT_ready, b + 1)
                mm(PB[1][:, 0:T], qkT[:, b % 2, 0, :], qkT[:, b % 2, 1, :], start=True, stop=True).then_inc(s2_ps, 1)

            def turn_p(b):
                pe.wait_ge(kp_used, b + 2) if b + 1 < NB else pe.wait_ge(aT_ready, b)
                pe.wait_ge(pn_ready, b + 1)
                tr(PB[3][:, 0:T], pn[:, b % 2, :], ident[:, :]).then_inc(pT2_ps, 1)

            def attend2(b):
                pe.wait_ge(pT2_ready, b + 1)
                mm(PB[3][:, 0:T], v2[:, b % 2, :, :].rearrange("p j d -> p (j d)"), pT2[:, b % 2, :], start=True, stop=True).then_inc(aT_ps, 1)

            def project_k(b):
                if b == 0:
                    pe.wait_ge(ld_attn, 16)
                    pe.wait_ge(rwT_ready, 2)
                if b == 1:
                    pe.wait_ge(kp_used, 1)
                if b >= 2:
                    pe.wait_ge(aT_ready, b - 1)
                mm(PB[3][:, 0:C], cxT[:, T * b:T * b + T], wattn[:, 0, :], start=True, stop=True).then_inc(kp_ready, 1)

            def turn_k(b):
                pe.wait_ge(s2_ready, b + 1)
                pe.wait_ge(ksp_ready, b + 1)
                for g in range(4):
                    last = tr(PB[1][:, T * g:T * g + T], ksp[:, g, :, :].rearrange("p a c -> p (a c)"), ident[:, :])
                last.then_inc(ksT_ps, 1)

            def spread_pairs(b, i):
                if i == 0:
                    pe.wait_ge(c_sel, 2)
                    pe.wait_ge(x2_ready, b) if b >= 1 else pe.wait_ge(x1_ready, 2)
                if i == 1:
                    pe.wait_ge(mix_ready, 2 * b + 1)
                for r in range(4):
                    last = mm(PB[5][:, T * r:T * r + T], sel2[:, 4 * i + r, :, :].rearrange("p j d -> p (j d)"), rwT[:, b, :],
                              start=True, stop=True)
                last.then_inc(mixw_ready, 1)

            def project_o(b):
                if b == 0:
                    pe.wait_ge(ld_o, 16)
                pe.wait_ge(mix_ready, 2 * b + 2)
                for r in range(E0 // 2):
                    last = mm(PB[5][:, 0:C], mixT[:, r, :], wo[:, r, :], start=(r == 0), stop=(r == E0 // 2 - 1))
                last.then_inc(o_ready, 1)

            def turn_x3(b):
                pe.wait_ge(qs_ready, b) if b >= 1 else pe.wait_ge(xn2T_ready, 2)
                pe.wait_ge(xn3_ready, b + 1)
                tr(PB[7][:, 0:T], xna[:, b, :], ident[:, :]).then_inc(xn3T_ps, 1)

            def project_q(b):
                pe.wait_ge(xn3T_ready, b + 1)
                mm(PB[7][:, 0:C], xn3T[:, :], wattn[:, 1, :], start=True, stop=True).then_inc(qp_ready, 1)

            def turn_q(b):
                pe.wait_ge(qsp_ready, b + 1)
                for g in range(4):
                    last = tr(PB[7][:, T * g:T * g + T], qsp[:, g, :, :].rearrange("p a c -> p (a c)"), ident[:, :])
                last.then_inc(qsT_ps, 1)

            def scores3(u):
                b, g = u // 4, u % 4
                if u < 2:
                    pe.wait_ge(qk_ready, NB - 1 + u)
                else:
                    pe.wait_ge(ex_in, u - 1)
                pe.wait_ge(km_ready, b + 1)
                pe.wait_ge(qs_ready, b + 1)
                mm(PB[0 if u % 2 == 0 else 2][:, :], qs[:, b, g, :], km[:, b % 2, g, :, :].rearrange("p j k -> p (j k)"),
                   start=True, stop=True).then_inc(s3_ready, 1)

            def turn_ex(v):
                if v == 0:
                    pe.wait_ge(ks_ready, NB)
                elif v == 1:
                    pe.wait_ge(aT_ready, NB)
                else:
                    pe.wait_ge(exT_ready, v - 1)
                pe.wait_ge(ex_ready, v + 1)
                for j in range(4):
                    last = tr(PB[1 if v % 2 == 0 else 3][:, T * j:T * j + T], ex[:, v % 4, T * j:T * j + T], ident[:, :])
                last.then_inc(exT_ps, 1)

            def attend3(w):
                b, g = w // 4, w % 4
                pe.wait_ge(exT_ready, w + 1)
                if g == 0:
                    pe.wait_ge(vm_ready, b + 1)
                    pe.wait_ge(yT_ready, b) if b >= 1 else pe.wait_ge(hm_ready, 4 * NB)
                for j in range(4):
                    h = 4 * g + j
                    last = mm(PB[4][:, T * (g // 2):T * (g // 2) + T], vm[:, b % 2, h, :], exT[:, w % 4, T * j:T * j + T],
                              start=(h % 8 == 0), stop=(h % 8 == 7))
                last.then_inc(pv_done, 1)

            def project_c(b):
                pe.wait_ge(x3_ready, b) if b >= 1 else pe.wait_ge(hm_ready, 4 * NB)
                pe.wait_ge(yT_ready, b + 1)
                mm(PB[6][:, 0:C], yT[:, b % 2, :], wattn[:, 2, :], start=True, stop=True).then_inc(c_ready, 1)

            def turn_x4(hf):
                pe.wait_ge(wT_ready, 1) if hf else pe.wait_ge(x2_ready, NB)
                pe.wait_ge(xn4_ready, HALF * hf + HALF)
                for i in range(HALF):
                    last = tr(PB[5][:, T * i:T * i + T], xnb[:, HALF * hf + i, :], ident[:, :])
                last.then_inc(xn4T_ps, 1)

            def router(hf):
                pe.wait_ge(xn4T_ready, hf + 1)
                if hf == 0:
                    pe.wait_ge(ld_up, 48)
                for i in range(HALF):
                    b = HALF * hf + i
                    last = mm(PB[5][:, E1 * i:E1 * i + E1], xn4T[:, T * b:T * b + T], wg[:, :], start=True, stop=True)
                last.then_inc(rt_ps, 1)

            def turn_w(hf):
                pe.wait_ge(wparts_ready, hf + 1)
                for i in range(HALF):
                    last = tr(PB[5][:, 0:256].bitcast(BF16)[:, T * i:T * i + T], wparts[:, HALF * hf + i, :], identb[:, :])
                last.then_inc(wT_ps, 1)

            def up(k):
                hf, ch = k // NCH, k % NCH
                n = chunk_rows(ch)
                c0 = 128 * ch
                x = xn4T[:, 512 * hf:512 * hf + 512]
                if k < 2:
                    pe.wait_ge(ex_in, 4 * NB - 1 + k)
                    pe.wait_ge(exT_ready, 4 * NB)
                    pe.wait_ge(qs_ready, NB)
                else:
                    pe.wait_ge(gated_ready, k - 1)
                    b_read(pe, k - 2)
                pe.wait_ge(xn4T_ready, hf + 1)
                mm(PB[0 if k % 2 == 0 else 2][0:n, :], wa[:, c0:c0 + n], x, start=True, stop=True)
                last = mm(PB[7 if k % 2 == 0 else 1][0:n, :], wb[:, c0:c0 + n], x, start=True, stop=True)
                if ch < NROUTED:
                    r = n_routed(k)
                    if r == 2:
                        pe.wait_ge(yT_ready, NB)
                    if r >= 3:
                        pe.wait_ge(hid_ready, routed_chunk(r - 2) + 1)
                    pe.wait_ge(wT_ready, hf + 1)
                    last = mm(PB[3 if r % 2 == 1 else 4][:, :], selw[:, :, :].rearrange("p e j -> p (e j)")[:, c0:c0 + 128],
                              wT[:, 512 * hf:512 * hf + 512], start=True, stop=True)
                last.then_inc(up_ready, 1)

            def down(k):
                hf, ch = k // NCH, k % NCH
                n = chunk_rows(ch)
                pe.wait_ge(hid_ready, k + 1)
                if ch == 0:
                    pe.wait_ge(out_ready, 1) if hf else pe.wait_ge(x3_ready, NB)
                    pe.wait_ge(ld_dn, 32)
                for i in range(HALF):
                    last = mm(PB[6][:, C * i:C * i + C], hid[0:n, k % 3, T * i:T * i + T], wdn[0:n, ch, :],
                              start=(ch == 0 and i == 0), stop=(ch == NCH - 1), skip_group_check=True)
                last.then_inc(down_done, 1)

            spread(0)
            spread(1)
            for s in range(LAST):
                for b in range(NB):
                    if s == 4 * b + 5:
                        turn_qk(b)
                    if s == 4 * b + 6:
                        scores2(b)
                    if s == 4 * b + 8:
                        turn_k(b)
                    if s == 4 * b + 9:
                        turn_p(b)
                    if s == 4 * b + 10:
                        attend2(b)
                    if s == 4 * b + 11:
                        spread_pairs(b, 0)
                    if s == 4 * b + 12:
                        spread_pairs(b, 1)
                    if s == 4 * b + 13:
                        project_o(b)
                    if s == 4 * b + 16:
                        turn_x3(b)
                    if s == 4 * b + 17:
                        project_q(b)
                    if s == 4 * b + 19:
                        turn_q(b)
                    if s == 4 * b + 3:
                        project_k(b)
                if s + 2 < 4 * NB:
                    spread(s + 2)
                if s < 4 * NB:
                    project(s)
                for b in range(NB):
                    if s == Q3 + 4 * b + 9:
                        project_c(b)
                for hf in range(2):
                    if s == tail(hf):
                        turn_x4(hf)
                    if s == tail(hf) + 1:
                        router(hf)
                    if s == tail(hf) + 4:
                        turn_w(hf)
                if 0 <= s - Q3 + 1 < 4 * NB:
                    scores3(s - Q3 + 1)
                if 0 <= s - Q3 - 3 < 4 * NB:
                    turn_ex(s - Q3 - 3)
                if 0 <= s - Q3 - 4 < 4 * NB:
                    attend3(s - Q3 - 4)
                if 0 <= s - F4 < 2 * NCH:
                    up(s - F4)
                if 0 <= s - F4 - 2 < 2 * NCH:
                    down(s - F4 - 2)


def kernel(**inputs):
    import numpy as np
    import concourse.bacc as bacc
    from concourse.bass_utils import run_bass_kernel_spmd

    a = {k: np.asarray(v) for k, v in inputs.items()}
    xa, fa, xb, fb = "L0_xattn_", "L0_ffn_", "L1_xattn_", "L1_ffn_"
    ctx = a["ctx_1024"]
    kvecs = np.stack([a[xa + n] for n in ("wkg", "bkg", "wkl", "bkl")])
    laid = {
        "x": a["x"].transpose(1, 0, 2),
        "ctx": ctx.transpose(1, 0, 2),
        "ctxT": ctx.reshape(NB * T, C).T,
        "cols": np.stack([a[xa + n] for n in ("wqg", "bqg", "wql", "bql", "wvg", "bvg", "wvl", "bvl", "wp")] + list(a[fa + "sim_matrix"].T), axis=1),
        "rows": np.concatenate([a[xa + "bp"], a[xb + "bc"], a[xb + "bk"], a[xb + "bq"], a[fa + "gates"]]),
        "kv": kvecs.reshape(4, H0, D0).transpose(1, 0, 2).reshape(H0, 4 * D0),
        "wattn": np.stack([a[xb + n].T for n in ("Wk", "Wq", "Wc")], axis=1),
        "wqkv": np.concatenate([a[fa + n] for n in ("q_proj", "k_proj", "v_proj")], axis=2).transpose(1, 0, 2),
        "wo": a[fa + "o_proj"].reshape(E0 // 2, 2 * HD, C).transpose(1, 0, 2),
        "wa": np.concatenate([a[fb + "W1"].transpose(1, 0, 2).reshape(C, E1 * HID), a[fb + "Ws1"]], axis=1),
        "wb": np.concatenate([a[fb + "W2"].transpose(1, 0, 2).reshape(C, E1 * HID), a[fb + "Ws2"]], axis=1),
        "wdn": np.concatenate([a[fb + "W3"].reshape(E1 * HID, C), a[fb + "Ws3"]], axis=0),
        "wg": a[fb + "Wg"],
    }
    nc = bacc.Bacc("TRN2", target_bir_lowering=False, num_devices=1)
    arrays, args = {}, []
    for name, v in laid.items():
        v = np.ascontiguousarray(v)
        arrays[f"{name}_dram"] = v
        args.append(nc.dram_tensor(f"{name}_dram", v.shape, mybir.dt.from_np(v.dtype), kind="ExternalInput").ap())
    out = nc.dram_tensor("out_dram", (T, NB, C), F32, kind="ExternalOutput").ap()
    build(nc, *args, out)
    r = run_bass_kernel_spmd(nc, [arrays], core_ids=[0])
    return np.ascontiguousarray(r.results[0]["out_dram"].transpose(1, 0, 2))
```

```python
import math
from contextlib import ExitStack

import concourse.bass as bass
from concourse import mybir

F32 = mybir.dt.float32
F32R = mybir.dt.float32r
BF16 = mybir.dt.bfloat16
I32 = mybir.dt.int32
ALU = mybir.AluOpType
ACT = mybir.ActivationFunctionType
AX = mybir.AxisListType

NB = 8
T = 128
C = 128
H0, D0 = 4, 32
E0, HD = 16, 64
H1, D1 = 16, 8
E1, HID = 8, 176
HS = 2 * HID
HALF = NB // 2
EPS = 1e-5
NEG = -1e30
RUP = HS + E1 * HID
NSHARED = HS // 128
NROUTED = E1 * HID // 128
NCH = NSHARED + NROUTED + 1
S0_SCALE = C ** -0.5
A_SCALE = HD ** -0.5
S1_SCALE = D1 ** -0.5

Q3 = 4 * NB + 3
F4 = Q3 + 4 * NB + 4
LAST = F4 + 2 * NCH + 4
ON_POOL = 2 * NCH - 2

WQG, BQG, WQL, BQL, WVG, BVG, WVL, BVL, WP = range(9)
R_BP, R_BC, R_BK, R_BQ = range(4)


def bc(ap, axis, n):
    a = ap.unsqueeze(axis)
    shape = list(a.shape)
    shape[axis] = n
    return a.to_broadcast(shape)


def diag(tile, start):
    a = tile.rearrange("p h c -> p (h c)")
    return bass.AP(a.tensor, a.offset + start, [list(a.ap[0]), [128 + D1, 8], [1, D1]])


def build(nc, x_d, ctx_d, ctxT_d, cols_d, rows_d, kv_d, wattn_d, wqkv_d, wo_d, wa_d, wb_d, wdn_d, wg_d, out_d):
    starts, ends = {}, {}
    with ExitStack() as ctx:
        def sb(name, shape, dt=F32):
            t = ctx.enter_context(nc.sbuf_tensor(name, shape, dt))
            ends[name] = nc.sbuf_base
            starts[name] = nc.sbuf_base - math.prod(shape[1:]) * mybir.dt.size(dt)
            return t

        def over(name, shape, dt, under, skip=0):
            at = starts[under] + skip
            assert at + math.prod(shape[1:]) * mybir.dt.size(dt) <= ends[under]
            return nc.alloc_sbuf_tensor_at(name, shape, dt, offset=at)

        def sem(name):
            return ctx.enter_context(nc.semaphore(name))

        xr = sb("xr", [T, NB, C])
        cx = sb("cx", [T, NB, C])
        cxT = sb("cxT", [C, NB * T])
        colsim = sb("colsim", [C, 9 + E0])
        cols, sim = colsim[:, 0:9], colsim[:, 9:9 + E0]
        rowv = sb("rowv", [128, 4 * C + E0])
        rows = rowv[:, 0:4 * C].rearrange("p (a c) -> p a c", c=C)
        gates = rowv[:, 4 * C:4 * C + E0]
        kv = sb("kv", [C, 4, D0])
        wattn = sb("wattn", [C, 3, C])
        wqkv = sb("wqkv", [C, E0, 3 * HD])
        wo = sb("wo", [2 * HD, E0 // 2, C])
        wa = sb("wa", [C, RUP])
        wb = sb("wb", [C, RUP])
        wdn = sb("wdn", [128, NCH, C])
        wg = sb("wg", [C, E1])

        ident = sb("ident", [128, 128])
        identb = sb("identb", [128, 128], BF16)
        ones = sb("ones", [128, 128])
        causal = sb("causal", [T, T])
        orderi = sb("orderi", [128, E0], I32)
        order = sb("order", [128, E0])
        wp2 = sb("wp2", [C, 1])
        part16 = sb("part16", [128, E0])
        part8 = sb("part8", [128, E1])
        hmask = sb("hmask", [128, 4])
        sel = sb("sel", [128, E0, 128], BF16)
        sel2 = sb("sel2", [128, E0 // 2, 2, HD], BF16)
        selw = sb("selw", [128, E1, HID], BF16)

        st = sb("st", [128, 4, NB, 6])
        mv = sb("mv", [128, 4, NB, 2])
        ve = sb("ve", [128, 4, NB])
        rstd = sb("rstd", [128, 4, NB])
        hn = sb("hn", [128, NB])
        rhn = sb("rhn", [128, NB])
        xna = sb("xna", [T, NB, C])
        xnb = sb("xnb", [T, NB, C])
        xn2T = sb("xn2T", [C, NB, T])
        xn4T = xn2T[:, :, :].rearrange("p b t -> p (b t)")

        kw = sb("kw", [C, 2, 2, HALF, D0])
        kb = sb("kb", [C, 2, D0])
        cm = sb("cm", [C, 2, 2 * HALF])
        cs = sb("cs", [C, 2, 2 * HALF])

        sim2 = sb("sim2", [C, E0])
        simn = sb("simn", [C, E0])
        sgate = sb("sgate", [128, E0])
        lg = sb("lg", [T, NB, E0])
        ga = sb("ga", [T, NB, E0])
        f1 = sb("f1", [T, NB, E0])
        f2 = sb("f2", [T, NB, E0])
        gv = sb("gv", [T, 6, NB])
        gin = sb("gin", [T, NB, E0])
        gex = sb("gex", [T, NB, E0])
        rw = sb("rw", [T, NB, E0])
        parts = sb("parts", [T, NB, 128], BF16)
        rwT = sb("rwT", [128, NB, T], BF16)
        wparts = sb("wparts", [T, NB, 128], BF16)
        wT = sb("wT", [128, NB * T], BF16)

        hm = sb("hm", [C, 2, E0, T])
        qk = sb("qk", [T, 2, 2 * HD])
        v2 = sb("v2", [T, 2, 2, HD])
        qkT = sb("qkT", [HD, 2, 2, T])
        s2 = sb("s2", [T, 2, T])
        mx2 = sb("mx2", [T, NB])
        nmx2 = sb("nmx2", [T, NB])
        den2 = sb("den2", [T, NB])
        rden2 = sb("rden2", [T, NB])
        pn = sb("pn", [T, 2, T])
        pT2 = sb("pT2", [T, 2, T])
        aT = sb("aT", [2 * HD, 2, T])
        m16 = sb("m16", [128, E0])
        mixT = sb("mixT", [2 * HD, E0 // 2, T])

        qf = sb("qf", [T, C])
        qsp = sb("qsp", [T, 4, 4, 32])
        ks = sb("ks", [128, NB, 4, T], F32R)
        qs = sb("qs", [128, NB, 4, T], F32R)
        xn3T = sb("xn3T", [C, T])
        km = sb("km", [128, 2, 4, 4, T], F32R)
        vm = sb("vm", [T, 2, H1, 128])
        ex = sb("ex", [T, 4, 4 * T])
        exT = sb("exT", [T, 4, 4 * T])
        mx3 = sb("mx3", [T, 8, 4])
        ry = sb("ry", [64, 2, T])
        yT = sb("yT", [C, 2, T])
        vT = exT[:, :, :].rearrange("p a n -> p (a n)").rearrange("p (v n) -> p v n", v=2)
        bd = ex[:, :, :].rearrange("p a n -> p (a n)").rearrange("p (f v i n) -> p f v i n", f=2, v=2, i=HALF)
        early = hm[:, 1, :, :].rearrange("p e t -> p (e t)")
        sc = early[:, 0:512].rearrange("p (f v i e) -> p f v i e", f=2, v=2, i=HALF)
        sc2 = early[:, 512:1024].rearrange("p (f v i e) -> p f v i e", f=2, v=2, i=HALF)
        ff = hm[:, :, :, :].rearrange("p a e t -> p (a e t)").rearrange("p (k n) -> p k n", n=4 * T)
        gated, hid = ff[:, 0:2, :], ff[:, 2:4, :]
        outT = xna[:, :, :].rearrange("p b c -> p (b c)").rearrange("p (h n) -> p h n", h=2)
        x4hi = over("x4hi", [C, NB * T], F32R, "wqkv")
        x4lo = over("x4lo", [C, NB * T], F32R, "wqkv", 4 * NB * T)
        kf = over("kf", [T, 2, NB * C // 2], F32, "vm")
        ksp = over("ksp", [T, NB * 2, 4, 32], F32, "vm", 4 * NB * C)
        walo = over("walo", [C, RUP], F32R, "wa")
        wblo = over("wblo", [C, RUP], F32R, "wb")
        wdlo = over("wdlo", [128, NCH, C], F32R, "wdn")
        wparts_up = ks[:, :, :, :].rearrange("p b g t -> p (b g t)")
        wahi, wbhi = wparts_up[:, 0:RUP], wparts_up[:, RUP:2 * RUP]
        wdhi = km[:, :, :, :, :].rearrange("p a g j t -> p (a g j t)")[:, 0:NCH * C].rearrange("p (k c) -> p k c", c=C)
        hparts = qs[:, :, :, :].rearrange("p b g t -> p (b g t)").rearrange("p (k n) -> p k n", n=4 * T)
        hhi, hlo = hparts[:, 0:3, :], hparts[:, 3:6, :]

        PB = [ctx.enter_context(nc.psum_tensor(f"bank{i}", [128, 512], F32)) for i in range(8)]

        ld_x = [sem(f"ld_x{i}") for i in range(2)]
        ld_ctx = [sem(f"ld_ctx{i}") for i in range(2)]
        ld_vec = sem("ld_vec")
        ld_ctxT = sem("ld_ctxT")
        ld_attn = sem("ld_attn")
        ld_qkv = sem("ld_qkv")
        ld_o = sem("ld_o")
        ld_up = sem("ld_up")
        ld_dn = sem("ld_dn")
        c_id = sem("c_id"); c_ones = sem("c_ones"); c_pool = sem("c_pool"); pool_step = sem("pool_step")
        c_part = sem("c_part"); c_sel = sem("c_sel")
        zeroed = sem("zeroed")
        dve_step = sem("dve_step")
        ve_ready = sem("ve_ready"); rstd_ready = sem("rstd_ready")
        hn_ready = sem("hn_ready"); rhn_ready = sem("rhn_ready")
        xbp_ready = sem("xbp_ready")
        k1_used = sem("k1_used"); s_used = sem("s_used"); x1_ready = sem("x1_ready"); lg_used = sem("lg_used")
        x2_ready = sem("x2_ready"); kf_ready = sem("kf_ready"); khi_ready = sem("khi_ready"); x3_ready = sem("x3_ready"); xbc_ready = sem("xbc_ready")
        nmx_ready = sem("nmx_ready"); mixw_ready = sem("mixw_ready")
        k1_ready = sem("k1_ready"); sim2_ready = sem("sim2_ready"); simsum_ready = sem("simsum_ready")
        ssq_ready = sem("ssq_ready"); simr_ready = sem("simr_ready"); simn_ready = sem("simn_ready")
        egate_ready = sem("egate_ready"); vT_ready = sem("vT_ready")
        xn1_ready = sem("xn1_ready"); s_ready = sem("s_ready"); sc_ready = sem("sc_ready"); sce_ready = sem("sce_ready")
        bd_ready = sem("bd_ready"); att_ready = sem("att_ready")
        xn2_ready = sem("xn2_ready"); xn2T_ps = sem("xn2T_ps"); xn2T_ready = sem("xn2T_ready")
        lg_ps = sem("lg_ps"); gin_ready = sem("gin_ready"); gex_ready = sem("gex_ready")
        parts_ready = sem("parts_ready"); rwT_ps = sem("rwT_ps"); rwT_ready = sem("rwT_ready")
        rb_ready = sem("rb_ready"); hm_ready = sem("hm_ready"); qkv_done = sem("qkv_done")
        qk_ready = sem("qk_ready"); qkT_ps = sem("qkT_ps"); qkT_ready = sem("qkT_ready")
        s2_ps = sem("s2_ps"); s2_ready = sem("s2_ready"); p2_ready = sem("p2_ready"); pn_ready = sem("pn_ready")
        pT2_ps = sem("pT2_ps"); pT2_ready = sem("pT2_ready"); aT_ps = sem("aT_ps"); aT_ready = sem("aT_ready")
        mix_ready = sem("mix_ready"); o_ready = sem("o_ready")
        kp_ready = sem("kp_ready"); ksp_ready = sem("ksp_ready"); ksT_ps = sem("ksT_ps"); ks_ready = sem("ks_ready")
        xn3_ready = sem("xn3_ready"); xn3T_ps = sem("xn3T_ps"); xn3T_ready = sem("xn3T_ready")
        qp_ready = sem("qp_ready"); qsp_ready = sem("qsp_ready"); qsT_ps = sem("qsT_ps"); qs_ready = sem("qs_ready")
        km_ready = sem("km_ready"); vm_ready = sem("vm_ready")
        s3_ready = sem("s3_ready"); mx3_ready = sem("mx3_ready"); ex_ready = sem("ex_ready")
        exT_ps = sem("exT_ps"); exT_ready = sem("exT_ready"); pv_done = sem("pv_done")
        yT_ready = sem("yT_ready"); c_ready = sem("c_ready")
        xn4_ready = sem("xn4_ready"); xn4T_ps = sem("xn4T_ps"); xn4T_ready = sem("xn4T_ready")
        rt_ps = sem("rt_ps"); rt_used = sem("rt_used"); rin_ready = sem("rin_ready"); rex_ready = sem("rex_ready")
        wparts_ready = sem("wparts_ready"); wT_ps = sem("wT_ps"); wT_ready = sem("wT_ready")
        up_ready = sem("up_ready"); gated_ready = sem("gated_ready"); prod_ready = sem("prod_ready")
        hid_ready = sem("hid_ready"); hhi_ready = sem("hhi_ready"); hlo_ready = sem("hlo_ready")
        x4hi_ready = sem("x4hi_ready"); x4lo_ready = sem("x4lo_ready")
        whi_ready = sem("whi_ready"); wlo_ready = sem("wlo_ready"); wdlo_ready = sem("wdlo_ready"); down_done = sem("down_done")
        out_ready = sem("out_ready"); stored = sem("stored")

        def bs(hf):
            return slice(HALF * hf, HALF * hf + HALF)

        def head_rows(h):
            return slice(D0 * h, D0 * h + D0)

        def chunk_rows(ch):
            return min(128, RUP - 128 * ch)

        def is_routed(k):
            return NSHARED <= k % NCH < NSHARED + NROUTED

        def n_routed(k):
            return NROUTED * (k // NCH) + min(max(k % NCH + 1 - NSHARED, 0), NROUTED)

        def routed_chunk(r):
            return (r - 1) // NROUTED * NCH + NSHARED + (r - 1) % NROUTED

        def tail(hf):
            return Q3 + 4 * (HALF * hf + HALF - 1) + 15

        def score_bank(u):
            return (0, 2, 7)[u % 3]

        def key_bank(hf):
            return 0 if hf else 5

        def turned_key_bank(b):
            return (6, 7, 5, 2, 3, 2, 0, 7)[b]

        def query_bank(b):
            return 7 if b < HALF else 6

        def pv_bank(b):
            return 4 if b % 2 == 0 else 5

        def router_bank(hf):
            return 5 if hf else 6

        def weights_in(hf):
            return tail(hf) + 9

        def b_read(eng, k):
            if is_routed(k):
                eng.wait_ge(prod_ready, n_routed(k))
            else:
                eng.wait_ge(hid_ready, k + 1)

        block = ctx.enter_context(nc.Block())

        @block.sync
        def _(sp):
            sp.dma_start(xr[:, bs(0), :], x_d[:, bs(0), :]).then_inc(ld_x[0], 16)
            sp.dma_start(colsim[:, :], cols_d).then_inc(ld_vec, 16)
            sp.dma_start(rowv[:, :], rows_d.partition_broadcast(128)).then_inc(ld_vec, 16)
            sp.dma_start(cx[:, bs(0), :], ctx_d[:, bs(0), :]).then_inc(ld_ctx[0], 16)
            sp.dma_start(xr[:, bs(1), :], x_d[:, bs(1), :]).then_inc(ld_x[1], 16)
            sp.dma_start(cx[:, bs(1), :], ctx_d[:, bs(1), :]).then_inc(ld_ctx[1], 16)
            sp.dma_start(cxT[:, :], ctxT_d).then_inc(ld_ctxT, 16)
            sp.dma_start(wattn[:, :, :], wattn_d).then_inc(ld_attn, 16)
            sp.dma_start(wqkv[:, :, :], wqkv_d).then_inc(ld_qkv, 16)
            sp.dma_start(wo[:, :, :], wo_d).then_inc(ld_o, 16)
            sp.dma_start(wa[:, :], wa_d).then_inc(ld_up, 16)
            sp.dma_start(wb[:, :], wb_d).then_inc(ld_up, 16)
            sp.dma_start(wg[:, :], wg_d).then_inc(ld_up, 16)
            full = RUP // 128
            sp.dma_start(wdn[:, 0:full, :], wdn_d[0:full * 128, :].rearrange("(k p) c -> p k c", p=128)).then_inc(ld_dn, 16)
            sp.dma_start(wdn[0:RUP - full * 128, full, :], wdn_d[full * 128:RUP, :]).then_inc(ld_dn, 16)
            for hf in range(2):
                sp.wait_ge(out_ready, hf + 1)
                sp.dma_start(out_d[:, 512 * hf:512 * hf + 512], outT[:, hf, :]).then_inc(stored, 16)
            sp.wait_ge(stored, 32)

        @block.gpsimd
        def _(pool):
            steps = [0]

            def link(ins):
                steps[0] += 1
                ins.then_inc(pool_step, 1)
                pool.wait_ge(pool_step, steps[0])

            link(nc.gpsimd.memset(ident[:, :], 0.0))
            nc.gpsimd.affine_select(out=ident[:, :], in_=ident[:, :], compare_op=ALU.not_equal, fill=1.0, base=0,
                                    pattern=[[-1, 128]], channel_multiplier=1).then_inc(c_id, 1)
            nc.gpsimd.memset(m16[:, :], -0.5).then_inc(c_pool, 1)
            nc.gpsimd.iota(orderi[:, :], [[-1, E0]], base=E0, channel_multiplier=0).then_inc(c_pool, 1)

            def power(dst, src, signal):
                nc.gpsimd.tensor_tensor(dst, src, m16[:, 0:src.shape[1]], ALU.pow).then_inc(signal, 1)

            def rstd_of(n, k, b0, b1):
                pool.wait_ge(ve_ready, n)
                power(rstd[:, k, b0:b1], ve[:, k, b0:b1], rstd_ready)

            pool.wait_ge(c_pool, 2)
            rstd_of(1, 0, 0, HALF)
            rstd_of(2, 0, HALF, NB)
            nc.gpsimd.memset(ex[:, :, :], 0.0).then_inc(zeroed, 1)
            pool.wait_ge(ld_vec, 16 * 6)

            def add_bp(hf):
                pool.wait_ge(xn1_ready, hf + 1)
                nc.gpsimd.tensor_tensor(xr[:, bs(hf), :], xr[:, bs(hf), :], bc(rows[:, R_BP, :], 1, HALF), ALU.add).then_inc(xbp_ready, 1)

            def low_keys(hf):
                pool.wait_ge(khi_ready, hf + 1)
                nc.gpsimd.tensor_tensor(ksp[:, :, 1:4:2, :], bc(kf[:, hf, :].rearrange("p (g c) -> p g c", c=32), 2, 2),
                                        ksp[:, :, 0:4:2, :], ALU.subtract).then_inc(ksp_ready, 1)

            add_bp(0)
            nc.gpsimd.memset(parts[:, :, :], 0.0).then_inc(zeroed, 1)
            link(nc.gpsimd.memset(causal[:, :], 0.0))
            nc.gpsimd.affine_select(out=causal[:, :], in_=causal[:, :], compare_op=ALU.is_ge, fill=NEG, base=0,
                                    pattern=[[-1, T]], channel_multiplier=1).then_inc(c_pool, 1)
            add_bp(1)
            low_keys(0)
            pool.wait_ge(ssq_ready, 1)
            power(sim2[:, :], sim2[:, :], simr_ready)
            for hf in range(2):
                rstd_of(3 + hf, 1, HALF * hf, HALF * hf + HALF)
                pool.wait_ge(hn_ready, hf + 1)
                power(rhn[:, bs(hf)], hn[:, bs(hf)], rhn_ready)
                if hf == 0:
                    low_keys(1)
            pool.wait_ge(ksT_ps, NB)
            nc.gpsimd.memset(wparts[:, :, :], 0.0).then_inc(zeroed, 1)
            link(nc.gpsimd.memset(vm[:, :, :, :], 0.0))
            for p in range(2):
                for g in range(2):
                    ins = nc.gpsimd.memset(diag(vm[:, p, 8 * g:8 * g + 8, :], 64), 1.0)
            link(ins)

            def fill_vm(b):
                if b >= 2:
                    pool.wait_ge(pv_done, 4 * (b - 1))
                for g in range(2):
                    ins = nc.gpsimd.tensor_copy(diag(vm[:, b % 2, 8 * g:8 * g + 8, :], 0),
                                                cx[:, b, 64 * g:64 * g + 64].rearrange("p (h i) -> p h i", i=D1))
                ins.then_inc(vm_ready, 1)

            def mask_k(b):
                pool.wait_ge(ks_ready, b + 1)
                if b >= 2:
                    pool.wait_ge(s3_ready, 4 * (b - 1))
                for g in range(4):
                    ins = nc.gpsimd.tensor_tensor(km[:, b % 2, g, :, :], bc(ks[:, b, g, :].bitcast(F32), 1, 4),
                                                  bc(hmask[:, :], 2, T), ALU.mult)
                ins.then_inc(km_ready, 1)

            def add_bc(b):
                pool.wait_ge(xn3_ready, b + 1)
                nc.gpsimd.tensor_tensor(xr[:, b, :], xr[:, b, :], rows[:, R_BC, :], ALU.add).then_inc(xbc_ready, 1)

            pool.wait_ge(ld_ctx[0], 16)
            pool.wait_ge(ld_ctx[1], 16)
            pool.wait_ge(c_part, 1)
            for b in range(NB):
                rstd_of(5 + b, 2, b, b + 1)
                add_bc(b)
                if b in (2, 4):
                    fill_vm(b // 2 - 1)
                    mask_k(b // 2 - 1)
                if b == 6:
                    mask_k(2)

            def low_part(dst, src, hi):
                return nc.gpsimd.tensor_tensor(dst, src, hi.bitcast(F32), ALU.subtract)

            def split_x4(hf):
                cols4 = slice(512 * hf, 512 * hf + 512)
                pool.wait_ge(x4hi_ready, hf + 1)
                low_part(x4lo[:, cols4], xn4T[:, cols4], x4hi[:, cols4]).then_inc(x4lo_ready, 1)

            def split_up(ch):
                c = slice(128 * ch, 128 * ch + chunk_rows(ch))
                pool.wait_ge(whi_ready, ch + 1)
                low_part(walo[:, c], wa[:, c], wahi[:, c])
                low_part(wblo[:, c], wb[:, c], wbhi[:, c]).then_inc(wlo_ready, 1)

            def split_hidden(k):
                n = chunk_rows(k % NCH)
                pool.wait_ge(hhi_ready, k + 1)
                if k >= 3:
                    pool.wait_ge(down_done, k - 2)
                low_part(hlo[0:n, k % 3, :], hid[0:n, k % 2, :], hhi[0:n, k % 3, :]).then_inc(hlo_ready, 1)

            for s in range(Q3, LAST):
                for b in range(NB):
                    if s == Q3 + 4 * b + 11:
                        rstd_of(5 + NB + b, 3, b, b + 1)
                    if b >= 3 and s == Q3 + 4 * b - 5:
                        mask_k(b)
                    if b >= 2 and s == Q3 + 4 * b:
                        fill_vm(b)
                for hf in range(2):
                    if s == tail(hf):
                        split_x4(hf)
                if 0 <= s - F4 + 3 < NCH:
                    split_up(s - F4 + 3)
                if 0 <= s - F4 - 1 < ON_POOL:
                    split_hidden(s - F4 - 1)

        @block.scalar
        def _(act):
            for h in range(H0):
                act.dma_start(kv[head_rows(h), :, :].rearrange("p v e -> p (v e)"), kv_d[h, :].partition_broadcast(D0)).then_inc(ld_vec, 16)
            act.wait_ge(ld_vec, 16 * 6)
            nc.scalar.activation(sgate[:, :], gates[:, :], ACT.Exp, scale=-1.0).then_inc(egate_ready, 1)
            act.wait_ge(ld_ctxT, 16)
            for v, (w, b) in enumerate(((WVG, BVG), (WVL, BVL))):
                nc.scalar.activation(vT[:, v, :], cxT[:, :], ACT.Identity, bias=cols[:, b:b + 1],
                                     scale=cols[:, w:w + 1]).then_inc(vT_ready, 1)
            def exp_channels(hf):
                act.wait_ge(sc_ready, hf + 1)
                nc.scalar.activation(sc2[:, hf, :, :, :], sc[:, hf, :, :, :], ACT.Exp, scale=S0_SCALE).then_inc(sce_ready, 1)

            def take_xn2T(hf):
                act.wait_ge(xn2T_ps, hf + 1)
                nc.scalar.activation(xn2T[:, bs(hf), :].rearrange("p b t -> p (b t)"), PB[6 + hf][:, :], ACT.Copy).then_inc(xn2T_ready, 1)

            def gate_exp(hf):
                act.wait_ge(gin_ready, hf + 1)
                nc.scalar.activation(gex[:, 0:HALF, :], gin[:, 0:HALF, :], ACT.Exp).then_inc(gex_ready, 1)

            def take_rwT(hf):
                act.wait_ge(rwT_ps, hf + 1)
                nc.scalar.activation(rwT[:, bs(hf), :].rearrange("p b t -> p (b t)"), PB[7 if hf else 3][:, 0:256].bitcast(BF16), ACT.Copy).then_inc(rwT_ready, 1)

            def high_keys(hf):
                act.wait_ge(kf_ready, hf + 1)
                if hf == 1:
                    act.wait_ge(ksT_ps, HALF)
                nc.scalar.activation(ksp[:, :, 0:4:2, :].bitcast(F32R), bc(kf[:, hf, :].rearrange("p (g c) -> p g c", c=32), 2, 2),
                                     ACT.Copy).then_inc(khi_ready, 1)

            def take_ks(b):
                act.wait_ge(ksT_ps, b + 1)
                nc.scalar.activation(ks[:, b, :, :].rearrange("p g t -> p (g t)"), PB[turned_key_bank(b)][:, :], ACT.Copy).then_inc(ks_ready, 1)

            exp_channels(0)
            act.wait_ge(c_part, 1)
            nc.scalar.activation(identb[:, :], ident[:, :], ACT.Copy)
            high_keys(0)
            nc.scalar.activation(sel[:, :, :], bc(part16[:, :], 2, 128), ACT.Copy).then_inc(c_sel, 1)
            exp_channels(1)
            for b in range(HALF):
                take_ks(b)
            take_xn2T(0)
            nc.scalar.activation(sel2[:, :, :, :].rearrange("p r j d -> p (r j) d"), bc(part16[:, :], 2, HD), ACT.Copy)
            nc.scalar.activation(selw[:, :, :], bc(part8[:, :], 2, HID), ACT.Copy).then_inc(c_sel, 1)
            high_keys(1)
            take_ks(4)
            take_ks(5)
            gate_exp(0)
            take_ks(6)
            take_ks(7)
            take_rwT(0)

            def take_qkv(b):
                act.wait_ge(qkv_done, 4 * b + 4)
                if b >= 2:
                    act.wait_ge(aT_ps, b - 1)
                bank = PB[0 if b % 2 == 0 else 2]
                nc.scalar.activation(qk[:, b % 2, :], bank[:, 0:2 * HD], ACT.Copy)
                nc.scalar.activation(v2[:, b % 2, :, :], bc(bank[:, 2 * HD:3 * HD], 1, 2), ACT.Copy).then_inc(qk_ready, 1)

            def take_qkT(b):
                act.wait_ge(qkT_ps, b + 1)
                if b >= 2:
                    act.wait_ge(s2_ps, b - 1)
                nc.scalar.activation(qkT[:, b % 2, :, :].rearrange("p a t -> p (a t)"), PB[1][0:HD, 0:2 * T], ACT.Copy).then_inc(qkT_ready, 1)

            def exp2(b):
                act.wait_ge(s2_ready, b + 1)
                act.wait_ge(nmx_ready, b + 1)
                if b >= 2:
                    act.wait_ge(pT2_ps, b - 1)
                nc.scalar.activation(pn[:, b % 2, :], s2[:, b % 2, :], ACT.Exp, bias=nmx2[:, b:b + 1], scale=A_SCALE,
                                     accum_out=den2[:, b:b + 1]).then_inc(p2_ready, 1)

            def take_pT(b):
                act.wait_ge(pT2_ps, b + 1)
                if b >= 2:
                    act.wait_ge(aT_ps, b - 1)
                nc.scalar.activation(pT2[:, b % 2, :], PB[3][:, 0:T], ACT.Copy).then_inc(pT2_ready, 1)

            def take_aT(b):
                act.wait_ge(aT_ps, b + 1)
                if b >= 2:
                    act.wait_ge(mix_ready, 2 * (b - 1))
                nc.scalar.activation(aT[:, b % 2, :], PB[3][:, 0:T], ACT.Copy).then_inc(aT_ready, 1)

            def take_xn3T(b):
                act.wait_ge(xn3T_ps, b + 1)
                if b >= 1:
                    act.wait_ge(qp_ready, b)
                nc.scalar.activation(xn3T[:, :], PB[query_bank(b)][:, 0:T], ACT.Copy).then_inc(xn3T_ready, 1)

            def take_qs(b):
                act.wait_ge(qsT_ps, b + 1)
                nc.scalar.activation(qs[:, b, :, :].rearrange("p g t -> p (g t)"), PB[query_bank(b)][:, :], ACT.Copy).then_inc(qs_ready, 1)

            def exp3(u):
                act.wait_ge(mx3_ready, u + 1)
                if u >= 4:
                    act.wait_ge(exT_ps, u - 3)
                for j in range(4):
                    last = nc.scalar.activation(ex[:, u % 4, T * j:T * j + T], PB[score_bank(u)][:, T * j:T * j + T],
                                                ACT.Exp, bias=mx3[:, u % 8, j:j + 1])
                last.then_inc(ex_ready, 1)

            def take_exT(v):
                act.wait_ge(exT_ps, v + 1)
                if v >= 4:
                    act.wait_ge(pv_done, v - 3)
                nc.scalar.activation(exT[:, v % 4, :], PB[1 if v % 2 == 0 else 3][:, :], ACT.Copy).then_inc(exT_ready, 1)

            def take_xn4T(hf):
                act.wait_ge(xn4T_ps, hf + 1)
                nc.scalar.activation(xn4T[:, 512 * hf:512 * hf + 512], PB[router_bank(hf)][:, :], ACT.Copy).then_inc(xn4T_ready, 1)
                act.wait_ge(xn4T_ready, hf + 1)
                nc.scalar.activation(x4hi[:, 512 * hf:512 * hf + 512], xn4T[:, 512 * hf:512 * hf + 512], ACT.Copy).then_inc(x4hi_ready, 1)

            def high_weights(ch):
                n = chunk_rows(ch)
                c = slice(128 * ch, 128 * ch + n)
                if ch == 0:
                    act.wait_ge(ld_up, 48)
                    act.wait_ge(ld_dn, 32)
                    act.wait_ge(km_ready, NB)
                    act.wait_ge(s3_ready, 4 * NB)
                nc.scalar.activation(wahi[:, c], wa[:, c], ACT.Copy)
                nc.scalar.activation(wbhi[:, c], wb[:, c], ACT.Copy)
                nc.scalar.activation(wdhi[0:n, ch, :], wdn[0:n, ch, :], ACT.Copy).then_inc(whi_ready, 1)

            def high_hidden(k):
                n = chunk_rows(k % NCH)
                act.wait_ge(hid_ready, k + 1)
                if k >= 3:
                    act.wait_ge(down_done, k - 2)
                nc.scalar.activation(hhi[0:n, k % 3, :], hid[0:n, k % 2, :], ACT.Copy).then_inc(hhi_ready, 1)

            def router_exp(hf):
                act.wait_ge(rin_ready, hf + 1)
                nc.scalar.activation(gex[:, 0:HALF, 0:E1], gin[:, 0:HALF, 0:E1], ACT.Exp).then_inc(rex_ready, 1)

            def take_wT(hf):
                act.wait_ge(wT_ps, hf + 1)
                nc.scalar.activation(wT[:, 512 * hf:512 * hf + 512], PB[router_bank(hf)][:, 0:256].bitcast(BF16), ACT.Copy).then_inc(wT_ready, 1)

            def silu(k):
                act.wait_ge(up_ready, k + 1)
                if k >= 2:
                    b_read(act, k - 2)
                n = chunk_rows(k % NCH)
                nc.scalar.activation(gated[0:n, k % 2, :], PB[0 if k % 2 == 0 else 2][0:n, :], ACT.Silu).then_inc(gated_ready, 1)

            def result(hf):
                act.wait_ge(down_done, NCH * (hf + 1))
                nc.scalar.activation(outT[:, hf, :], PB[5 if hf else 6][:, :], ACT.Copy).then_inc(out_ready, 1)

            for s in range(LAST):
                if s - F4 in (NCH + 3, 2 * NCH + 3):
                    result(0 if s - F4 == NCH + 3 else 1)
                if s == 2:
                    take_xn2T(1)
                if s == 12:
                    take_rwT(1)
                for b in reversed(range(NB)):
                    if s == 4 * b + 4:
                        take_qkv(b)
                    if s == 4 * b + 5:
                        take_qkT(b)
                    if s == 4 * b + 7:
                        exp2(b)
                    if s == 4 * b + 9:
                        take_pT(b)
                    if s == 4 * b + 10:
                        take_aT(b)
                    if s == 4 * b + 16:
                        take_xn3T(b)
                    if s == 4 * b + 19:
                        take_qs(b)
                if s == 8:
                    gate_exp(1)
                if 0 <= s - Q3 - 3 < 4 * NB:
                    take_exT(s - Q3 - 3)
                if 0 <= s - Q3 < 4 * NB:
                    exp3(s - Q3)
                for hf in range(2):
                    if s == tail(hf):
                        take_xn4T(hf)
                    if s == tail(hf) + 5:
                        router_exp(hf)
                    if s == weights_in(hf):
                        take_wT(hf)
                if 0 <= s - F4 + 3 < NCH:
                    high_weights(s - F4 + 3)
                if 0 <= s - F4 < 2 * NCH:
                    silu(s - F4)
                if 0 <= s - F4 - 1 < 2 * NCH:
                    high_hidden(s - F4 - 1)

        @block.vector
        def _(dve):
            steps = [0]

            def link(ins):
                steps[0] += 1
                ins.then_inc(dve_step, 1)
                dve.wait_ge(dve_step, steps[0])

            V = nc.vector

            def stats(k, b0, b1):
                for b in range(b0, b1):
                    ins = V.bn_stats(st[:, k, b, :], xr[:, b, :])
                link(ins)
                for b in range(b0, b1):
                    ins = V.bn_aggr(mv[:, k, b, :], st[:, k, b, :])
                link(ins)
                V.tensor_scalar(ve[:, k, b0:b1], mv[:, k, b0:b1, 1], EPS, None, ALU.add).then_inc(ve_ready, 1)

            def normalise(dst, k, b0, b1, n, signal):
                dve.wait_ge(rstd_ready, n)
                for b in range(b0, b1):
                    ins = V.tensor_scalar(dst[:, b, :], xr[:, b, :], mv[:, k, b, 0:1], rstd[:, k, b:b + 1],
                                          ALU.subtract, ALU.mult)
                ins.then_inc(signal, 1)

            def greatest(l, vi, e, n):
                link(V.tensor_reduce(gv[:, vi, 0:n], l, AX.X, ALU.max))
                link(V.tensor_tensor(ga[:, 0:n, 0:e], l, bc(gv[:, vi, 0:n], 2, e), ALU.is_equal))

            def earliest(f, vi, e, n):
                link(V.tensor_tensor(ga[:, 0:n, 0:e], ga[:, 0:n, 0:e], bc(order[:, E0 - e:E0], 1, n), ALU.mult))
                link(V.tensor_reduce(gv[:, vi, 0:n], ga[:, 0:n, 0:e], AX.X, ALU.max))
                link(V.tensor_tensor(f, ga[:, 0:n, 0:e], bc(gv[:, vi, 0:n], 2, e), ALU.is_equal))

            def two_best(e, n, step):
                l, a, b, rest = lg[:, 0:n, 0:e], f1[:, 0:n, 0:e], f2[:, 0:n, 0:e], gin[:, 0:n, 0:e]
                if step == 0:
                    greatest(l, 0, e, n)
                if step == 1:
                    earliest(a, 1, e, n)
                if step == 2:
                    link(V.scalar_tensor_tensor(out=rest, in0=a, scalar=-1e30, in1=l, op0=ALU.mult, op1=ALU.add))
                    greatest(rest, 2, e, n)
                if step == 3:
                    earliest(b, 3, e, n)
                    link(V.tensor_tensor(a, a, b, ALU.add))

            def weigh(e, n, mask):
                p = rw[:, 0:n, 0:e]
                link(V.tensor_tensor(p, gex[:, 0:n, 0:e], mask, ALU.mult))
                link(V.tensor_reduce(gv[:, 4, 0:n], p, AX.X, ALU.add))
                link(V.reciprocal(gv[:, 5, 0:n], gv[:, 4, 0:n]))
                link(V.tensor_tensor(p, p, bc(gv[:, 5, 0:n], 2, e), ALU.mult))

            def three_parts(e, n, into, b0):
                p = rw[:, 0:n, 0:e]
                for j in range(3):
                    part = into[:, b0:b0 + n, j * e:j * e + e]
                    ins = V.tensor_copy(part, p)
                    if j < 2:
                        link(ins)
                        link(V.tensor_tensor(p, p, part, ALU.subtract))
                return ins

            V.memset(ones[:, :], 1.0).then_inc(c_ones, 1)
            dve.wait_ge(ld_x[0], 16)
            stats(0, 0, HALF)
            dve.wait_ge(c_pool, 2)
            V.tensor_copy(order[:, :], orderi[:, :])
            normalise(xna, 0, 0, HALF, 1, xn1_ready)
            dve.wait_ge(ld_x[1], 16)
            stats(0, HALF, NB)
            dve.wait_ge(ld_vec, 16 * 6)
            dve.wait_ge(c_ones, 1)
            V.tensor_scalar(wp2[:, :], cols[:, WP:WP + 1], 2.0, None, ALU.mult)
            V.tensor_scalar(rows[:, R_BQ, :], rows[:, R_BQ, :], S1_SCALE, None, ALU.mult)
            V.tensor_scalar(kb[:, 0, :], kv[:, 1, :], float(T), None, ALU.mult)
            V.tensor_scalar(kb[:, 1, :], kv[:, 3, :], float(T), None, ALU.mult)
            V.tensor_tensor(sim2[:, :], sim, sim, ALU.mult).then_inc(sim2_ready, 1)

            def key_terms(hf):
                dve.wait_ge(k1_ready, hf + 1)
                for v in range(2):
                    ins = V.tensor_tensor(kw[:, hf, v, :, :], PB[1 + 2 * hf][:, 0:HALF * D0].rearrange("p (b e) -> p b e", e=D0),
                                          bc(kv[:, 2 * v, :], 1, HALF), ALU.mult)
                ins.then_inc(k1_used, 1)
                dve.wait_ge(k1_used, hf + 1)
                for v in range(2):
                    ins = V.tensor_tensor(kw[:, hf, v, :, :], kw[:, hf, v, :, :], bc(kb[:, v, :], 1, HALF), ALU.add)
                link(ins)
                for v, q in enumerate((BQG, BQL)):
                    V.tensor_scalar(kw[:, hf, v, :, :], kw[:, hf, v, :, :], cols[:, q:q + 1], None, ALU.mult)

            def channel_scores(hf):
                dve.wait_ge(s_ready, hf + 1)
                bank = PB[2 * hf]
                qk_sum = bank[:, 0:HALF * D0].rearrange("p (b e) -> p b e", e=D0)
                q_sum = bank[:, HALF * D0:HALF * D0 + HALF]
                for v in range(2):
                    V.tensor_tensor(sc[:, hf, v, :, :], qk_sum, bc(kv[:, 2 * v, :], 1, HALF), ALU.mult)
                for v in range(2):
                    ins = V.tensor_tensor(sc2[:, hf, v, :, :], bc(q_sum, 2, D0), bc(kv[:, 2 * v + 1, :], 1, HALF), ALU.mult)
                ins.then_inc(s_used, 1)
                dve.wait_ge(s_used, hf + 1)
                link(V.tensor_tensor(sc[:, hf, :, :, :], sc[:, hf, :, :, :], sc2[:, hf, :, :, :], ALU.add))
                for v, q in enumerate((WQG, WQL)):
                    ins = V.scalar_tensor_tensor(out=sc[:, hf, v, :, :], in0=sc[:, hf, v, :, :], scalar=cols[:, q:q + 1],
                                                 in1=kw[:, hf, v, :, :], op0=ALU.mult, op1=ALU.add)
                link(ins)
                w = sc[:, hf, :, :, :].rearrange("p v i e -> p (v i) e")
                link(V.tensor_reduce(cm[:, hf, :], w, AX.X, ALU.max))
                V.tensor_tensor(w, w, bc(cm[:, hf, :], 2, D0), ALU.subtract).then_inc(sc_ready, 1)

            def key_bias(hf):
                dve.wait_ge(kp_ready, hf + 1)
                V.tensor_tensor(kf[:, hf, :].rearrange("p (b c) -> p b c", c=C), PB[key_bank(hf)][:, :].rearrange("p (b c) -> p b c", c=C),
                                        bc(rows[:, R_BK, :], 1, HALF), ALU.add).then_inc(kf_ready, 1)

            def channel_softmax(hf):
                w = sc[:, hf, :, :, :].rearrange("p v i e -> p (v i) e")
                e = sc2[:, hf, :, :, :].rearrange("p v i e -> p (v i) e")
                dve.wait_ge(zeroed, 1)
                dve.wait_ge(sce_ready, hf + 1)
                link(V.tensor_reduce(cs[:, hf, :], e, AX.X, ALU.add))
                link(V.reciprocal(cs[:, hf, :], cs[:, hf, :]))
                link(V.scalar_tensor_tensor(out=w, in0=e, scalar=wp2[:, 0:1], in1=bc(cs[:, hf, :], 2, D0), op0=ALU.mult, op1=ALU.mult))

            def turn_heads(hf):
                w = sc[:, hf, :, :, :].rearrange("p v i e -> p (v i) e")
                for h in range(H0):
                    r = head_rows(h)
                    ins = V.transpose(bd[r, hf, :, :, r].rearrange("p v i e -> p (v i) e"), w[r, :, :])
                ins.then_inc(bd_ready, 1)

            def after_channels(hf):
                dve.wait_ge(att_ready, hf + 1)
                dve.wait_ge(xbp_ready, hf + 1)
                x = xr[:, bs(hf), :].rearrange("p b c -> p (b c)")
                V.tensor_tensor(x, x, PB[4 + hf][:, :], ALU.add).then_inc(x1_ready, 1)
                dve.wait_ge(x1_ready, hf + 1)
                stats(1, HALF * hf, HALF * hf + HALF)

            def norms(hf):
                n = hn[:, bs(hf)]
                link(V.tensor_tensor(n, rstd[:, 1, bs(hf)], rstd[:, 1, bs(hf)], ALU.mult))
                link(V.scalar_tensor_tensor(out=n, in0=n, scalar=float(C), in1=mv[:, 1, bs(hf), 1], op0=ALU.mult, op1=ALU.mult))
                V.tensor_scalar(n, n, 1e-24, None, ALU.max).then_inc(hn_ready, 1)

            def gate(hf, step):
                l, g0, mark = lg[:, 0:HALF, :], gv[:, 0, 0:HALF], f1[:, 0:HALF, :]
                if step == 0:
                    dve.wait_ge(lg_ps, hf + 1)
                    dve.wait_ge(rhn_ready, hf + 1)
                    V.tensor_tensor(l, PB[5 if hf else 1][:, 0:HALF * E0].rearrange("p (b e) -> p b e", e=E0),
                                    bc(rhn[:, bs(hf)], 2, E0), ALU.mult).then_inc(lg_used, 1)
                    dve.wait_ge(lg_used, hf + 1)
                    link(V.tensor_tensor(l, l, bc(sgate[:, :], 1, HALF), ALU.subtract))
                two_best(E0, HALF, step)
                if step == 4:
                    link(V.tensor_scalar(gv[:, 1, 0:HALF], g0, 0.0, None, ALU.is_le))
                    link(V.tensor_tensor(mark, mark, bc(gv[:, 1, 0:HALF], 2, E0), ALU.mult))
                    link(V.scalar_tensor_tensor(out=f2[:, 0:HALF, :], in0=l, scalar=0.0, in1=mark, op0=ALU.is_gt, op1=ALU.max))
                    link(V.tensor_scalar(g0, g0, 0.0, None, ALU.max))
                    V.scalar_tensor_tensor(out=gin[:, 0:HALF, :], in0=l, scalar=0.0, in1=bc(g0, 2, E0),
                                           op0=ALU.max, op1=ALU.subtract).then_inc(gin_ready, 1)
                if step == 5:
                    dve.wait_ge(gex_ready, hf + 1)
                    weigh(E0, HALF, f2[:, 0:HALF, :])
                if step == 6:
                    dve.wait_ge(zeroed, 2)
                    three_parts(E0, HALF, parts, HALF * hf).then_inc(parts_ready, 1)

            dve.wait_ge(sim2_ready, 1)
            key_terms(0)
            dve.wait_ge(c_id, 1)
            V.tensor_reduce(part16[:, :], ident[:, 0:3 * E0].rearrange("p (m e) -> p e m", m=3), AX.X, ALU.add)
            V.tensor_reduce(part8[:, :], ident[:, 0:3 * E1].rearrange("p (m e) -> p e m", m=3), AX.X, ALU.add)
            V.tensor_reduce(hmask[:, :], ident[:, :].rearrange("p (g j i) -> p j g i", g=4, j=4), AX.XY, ALU.add).then_inc(c_part, 1)
            channel_scores(0)
            normalise(xna, 0, HALF, NB, 2, xn1_ready)
            channel_softmax(0)
            turn_heads(0)
            key_bias(0)
            dve.wait_ge(simsum_ready, 1)
            V.tensor_scalar(sim2[:, :], PB[7][:, 0:E0], 1e-24, None, ALU.max).then_inc(ssq_ready, 1)
            key_terms(1)
            channel_scores(1)
            dve.wait_ge(egate_ready, 1)
            link(V.tensor_scalar(sgate[:, :], sgate[:, :], 1.0, None, ALU.add))
            V.reciprocal(sgate[:, :], sgate[:, :])
            after_channels(0)
            channel_softmax(1)
            normalise(xnb, 1, 0, HALF, 3, xn2_ready)
            norms(0)
            dve.wait_ge(simr_ready, 1)
            V.tensor_tensor(simn[:, :], sim, sim2[:, :], ALU.mult).then_inc(simn_ready, 1)
            turn_heads(1)
            key_bias(1)
            for step in range(7):
                gate(0, step)

            def scale_hidden(i):
                b, q = i // 4, i % 4
                dve.wait_ge(rb_ready, i + 1)
                if i >= 8:
                    dve.wait_ge(qkv_done, i - 7)
                V.tensor_tensor(hm[:, b % 2, 4 * q:4 * q + 4, :], bc(xn2T[:, b, :], 1, 4),
                                PB[4 if i % 2 == 0 else 6][:, :].rearrange("p (e t) -> p e t", e=4), ALU.mult).then_inc(hm_ready, 1)

            def split(src, dst, hi, lo):
                s4 = bc(src[:, :].rearrange("p (g c) -> p g c", g=4), 2, 2)
                link(V.tensor_copy(dst[:, :, hi, :].bitcast(F32R), s4))
                return V.tensor_tensor(dst[:, :, lo, :], s4, dst[:, :, hi, :], ALU.subtract)

            def split_q(b):
                dve.wait_ge(qp_ready, b + 1)
                if b >= 1:
                    dve.wait_ge(qsT_ps, b)
                link(V.scalar_tensor_tensor(out=qf[:, :], in0=PB[query_bank(b)][:, 0:C], scalar=S1_SCALE, in1=rows[:, R_BQ, :],
                                            op0=ALU.mult, op1=ALU.add))
                split(qf, qsp, slice(0, 2), slice(2, 4)).then_inc(qsp_ready, 1)

            def softmax2_max(b):
                dve.wait_ge(s2_ps, b + 1)
                V.tensor_tensor_reduce(s2[:, b % 2, :], PB[1][:, 0:T], causal[:, :], 1.0, NEG, ALU.add, ALU.max,
                                       mx2[:, b:b + 1]).then_inc(s2_ready, 1)
                dve.wait_ge(s2_ready, b + 1)
                V.tensor_scalar(nmx2[:, b:b + 1], mx2[:, b:b + 1], -A_SCALE, None, ALU.mult).then_inc(nmx_ready, 1)

            def softmax2_norm(b):
                dve.wait_ge(p2_ready, b + 1)
                link(V.reciprocal(rden2[:, b:b + 1], den2[:, b:b + 1]))
                V.tensor_scalar(pn[:, b % 2, :], pn[:, b % 2, :], rden2[:, b:b + 1], None, ALU.mult).then_inc(pn_ready, 1)

            def mix(b, i):
                dve.wait_ge(mixw_ready, 2 * b + i + 1)
                dve.wait_ge(aT_ready, b + 1)
                if b >= 1:
                    dve.wait_ge(o_ready, b)
                V.tensor_tensor(mixT[:, 4 * i:4 * i + 4, :], bc(aT[:, b % 2, :], 1, 4),
                                PB[5][:, :].rearrange("p (r t) -> p r t", r=4), ALU.mult).then_inc(mix_ready, 1)

            def after_mixture(b):
                dve.wait_ge(o_ready, b + 1)
                V.tensor_tensor(xr[:, b, :], xr[:, b, :], PB[5][:, 0:C], ALU.add).then_inc(x2_ready, 1)
                dve.wait_ge(x2_ready, b + 1)
                stats(2, b, b + 1)

            def softmax3(u):
                b, g = u // 4, u % 4
                bank = PB[score_bank(u)][:, :].rearrange("p (j k) -> p j k", j=4)
                dve.wait_ge(s3_ready, u + 1)
                V.tensor_reduce(mx3[:, u % 8, :], bank, AX.X, ALU.max, negate=True).then_inc(mx3_ready, 1)

            def divide(b):
                dve.wait_ge(pv_done, 4 * b + 4)
                bank = PB[pv_bank(b)][:, 0:2 * T]
                link(V.reciprocal(ry[:, :, :].rearrange("p g t -> p (g t)"), bank[64:128, :]))
                if b >= 2:
                    dve.wait_ge(c_ready, b - 1)
                for g in range(2):
                    ins = V.tensor_tensor(yT[64 * g:64 * g + 64, b % 2, :], ry[:, g, :], bank[0:64, T * g:T * g + T], ALU.mult)
                ins.then_inc(yT_ready, 1)

            def after_attention(b):
                dve.wait_ge(c_ready, b + 1)
                dve.wait_ge(xbc_ready, b + 1)
                V.tensor_tensor(xr[:, b, :], xr[:, b, :], PB[pv_bank(b)][:, 0:C], ALU.add).then_inc(x3_ready, 1)
                dve.wait_ge(x3_ready, b + 1)
                stats(3, b, b + 1)

            def route(hf, step):
                if step == 0:
                    dve.wait_ge(rt_ps, hf + 1)
                    V.tensor_copy(lg[:, 0:HALF, 0:E1], PB[router_bank(hf)][:, 0:HALF * E1].rearrange("p (b e) -> p b e", e=E1)).then_inc(rt_used, 1)
                    dve.wait_ge(rt_used, hf + 1)
                two_best(E1, HALF, step)
                if step == 3:
                    V.tensor_tensor(gin[:, 0:HALF, 0:E1], lg[:, 0:HALF, 0:E1], bc(gv[:, 0, 0:HALF], 2, E1), ALU.subtract).then_inc(rin_ready, 1)

            def route_weights(hf, step):
                if step == 0:
                    dve.wait_ge(rex_ready, hf + 1)
                    weigh(E1, HALF, f1[:, 0:HALF, 0:E1])
                if step == 1:
                    dve.wait_ge(zeroed, 3)
                    three_parts(E1, HALF, wparts, HALF * hf).then_inc(wparts_ready, 1)

            def hidden(k):
                ch = k % NCH
                n = chunk_rows(ch)
                bank = PB[7 if k % 2 == 0 else 1][0:n, :]
                dve.wait_ge(gated_ready, k + 1)
                if k >= 2:
                    dve.wait_ge(hlo_ready, k - 1)
                if not is_routed(k):
                    V.tensor_tensor(hid[0:n, k % 2, :], gated[0:n, k % 2, :], bank, ALU.mult).then_inc(hid_ready, 1)
                    return
                V.tensor_tensor(hid[:, k % 2, :], gated[:, k % 2, :], bank, ALU.mult).then_inc(prod_ready, 1)
                dve.wait_ge(prod_ready, n_routed(k))
                V.tensor_tensor(hid[:, k % 2, :], hid[:, k % 2, :], PB[3 if n_routed(k) % 2 == 1 else 4][:, :], ALU.mult).then_inc(hid_ready, 1)

            def low_down(ch):
                n = chunk_rows(ch)
                dve.wait_ge(whi_ready, ch + 1)
                V.tensor_tensor(wdlo[0:n, ch, :], wdn[0:n, ch, :], wdhi[0:n, ch, :].bitcast(F32), ALU.subtract).then_inc(wdlo_ready, 1)

            def low_hidden(k):
                n = chunk_rows(k % NCH)
                dve.wait_ge(hhi_ready, k + 1)
                dve.wait_ge(down_done, k - 2)
                dve.wait_ge(hlo_ready, k)
                V.tensor_tensor(hlo[0:n, k % 3, :], hid[0:n, k % 2, :], hhi[0:n, k % 3, :].bitcast(F32), ALU.subtract).then_inc(hlo_ready, 1)

            scale_hidden(0)
            scale_hidden(1)
            dve.wait_ge(c_pool, 3)
            for s in range(LAST):
                for b in reversed(range(NB)):
                    if s == 4 * b + 7:
                        softmax2_max(b)
                    if s == 4 * b + 8:
                        softmax2_norm(b)
                    if s == 4 * b + 11:
                        mix(b, 0)
                    if s == 4 * b + 12:
                        mix(b, 1)
                    if s == 4 * b + 14:
                        after_mixture(b)
                    if s == 4 * b + 15:
                        normalise(xna, 2, b, b + 1, 5 + b, xn3_ready)
                    if s == 4 * b + 18:
                        split_q(b)
                if s == 0:
                    after_channels(1)
                if s == 1:
                    normalise(xnb, 1, HALF, NB, 4, xn2_ready)
                    norms(1)
                if 4 <= s < 9:
                    gate(1, s - 4)
                if 9 <= s < 11:
                    gate(1, s - 4)
                if s + 2 < 4 * NB:
                    scale_hidden(s + 2)
                if 0 <= s - Q3 < 4 * NB:
                    softmax3(s - Q3)
                for b in range(NB):
                    if s == Q3 + 4 * b + 8:
                        divide(b)
                    if s == Q3 + 4 * b + 11:
                        after_attention(b)
                    if s == Q3 + 4 * b + 13:
                        normalise(xnb, 3, b, b + 1, 5 + NB + b, xn4_ready)
                for hf in range(2):
                    if 0 <= s - tail(hf) - 1 < 4:
                        route(hf, s - tail(hf) - 1)
                    if 0 <= s - tail(hf) - 6 < 2:
                        route_weights(hf, s - tail(hf) - 6)
                if 0 <= s - F4 < 2 * NCH:
                    hidden(s - F4)
                if 0 <= s - F4 + 2 < NCH:
                    low_down(s - F4 + 2)
                if ON_POOL <= s - F4 - 1 < 2 * NCH:
                    low_hidden(s - F4 - 1)

        @block.tensor
        def _(pe):
            mm = nc.tensor.matmul
            tr = nc.tensor.transpose
            pe.wait_ge(c_ones, 1)

            def sum_keys(hf):
                pe.wait_ge(ld_ctx[hf], 16)
                for i in range(HALF):
                    b = HALF * hf + i
                    for h in range(H0):
                        r = head_rows(h)
                        last = mm(PB[1 + 2 * hf][r, D0 * i:D0 * i + D0], ones[:, 0:D0], cx[:, b, r], start=True, stop=True)
                last.then_inc(k1_ready, 1)

            def sum_queries(hf):
                pe.wait_ge(xn1_ready, hf + 1)
                for i in range(HALF):
                    b = HALF * hf + i
                    for h in range(H0):
                        r = head_rows(h)
                        mm(PB[2 * hf][r, D0 * i:D0 * i + D0], xna[:, b, r], cx[:, b, r], start=True, stop=True)
                        last = mm(PB[2 * hf][r, HALF * D0 + i:HALF * D0 + i + 1], xna[:, b, r], ones[:, 0:1], start=True, stop=True)
                last.then_inc(s_ready, 1)

            sum_keys(0)
            sum_queries(0)
            sum_keys(1)
            pe.wait_ge(sim2_ready, 1)
            mm(PB[7][:, 0:E0], ones[:, :], sim2[:, :], start=True, stop=True).then_inc(simsum_ready, 1)

            def project_keys(hf):
                if hf == 0:
                    pe.wait_ge(ld_attn, 16)
                    pe.wait_ge(ld_ctxT, 16)
                else:
                    pe.wait_ge(s_used, 1)
                for i in range(HALF):
                    b = HALF * hf + i
                    last = mm(PB[key_bank(hf)][:, C * i:C * i + C], cxT[:, T * b:T * b + T], wattn[:, 0, :], start=True, stop=True)
                last.then_inc(kp_ready, 1)

            def turn_keys(b):
                if b == 1:
                    pe.wait_ge(ssq_ready, 1)
                if b in (2, 6):
                    pe.wait_ge(kf_ready, 1 if b == 2 else 2)
                if b == 3:
                    pe.wait_ge(s_used, 2)
                if b == 4:
                    pe.wait_ge(k1_used, 2)
                if b in (5, 7):
                    pe.wait_ge(ks_ready, 4 if b == 5 else 2)
                pe.wait_ge(ksp_ready, b // HALF + 1)
                for g in range(4):
                    last = tr(PB[turned_key_bank(b)][:, T * g:T * g + T],
                              ksp[:, 4 * (b % HALF) + g, :, :].rearrange("p a c -> p (a c)"), ident[:, :])
                last.then_inc(ksT_ps, 1)

            project_keys(0)
            sum_queries(1)

            def attend_channels(hf):
                pe.wait_ge(bd_ready, hf + 1)
                if hf == 1:
                    pe.wait_ge(ks_ready, 3)
                for i in range(HALF):
                    b = HALF * hf + i
                    for v in range(2):
                        last = mm(PB[4 + hf][:, C * i:C * i + C], vT[:, v, T * b:T * b + T], bd[:, hf, v, i, :],
                                  start=(v == 0), stop=(v == 1))
                last.then_inc(att_ready, 1)

            def turn_x2(hf):
                pe.wait_ge(ks_ready, NB if hf else 1)
                pe.wait_ge(xn2_ready, hf + 1)
                for i in range(HALF):
                    last = tr(PB[6 + hf][:, T * i:T * i + T], xnb[:, HALF * hf + i, :], ident[:, :])
                last.then_inc(xn2T_ps, 1)

            def gate_logits(hf):
                if hf:
                    pe.wait_ge(x1_ready, 2)
                else:
                    pe.wait_ge(k1_used, 1)
                pe.wait_ge(xn2T_ready, hf + 1)
                for i in range(HALF):
                    last = mm(PB[5 if hf else 1][:, E0 * i:E0 * i + E0], xn2T[:, HALF * hf + i, :], simn[:, :], start=True, stop=True)
                last.then_inc(lg_ps, 1)

            def turn_rw(hf):
                if hf:
                    pe.wait_ge(xn2T_ready, 2)
                else:
                    pe.wait_ge(ks_ready, 5)
                pe.wait_ge(parts_ready, hf + 1)
                for i in range(HALF):
                    last = tr(PB[7 if hf else 3][:, 0:256].bitcast(BF16)[:, T * i:T * i + T], parts[:, HALF * hf + i, :], identb[:, :])
                last.then_inc(rwT_ps, 1)

            pe.wait_ge(vT_ready, 2)
            attend_channels(0)
            for b in range(HALF):
                turn_keys(b)
            project_keys(1)
            turn_x2(0)
            pe.wait_ge(simn_ready, 1)
            gate_logits(0)
            attend_channels(1)
            for b in range(HALF, NB):
                turn_keys(b)
            pe.wait_ge(c_sel, 1)
            turn_rw(0)

            def spread(i):
                b, q = i // 4, i % 4
                pe.wait_ge(rwT_ready, b // HALF + 1)
                if i == 0:
                    pe.wait_ge(x1_ready, 1)
                if i == 1:
                    pe.wait_ge(xn2T_ready, 1)
                if i >= 2:
                    pe.wait_ge(hm_ready, i - 1)
                for e in range(4):
                    last = mm(PB[4 if i % 2 == 0 else 6][:, T * e:T * e + T], sel[:, 4 * q + e, :], rwT[:, b, :],
                              start=True, stop=True)
                last.then_inc(rb_ready, 1)

            def project(i):
                b, q = i // 4, i % 4
                bank = PB[0 if b % 2 == 0 else 2]
                pe.wait_ge(hm_ready, i + 1)
                if i == 0:
                    pe.wait_ge(ld_qkv, 16)
                    pe.wait_ge(ks_ready, 7)
                if i == 4:
                    pe.wait_ge(ks_ready, 6)
                if q == 0 and b >= 2:
                    pe.wait_ge(qk_ready, b - 1)
                for e in range(4 * q, 4 * q + 4):
                    last = mm(bank[:, 0:3 * HD], hm[:, b % 2, e, :], wqkv[:, e, :], start=(e == 0), stop=(e == E0 - 1))
                last.then_inc(qkv_done, 1)

            def turn_qk(b):
                if b >= 1:
                    pe.wait_ge(s2_ready, b)
                else:
                    pe.wait_ge(lg_used, 1)
                pe.wait_ge(qk_ready, b + 1)
                tr(PB[1][0:HD, 0:T], qk[:, b % 2, 0:HD], ident[:, :])
                tr(PB[1][0:HD, T:2 * T], qk[:, b % 2, HD:2 * HD], ident[:, :]).then_inc(qkT_ps, 1)

            def scores2(b):
                pe.wait_ge(qkT_ready, b + 1)
                mm(PB[1][:, 0:T], qkT[:, b % 2, 0, :], qkT[:, b % 2, 1, :], start=True, stop=True).then_inc(s2_ps, 1)

            def turn_p(b):
                if b >= 1:
                    pe.wait_ge(aT_ready, b)
                else:
                    pe.wait_ge(rwT_ready, 1)
                pe.wait_ge(pn_ready, b + 1)
                tr(PB[3][:, 0:T], pn[:, b % 2, :], ident[:, :]).then_inc(pT2_ps, 1)

            def attend2(b):
                pe.wait_ge(pT2_ready, b + 1)
                mm(PB[3][:, 0:T], v2[:, b % 2, :, :].rearrange("p j d -> p (j d)"), pT2[:, b % 2, :], start=True, stop=True).then_inc(aT_ps, 1)

            def spread_pairs(b, i):
                if i == 0:
                    pe.wait_ge(c_sel, 2)
                    if b >= 1:
                        pe.wait_ge(x2_ready, b)
                    else:
                        pe.wait_ge(lg_used, 2)
                if i == 1:
                    pe.wait_ge(mix_ready, 2 * b + 1)
                for r in range(4):
                    last = mm(PB[5][:, T * r:T * r + T], sel2[:, 4 * i + r, :, :].rearrange("p j d -> p (j d)"), rwT[:, b, :],
                              start=True, stop=True)
                last.then_inc(mixw_ready, 1)

            def project_o(b):
                if b == 0:
                    pe.wait_ge(ld_o, 16)
                pe.wait_ge(mix_ready, 2 * b + 2)
                for r in range(E0 // 2):
                    last = mm(PB[5][:, 0:C], mixT[:, r, :], wo[:, r, :], start=(r == 0), stop=(r == E0 // 2 - 1))
                last.then_inc(o_ready, 1)

            def turn_x3(b):
                if b == 0:
                    pe.wait_ge(rwT_ready, 2)
                elif b == HALF:
                    pe.wait_ge(hm_ready, 4 * NB)
                else:
                    pe.wait_ge(qs_ready, b)
                pe.wait_ge(xn3_ready, b + 1)
                tr(PB[query_bank(b)][:, 0:T], xna[:, b, :], ident[:, :]).then_inc(xn3T_ps, 1)

            def project_q(b):
                pe.wait_ge(xn3T_ready, b + 1)
                mm(PB[query_bank(b)][:, 0:C], xn3T[:, :], wattn[:, 1, :], start=True, stop=True).then_inc(qp_ready, 1)

            def turn_q(b):
                pe.wait_ge(qsp_ready, b + 1)
                for g in range(4):
                    last = tr(PB[query_bank(b)][:, T * g:T * g + T], qsp[:, g, :, :].rearrange("p a c -> p (a c)"), ident[:, :])
                last.then_inc(qsT_ps, 1)

            def scores3(u):
                b, g = u // 4, u % 4
                bank = score_bank(u)
                if u >= 3:
                    pe.wait_ge(ex_ready, u - 2)
                elif bank == 7:
                    pe.wait_ge(qs_ready, HALF)
                else:
                    pe.wait_ge(qk_ready, NB - 1 + u)
                pe.wait_ge(km_ready, b + 1)
                pe.wait_ge(qs_ready, b + 1)
                mm(PB[bank][:, :], qs[:, b, g, :], km[:, b % 2, g, :, :].rearrange("p j k -> p (j k)"),
                   start=True, stop=True).then_inc(s3_ready, 1)

            def turn_ex(v):
                if v == 0:
                    pe.wait_ge(s2_ready, NB)
                elif v == 1:
                    pe.wait_ge(aT_ready, NB)
                else:
                    pe.wait_ge(exT_ready, v - 1)
                pe.wait_ge(ex_ready, v + 1)
                for j in range(4):
                    last = tr(PB[1 if v % 2 == 0 else 3][:, T * j:T * j + T], ex[:, v % 4, T * j:T * j + T], ident[:, :])
                last.then_inc(exT_ps, 1)

            def attend3(w):
                b, g = w // 4, w % 4
                pe.wait_ge(exT_ready, w + 1)
                if g == 0:
                    pe.wait_ge(vm_ready, b + 1)
                    if b == 0:
                        pe.wait_ge(hm_ready, 4 * NB)
                    elif b == 1:
                        pe.wait_ge(x2_ready, NB)
                    else:
                        pe.wait_ge(x3_ready, b - 1)
                for j in range(4):
                    h = 4 * g + j
                    last = mm(PB[pv_bank(b)][:, T * (g // 2):T * (g // 2) + T], vm[:, b % 2, h, :], exT[:, w % 4, T * j:T * j + T],
                              start=(h % 8 == 0), stop=(h % 8 == 7))
                last.then_inc(pv_done, 1)

            def project_c(b):
                pe.wait_ge(yT_ready, b + 1)
                mm(PB[pv_bank(b)][:, 0:C], yT[:, b % 2, :], wattn[:, 2, :], start=True, stop=True).then_inc(c_ready, 1)

            def turn_x4(hf):
                if hf:
                    pe.wait_ge(x3_ready, NB)
                else:
                    pe.wait_ge(qs_ready, NB)
                pe.wait_ge(xn4_ready, HALF * hf + HALF)
                for i in range(HALF):
                    last = tr(PB[router_bank(hf)][:, T * i:T * i + T], xnb[:, HALF * hf + i, :], ident[:, :])
                last.then_inc(xn4T_ps, 1)

            def router(hf):
                pe.wait_ge(xn4T_ready, hf + 1)
                if hf == 0:
                    pe.wait_ge(ld_up, 48)
                for i in range(HALF):
                    b = HALF * hf + i
                    last = mm(PB[router_bank(hf)][:, E1 * i:E1 * i + E1], xn4T[:, T * b:T * b + T], wg[:, :], start=True, stop=True)
                last.then_inc(rt_ps, 1)

            def turn_w(hf):
                pe.wait_ge(rt_used, hf + 1)
                pe.wait_ge(wparts_ready, hf + 1)
                for i in range(HALF):
                    last = tr(PB[router_bank(hf)][:, 0:256].bitcast(BF16)[:, T * i:T * i + T], wparts[:, HALF * hf + i, :], identb[:, :])
                last.then_inc(wT_ps, 1)

            def up(k):
                hf, ch = k // NCH, k % NCH
                n = chunk_rows(ch)
                c0 = 128 * ch
                cols4 = slice(512 * hf, 512 * hf + 512)

                def three(bank, hi, lo):
                    for j, (w, x) in enumerate(((hi, x4hi), (hi, x4lo), (lo, x4hi))):
                        last = mm(bank[0:n, :], w[:, c0:c0 + n], x[:, cols4], start=(j == 0), stop=(j == 2))
                    return last

                if k < 2:
                    pe.wait_ge(ex_ready, 4 * NB)
                    if k == 1:
                        pe.wait_ge(exT_ready, 4 * NB)
                else:
                    pe.wait_ge(gated_ready, k - 1)
                    b_read(pe, k - 2)
                pe.wait_ge(x4lo_ready, hf + 1)
                if hf == 0:
                    pe.wait_ge(wlo_ready, ch + 1)
                three(PB[0 if k % 2 == 0 else 2], wahi, walo)
                last = three(PB[7 if k % 2 == 0 else 1], wbhi, wblo)
                if is_routed(k):
                    r = n_routed(k)
                    if r == 2:
                        pe.wait_ge(x3_ready, NB - 1)
                    if r >= 3:
                        pe.wait_ge(hid_ready, routed_chunk(r - 2) + 1)
                    pe.wait_ge(wT_ready, hf + 1)
                    last = mm(PB[3 if r % 2 == 1 else 4][:, :], selw[:, :, :].rearrange("p e j -> p (e j)")[:, c0 - 128 * NSHARED:c0 - 128 * NSHARED + 128],
                              wT[:, 512 * hf:512 * hf + 512], start=True, stop=True)
                last.then_inc(up_ready, 1)

            def down(k):
                hf, ch = k // NCH, k % NCH
                n = chunk_rows(ch)
                bank = PB[5 if hf else 6]
                pe.wait_ge(hhi_ready, k + 1)
                if ch == 0:
                    pe.wait_ge(wT_ready, hf + 1)
                if hf == 0:
                    pe.wait_ge(wdlo_ready, ch + 1)
                for j, (w, h) in enumerate(((wdhi, hhi), (wdlo, hhi), (wdhi, hlo))):
                    if j == 2:
                        pe.wait_ge(hlo_ready, k + 1)
                    last = mm(bank[:, :], w[0:n, ch, :], h[0:n, k % 3, :], start=(ch == 0 and j == 0), stop=(ch == NCH - 1 and j == 2))
                last.then_inc(down_done, 1)
                if ch == 0:
                    pe.wait_ge(x3_ready, HALF * (hf + 1))
                    for i in range(HALF):
                        mm(bank[:, T * i:T * i + T], xr[:, HALF * hf + i, :], ident[:, :], start=False, stop=False)

            spread(0)
            spread(1)
            for s in range(LAST):
                if s == 2:
                    turn_x2(1)
                if s == 3:
                    gate_logits(1)
                if s == 12:
                    turn_rw(1)
                for b in reversed(range(NB)):
                    if s == 4 * b + 5:
                        turn_qk(b)
                    if s == 4 * b + 6:
                        scores2(b)
                    if s == 4 * b + 9:
                        turn_p(b)
                    if s == 4 * b + 10:
                        attend2(b)
                    if s == 4 * b + 11:
                        spread_pairs(b, 0)
                    if s == 4 * b + 12:
                        spread_pairs(b, 1)
                    if s == 4 * b + 13:
                        project_o(b)
                    if s == 4 * b + 16:
                        turn_x3(b)
                    if s == 4 * b + 17:
                        project_q(b)
                    if s == 4 * b + 19:
                        turn_q(b)
                if s + 2 < 4 * NB:
                    spread(s + 2)
                if s < 4 * NB:
                    project(s)
                if 0 <= s - Q3 + 1 < 4 * NB:
                    scores3(s - Q3 + 1)
                if 0 <= s - Q3 - 3 < 4 * NB:
                    turn_ex(s - Q3 - 3)
                if 0 <= s - Q3 - 4 < 4 * NB:
                    attend3(s - Q3 - 4)
                for b in range(NB):
                    if s == Q3 + 4 * b + 10:
                        project_c(b)
                for hf in range(2):
                    if s == tail(hf):
                        turn_x4(hf)
                    if s == tail(hf) + 1:
                        router(hf)
                    if s == weights_in(hf):
                        turn_w(hf)
                if 0 <= s - F4 < 2 * NCH:
                    up(s - F4)
                if 0 <= s - F4 - 3 < 2 * NCH:
                    down(s - F4 - 3)


def kernel(**inputs):
    import numpy as np
    import concourse.bacc as bacc
    from concourse.bass_utils import run_bass_kernel_spmd

    a = {k: np.asarray(v) for k, v in inputs.items()}
    xa, fa, xb, fb = "L0_xattn_", "L0_ffn_", "L1_xattn_", "L1_ffn_"
    ctx = a["ctx_1024"]
    kvecs = np.stack([a[xa + n] for n in ("wkg", "bkg", "wkl", "bkl")])
    first = 128 * NSHARED
    laid = {
        "x": a["x"].transpose(1, 0, 2),
        "ctx": ctx.transpose(1, 0, 2),
        "ctxT": ctx.reshape(NB * T, C).T,
        "cols": np.stack([a[xa + n] for n in ("wqg", "bqg", "wql", "bql", "wvg", "bvg", "wvl", "bvl", "wp")] + list(a[fa + "sim_matrix"].T), axis=1),
        "rows": np.concatenate([a[xa + "bp"], a[xb + "bc"], a[xb + "bk"], a[xb + "bq"], a[fa + "gates"]]),
        "kv": kvecs.reshape(4, H0, D0).transpose(1, 0, 2).reshape(H0, 4 * D0),
        "wattn": np.stack([a[xb + n].T for n in ("Wk", "Wq", "Wc")], axis=1),
        "wqkv": np.concatenate([a[fa + n] for n in ("q_proj", "k_proj", "v_proj")], axis=2).transpose(1, 0, 2),
        "wo": a[fa + "o_proj"].reshape(E0 // 2, 2 * HD, C).transpose(1, 0, 2),
        "wa": np.concatenate([a[fb + "Ws1"][:, :first], a[fb + "W1"].transpose(1, 0, 2).reshape(C, E1 * HID), a[fb + "Ws1"][:, first:]], axis=1),
        "wb": np.concatenate([a[fb + "Ws2"][:, :first], a[fb + "W2"].transpose(1, 0, 2).reshape(C, E1 * HID), a[fb + "Ws2"][:, first:]], axis=1),
        "wdn": np.concatenate([a[fb + "Ws3"][:first], a[fb + "W3"].reshape(E1 * HID, C), a[fb + "Ws3"][first:]], axis=0),
        "wg": a[fb + "Wg"],
    }
    nc = bacc.Bacc("TRN2", target_bir_lowering=False, num_devices=1)
    arrays, args = {}, []
    for name, v in laid.items():
        v = np.ascontiguousarray(v)
        arrays[f"{name}_dram"] = v
        args.append(nc.dram_tensor(f"{name}_dram", v.shape, mybir.dt.from_np(v.dtype), kind="ExternalInput").ap())
    out = nc.dram_tensor("out_dram", (C, NB * T), F32, kind="ExternalOutput").ap()
    build(nc, *args, out)
    r = run_bass_kernel_spmd(nc, [arrays], core_ids=[0])
    return np.ascontiguousarray(r.results[0]["out_dram"].reshape(C, NB, T).transpose(1, 2, 0))
```
